# Optimizing a Trainium2 kernel written in Bass

```python
import numpy as np
import jax
import jax.numpy as jnp

def _softmax(x, axis=-1):
    return jax.nn.softmax(x, axis=axis)

def _gelu(x):
    return jax.nn.gelu(x, approximate=True)

def _silu(x):
    return jax.nn.silu(x)

def _sigmoid(x):
    return jax.nn.sigmoid(x)

def _layernorm(x, axis=-1, eps=1e-05):
    m = jnp.mean(x, axis=axis, keepdims=True)
    v = jnp.var(x, axis=axis, keepdims=True)
    return (x - m) / jnp.sqrt(v + eps)

def _scatter_add(tgt, idx, src, axis=0):
    return tgt.at[idx].add(src)

def _segment_sum(src, seg, n):
    return jax.ops.segment_sum(src, seg, n)
kernel_name = 'mk_hybrid_d1_jaxref_r8_acf71f'

def setup_inputs(seed: int=0):
    np.random.seed(seed)
    _w = jnp.asarray

    def _L0_attn_a_setup():
        import jax, jax.numpy as jnp
        import numpy as np
        import math
        D_MODEL = 128
        NUM_HEADS = 16
        key = jax.random.key(seed)
        k1, k2, k3 = jax.random.split(key, 3)
        B, S = (2, 256)
        x = jax.random.normal(k1, (B, S, D_MODEL), dtype=jnp.float32)
        W_kqv = jax.random.normal(k2, (D_MODEL, 3 * D_MODEL), dtype=jnp.float32) * (1.0 / math.sqrt(D_MODEL))
        m = jax.random.normal(k3, (NUM_HEADS, 1, 1), dtype=jnp.float32)
        return {'x': x, 'W_kqv': W_kqv, 'm': m}
    _L0_attn_a_in = _L0_attn_a_setup()

    def _L0_attn_b_setup():
        import jax, jax.numpy as jnp
        import numpy as np
        B, S, D, K = (4, 512, 128, 64)
        key = jax.random.key(seed)
        kx, kq, kk, kv, ko = jax.random.split(key, 5)
        scale = 1.0 / np.sqrt(D)
        return {'x': jax.random.normal(kx, (B, S, D), dtype=jnp.float32), 'Wq': jax.random.uniform(kq, (K, D), dtype=jnp.float32, minval=-scale, maxval=scale), 'Wk': jax.random.uniform(kk, (K, D), dtype=jnp.float32, minval=-scale, maxval=scale), 'Wv': jax.random.uniform(kv, (K, D), dtype=jnp.float32, minval=-scale, maxval=scale), 'Wo': jax.random.uniform(ko, (D, K), dtype=jnp.float32, minval=-1.0 / np.sqrt(K), maxval=1.0 / np.sqrt(K))}
    _L0_attn_b_in = _L0_attn_b_setup()

    def _L0_ffn_setup():
        import jax, jax.numpy as jnp
        import numpy as np
        D_MODEL = 128
        HIDDEN = 512
        NUM_EXPERTS = 8
        TOP_K = 2
        DEPTH = 12
        DEPTH_SCALE = 1.0 / np.sqrt(DEPTH)
        key = jax.random.key(seed)
        k_x, k_r, k_g, k_u, k_d = jax.random.split(key, 5)
        s_in = 1.0 / np.sqrt(D_MODEL)
        s_hid = 1.0 / np.sqrt(HIDDEN)
        return {'x': jax.random.normal(k_x, (2, 256, D_MODEL), dtype=jnp.float32), 'Wr': jax.random.normal(k_r, (D_MODEL, NUM_EXPERTS), dtype=jnp.float32) * s_in, 'Wg': jax.random.normal(k_g, (NUM_EXPERTS, D_MODEL, HIDDEN), dtype=jnp.float32) * s_in, 'Wu': jax.random.normal(k_u, (NUM_EXPERTS, D_MODEL, HIDDEN), dtype=jnp.float32) * s_in, 'Wd': jax.random.normal(k_d, (NUM_EXPERTS, HIDDEN, D_MODEL), dtype=jnp.float32) * s_hid}
    _L0_ffn_in = _L0_ffn_setup()
    _d = {'L0_attn_a_x': _L0_attn_a_in['x'], 'L0_attn_a_W_kqv': _L0_attn_a_in['W_kqv'], 'L0_attn_a_m': _L0_attn_a_in['m'], 'L0_attn_b_Wq': _L0_attn_b_in['Wq'], 'L0_attn_b_Wk': _L0_attn_b_in['Wk'], 'L0_attn_b_Wv': _L0_attn_b_in['Wv'], 'L0_attn_b_Wo': _L0_attn_b_in['Wo'], 'L0_ffn_Wr': _L0_ffn_in['Wr'], 'L0_ffn_Wg': _L0_ffn_in['Wg'], 'L0_ffn_Wu': _L0_ffn_in['Wu'], 'L0_ffn_Wd': _L0_ffn_in['Wd']}
    _x0 = _d['L0_attn_a_x']
    _d['L0_attn_a_x'] = jax.random.normal(jax.random.fold_in(jax.random.key(seed), 1), (4, 512, 128), dtype=_x0.dtype)
    del _x0
    return _d

def reference(L0_attn_a_x, L0_attn_a_W_kqv, L0_attn_a_m, L0_attn_b_Wq, L0_attn_b_Wk, L0_attn_b_Wv, L0_attn_b_Wo, L0_ffn_Wr, L0_ffn_Wg, L0_ffn_Wu, L0_ffn_Wd):

    def _L0_attn_a_ref(x, W_kqv, m):
        import jax, jax.numpy as jnp
        import numpy as np
        import math
        D_MODEL = 128
        NUM_HEADS = 16
        B, S, D = x.shape
        H = NUM_HEADS
        hd = D // H
        scale = math.sqrt(D)
        kqv = x @ W_kqv
        k, q, v = jnp.split(kqv, 3, axis=-1)
        q = q.reshape(B, S, H, hd)
        k = k.reshape(B, S, H, hd)
        v = v.reshape(B, S, H, hd)
        rel = (jnp.arange(S)[None, :] - jnp.arange(S)[:, None]).astype(x.dtype)
        bias = m[None, :, :, :] * rel[None, None, :, :]
        score = jnp.einsum('bqhd,bkhd->bhqk', q, k) / scale + bias
        causal = jnp.tril(jnp.ones((S, S), dtype=bool))
        score = jnp.where(causal[None, None, :, :], score, -jnp.inf)
        attn = jax.nn.softmax(score, axis=-1)
        out = jnp.einsum('bhqk,bkhd->bqhd', attn, v).reshape(B, S, D)
        return out

    def _L0_attn_b_ref(x, Wq, Wk, Wv, Wo):
        import jax, jax.numpy as jnp
        import numpy as np
        B, S, D, K = (4, 512, 128, 64)
        Q = jax.nn.elu(x @ Wq.T) + 1.0
        Kf = jax.nn.elu(x @ Wk.T) + 1.0
        V = x @ Wv.T
        KV_sum = jnp.cumsum(Kf[..., :, None] * V[..., None, :], axis=1)
        K_sum = jnp.cumsum(Kf, axis=1)
        num = jnp.einsum('bsk,bskm->bsm', Q, KV_sum)
        den = jnp.einsum('bsk,bsk->bs', Q, K_sum)[..., None]
        out = num / (den + 1e-06)
        return out @ Wo.T

    def _L0_ffn_ref(x, Wr, Wg, Wu, Wd):
        import jax, jax.numpy as jnp
        import numpy as np
        D_MODEL = 128
        HIDDEN = 512
        NUM_EXPERTS = 8
        TOP_K = 2
        DEPTH = 12
        DEPTH_SCALE = 1.0 / np.sqrt(DEPTH)
        B, T, C = x.shape
        flat_x = x.reshape(-1, C)
        logits = flat_x @ Wr
        top_vals, top_idx = jax.lax.top_k(logits, TOP_K)
        rw = jax.nn.softmax(top_vals.astype(jnp.float32), axis=-1).astype(x.dtype)
        combine = jnp.sum(rw[..., None] * jax.nn.one_hot(top_idx, NUM_EXPERTS, dtype=x.dtype), axis=1)
        g = jnp.einsum('nc,ech->neh', flat_x, Wg)
        u = jnp.einsum('nc,ech->neh', flat_x, Wu)
        h = jax.nn.silu(g) * u
        eo = jnp.einsum('neh,ehc->nec', h, Wd) * DEPTH_SCALE
        out = jnp.einsum('ne,nec->nc', combine, eo)
        return out.reshape(B, T, C)
    x = L0_attn_a_x
    x = x + _L0_attn_a_ref(_layernorm(x, axis=-1), L0_attn_a_W_kqv, L0_attn_a_m)
    x = x + _L0_ffn_ref(_layernorm(x, axis=-1), L0_ffn_Wr, L0_ffn_Wg, L0_ffn_Wu, L0_ffn_Wd)
    x = x + _L0_attn_b_ref(_layernorm(x, axis=-1), L0_attn_b_Wq, L0_attn_b_Wk, L0_attn_b_Wv, L0_attn_b_Wo)
    x = x + _L0_ffn_ref(_layernorm(x, axis=-1), L0_ffn_Wr, L0_ffn_Wg, L0_ffn_Wu, L0_ffn_Wd)
    return x

_drawn_inputs = setup_inputs


def setup_inputs(seed=0):
    import zlib

    import numpy as np

    out = dict(_drawn_inputs(seed))
    spreads = {}
    factors = {}
    for name, (base, spread) in spreads.items():
        noise = np.random.default_rng([zlib.crc32(name.encode()), seed]).standard_normal(out[name].shape)
        drawn = base * np.exp(spread * noise) if base else spread * noise
        out[name] = jnp.asarray(drawn.astype(out[name].dtype))
    for name, factor in factors.items():
        out[name] = (out[name] * factor).astype(out[name].dtype)
    return out
```

```python
import concourse.bass as bass
from concourse import mybir
from contextlib import ExitStack

B, S, D = 4, 512, 128
P = 128
T = B * S // P
BT = S // P
H, HD = 16, 8
HG, GH = 4, 4
E, HID = 8, 512
NJ = HID // P
K2 = 64
N_SLOT_TILES = 40
ROW = D + E
NPART = 3
PROD0 = 12
ZERO0 = PROD0 + 72
KROWS = 96
MROWS = KROWS + NPART
UC = GH * S
NEG = -1.0e30
EPS = 1e-5
SEG = [0, S, S + 384, S + 384 + 256]
PCOLS = 1280

MBANKS = [(0, 4, 0), (0, 2, 1), (2, 2, 1)] + [(a, 1, 2) for a in range(4)] + [(a, 1, 3) for a in range(4)]
NM = len(MBANKS)
XGROUPS = [(0, 2, 1, 0), (2, 2, 1, 0), (0, 2, 1, 1), (2, 2, 1, 1), (0, 4, 2, 2), (0, 4, 4, 3)]
NX = len(XGROUPS)
GROUPS_OF_KB = [2, 4, 5, 6]


def build(nc, x, wqk, wv, slopes, wq2, wk2, wv2, wo2, wr, wg, wu, wd, consts, pos_in, out):
    f32, bf16, i32 = mybir.dt.float32, mybir.dt.bfloat16, mybir.dt.int32
    ALU, ACT, AX = mybir.AluOpType, mybir.ActivationFunctionType, mybir.AxisListType
    ds = bass.ds
    ctx = ExitStack()
    with ctx:
        def sb(name, shape, dt=f32):
            return ctx.enter_context(nc.sbuf_tensor(name, shape, dt))

        def sem(name):
            return ctx.enter_context(nc.semaphore(name))

        def dram(name, shape, dt=f32):
            return nc.dram_tensor(name, shape, dt, kind="Internal").ap()

        q_parts_dram = dram("q_parts_dram", (B, 5, P, S), bf16)
        k_parts_dram = dram("k_parts_dram", (B, 3, P, S), bf16)
        q_rows_dram = q_parts_dram.rearrange("b i (d h) t -> b (i d) (h t)", h=H)
        k_rows_dram = k_parts_dram.rearrange("b i (d h) t -> b (i d) (h t)", h=H)
        bias_dram = dram("bias_dram", (26, H, S), bf16)
        xn_dram = [dram(f"xn_dram{f}", (T * P, ROW)) for f in range(2)]
        y_dram = [[dram(f"y_dram{f}_{i}", ((T + 1) * P, D)) for i in range(2)] for f in range(2)]

        X = sb("X", [P, T, D])
        XW = sb("XW", [P, T, ROW])
        XNT = sb("XNT", [P, T * P])
        SQ = sb("SQ", [P, T, D])
        CON = sb("CON", [P, consts.shape[1]])
        ident = CON[:, 0:128]
        upper1 = CON[:, 128:256]
        causal1 = CON[:, 256:384]
        tile_starts = CON[:, 384:400]
        rev = CON[:, 400:408]
        eidx = CON[:, 408:416]
        iota40 = CON[:, 416:456]
        pcol = CON[:, 456:457]
        padrow = CON[:, 457:458]
        tcol = CON[:, 458:490]
        iota128 = CON[:, 490:618]
        ones = sb("ones", [P, P])
        stat = sb("stat", [P, 5, T])
        ident_b = sb("ident_b", [P, P], bf16)
        mask_kq = sb("mask_kq", [P, GH, P], bf16)
        mask_qk4 = sb("mask_qk4", [P, GH, P], bf16)
        WQK = sb("WQK", [P, 2 * D])
        WV = sb("WV", [P, D])
        WQ2 = sb("WQ2", [P, K2])
        WK2 = sb("WK2", [P, K2])
        WV2 = sb("WV2", [P, K2])
        WO2 = sb("WO2", [K2 + 1, D + 1])
        WR = sb("WR", [P, E])
        WE = sb("WE", [P, 3, E * HID])
        WG, WU, WD = WE[:, 0], WE[:, 1], WE[:, 2]
        V = sb("V", [P, T, D])
        SCR = sb("SCR", [P, 5 * 4096], bf16)
        QK = SCR[:, 0:2048].bitcast(f32).rearrange("p (a n) -> p a n", a=2)
        QKR = SCR[:, 2048:4096].bitcast(f32).rearrange("p (a n) -> p a n", a=2)
        QKP = [SCR[:, 4096 + 3072 * i:7168 + 3072 * i].rearrange("p (c a n) -> p c a n", c=3, a=2)
               for i in range(2)]
        BIAS = WE[0:H].rearrange("p k n -> p (k n)")[:, 0:5 * S].bitcast(bf16).rearrange("p (r t) -> p r t", r=10)
        POS = WE[0:H].rearrange("p k n -> p (k n)")[:, 12 * S:14 * S]
        slope = sb("slope", [H, 1])
        slope_r = sb("slope_r", [H, 2])
        slope_p = sb("slope_p", [H, 3])
        slope_pb = sb("slope_pb", [H, 3], bf16)
        QA = [sb(f"QA{i}", [MROWS, UC], bf16) for i in range(HG)]
        KA = [sb(f"KA{i}", [MROWS, UC], bf16) for i in range(HG)]
        PT = [SCR[:, 10240 * i:10240 * (i + 1)].bitcast(f32).rearrange("p (a n) -> p a n", a=GH)
              for i in range(2)]
        VU = [sb(f"VU{i}", [P, BT, GH, 32]) for i in range(2)]
        cmax = [sb(f"cmax{i}", [P, GH, BT]) for i in range(2)]
        negc = [sb(f"negc{i}", [GH * BT, P]) for i in range(2)]
        negr = sb("negr", [GH * BT, 1, P])
        zeros16 = sb("zeros16", [GH * BT, P])
        carrier = sb("carrier", [GH * BT, 1])
        cparts = [sb(f"cparts{i}", [GH * BT, NPART, P], bf16) for i in range(2)]
        OT = sb("OT", [P, S])
        rden = sb("rden", [P, BT, GH])
        NRM = [sb(f"NRM{i}", [P, BT, GH, HD]) for i in range(2)]

        PS = ctx.enter_context(nc.psum_tensor("PS", [P, 8, 512], f32))

        ld_x = [sem(f"ld_x{g}") for g in range(B)]
        ld_const, ld_wqkv, ld_small, ld_experts = sem("ld_const"), sem("ld_wqkv"), sem("ld_small"), sem("ld_experts")
        dve_chain, pool_chain, act_chain = sem("dve_chain"), sem("pool_chain"), sem("act_chain")
        ln_centred, ln_squared, ln_var, ln_std = sem("ln_centred"), sem("ln_squared"), sem("ln_var"), sem("ln_std")
        ln_done, ln_transposed, xnt_ready = sem("ln_done"), sem("ln_transposed"), sem("xnt_ready")
        consts_cast = sem("consts_cast")
        qk_proj, v_proj, qk_copied, v_copied = sem("qk_proj"), sem("v_proj"), sem("qk_copied"), sem("v_copied")
        part1, rest1, part2, part3 = sem("part1"), sem("rest1"), sem("part2"), sem("part3")
        parts_stored = [sem(f"parts_stored{i}") for i in range(2)]
        slopes_spread = sem("slopes_spread")
        bias_built, bias_stored, bias_loaded, slope_split = (
            sem("bias_built"), sem("bias_stored"), sem("bias_loaded"), sem("slope_split"))
        vu_cleared = sem("vu_cleared")
        qk_loaded = [sem(f"qk_loaded{i}") for i in range(HG)]
        max_ready, max_used, st_ready, exp_done = (
            sem("max_ready"), sem("max_used"), sem("st_ready"), sem("exp_done"))
        cmax_transposed, negc_ready, cparts_ready, crows_loaded = (
            sem("cmax_transposed"), sem("negc_ready"), sem("cparts_ready"), [sem("crows_loaded0"), sem("crows_loaded1")])
        vu_ready, pv_done, ot_ready, to_ready, normed, x_added = (
            sem("vu_ready"), sem("pv_done"), sem("ot_ready"), sem("to_ready"), sem("normed"), sem("x_added"))

        def ln_vector(dve, link, LN, x_ready):
            mean, var, std, rstd = (stat[:, i, :] for i in range(4))
            for g in range(B):
                gs = slice(BT * g, BT * g + BT)
                x_ready(dve, g)
                link(nc.vector.reduce_sum(mean[:, gs], X[:, gs, :], AX.X))
                link(nc.vector.tensor_scalar(mean[:, gs], mean[:, gs], 1.0 / D, None, ALU.mult))
                nc.vector.tensor_tensor(XW[:, gs, 0:D], X[:, gs, :],
                                        mean[:, gs].unsqueeze(2).to_broadcast([P, BT, D]),
                                        ALU.subtract).then_inc(ln_centred, 1)
            for g in range(B):
                gs = slice(BT * g, BT * g + BT)
                dve.wait_ge(ln_squared, 4 * LN + g + 1)
                link(nc.vector.reduce_sum(var[:, gs], SQ[:, gs, :], AX.X))
                nc.vector.tensor_scalar(var[:, gs], var[:, gs], 1.0 / D, EPS, ALU.mult, ALU.add).then_inc(ln_var, 1)
            for g in range(B):
                gs = slice(BT * g, BT * g + BT)
                dve.wait_ge(ln_std, 4 * LN + g + 1)
                link(nc.vector.reciprocal(rstd[:, gs], std[:, gs]))
                nc.vector.tensor_tensor(XW[:, gs, 0:D], XW[:, gs, 0:D],
                                        rstd[:, gs].unsqueeze(2).to_broadcast([P, BT, D]),
                                        ALU.mult).then_inc(ln_done, 1)

        def ln_scalar_stats(act, LN):
            var, std = stat[:, 1, :], stat[:, 2, :]
            for g in range(B):
                gs = slice(BT * g, BT * g + BT)
                act.wait_ge(ln_centred, 4 * LN + g + 1)
                nc.scalar.activation(SQ[:, gs, :], XW[:, gs, 0:D], ACT.Square).then_inc(ln_squared, 1)
            for g in range(B):
                gs = slice(BT * g, BT * g + BT)
                act.wait_ge(ln_var, 4 * LN + g + 1)
                nc.scalar.activation(std[:, gs], var[:, gs], ACT.Sqrt).then_inc(ln_std, 1)

        def ln_scalar_copy(act, LN, g):
            act.wait_ge(ln_transposed, 4 * LN + g + 1)
            nc.scalar.activation(XNT[:, S * g:S * g + S], PS[:, g % 2, :], ACT.Copy).then_inc(xnt_ready, 1)

        def ln_tensor(pe, LN, g):
            pe.wait_ge(ln_done, 4 * LN + g + 1)
            if g >= 2:
                pe.wait_ge(xnt_ready, 4 * LN + g - 1)
            for t in range(BT):
                last = nc.tensor.transpose(PS[:, g % 2, P * t:P * t + P], XW[:, BT * g + t, 0:D], ident)
            last.then_inc(ln_transposed, 1)

        lg = sb("lg", [P, 10, T, E])
        (LOG, OH1, OH2, OHS, T0, T1, T2, SLOT, CA, CB) = (lg[:, i] for i in range(10))
        rt = sb("rt", [P, 8, T])
        ex = sb("ex", [P, 6, E])
        slots_f = sb("slots_f", [P, 2, T])
        slots_i = sb("slots_i", [P, 3, 2 * T], i32)
        hi_lo = sb("hi_lo", [P, 2, 2 * T])
        OHLO = SCR[:, 0:4096].rearrange("p (c n) -> p c n", n=P)
        RHS = SCR[:, 4096:4096 + 3840].rearrange("p (c k n) -> p c k n", c=2 * T, k=3)
        tmap = sb("tmap", [P, N_SLOT_TILES, E])
        tsel = sb("tsel", [P, N_SLOT_TILES, E])
        te = sb("te", [P, N_SLOT_TILES])
        te_off = sb("te_off", [P, N_SLOT_TILES], i32)
        tok = sb("tok", [P, 3, N_SLOT_TILES])
        occ_tok = sb("occ_tok", [P, 3, N_SLOT_TILES])
        gidx = sb("gidx", [P, N_SLOT_TILES], i32)
        sidx = sb("sidx", [P, N_SLOT_TILES], i32)
        gcur = [sb(f"gcur{i}", [P, 1], i32) for i in range(2)]
        scur = [sb(f"scur{i}", [P, 1], i32) for i in range(2)]
        G = [sb(f"G{i}", [P, ROW]) for i in range(4)]
        xt = [sb(f"xt{i}", [P, P]) for i in range(2)]
        hs = [sb(f"hs{i}", [P, HID]) for i in range(2)]
        ht = [sb(f"ht{i}", [P, HID]) for i in range(2)]
        wsel = [sb(f"wsel{i}", [P, E]) for i in range(2)]
        wslot = [sb(f"wslot{i}", [P, 1]) for i in range(4)]
        ytile = [sb(f"ytile{i}", [P, D]) for i in range(2)]
        zrow = sb("zrow", [P, 1, D])
        Y0 = SCR[:, 0:4096].bitcast(f32).rearrange("p (t d) -> p t d", d=D)
        Y1 = SCR[:, 4096:8192].bitcast(f32).rearrange("p (t d) -> p t d", d=D)

        def ffn_sems(f):
            names = ("logits exp_arg exp_done comb ohs prefix onehots tokens idx toff xn_stored y_init gath0 gath1 "
                     "gath2 gath3 gcopied xT xt gate up silu h hT ht down wsel y scat0 scat1 scopied y_loaded out_sum")
            return {n: sem(f"f{f}_{n}") for n in names.split()}

        FS = [ffn_sems(0), ffn_sems(1)]
        DEPTH_SCALE = 12.0 ** -0.5
        NCH = 4

        def route_vector(dve, link, f):
            s = FS[f]
            m1, m2, k1, k2, dlt, w1, w2, ew = (rt[:, i, :] for i in range(8))

            def bt(a):
                return a.unsqueeze(2).to_broadcast([P, T, E])

            def be(a):
                return a.unsqueeze(1).to_broadcast([P, T, E])
            dve.wait_ge(s["logits"], 1)
            link(nc.vector.tensor_copy(LOG, PS[:, 2, 0:T * E].rearrange("p (t e) -> p t e", e=E)))
            link(nc.vector.reduce_max(m1, LOG, AX.X))
            link(nc.vector.tensor_tensor(T0, LOG, bt(m1), ALU.is_ge))
            link(nc.vector.tensor_tensor(T0, T0, be(rev), ALU.mult))
            link(nc.vector.reduce_max(k1, T0, AX.X))
            link(nc.vector.tensor_tensor(OH1, be(rev), bt(k1), ALU.is_equal))
            link(nc.vector.scalar_tensor_tensor(T1, OH1, NEG, LOG, ALU.mult, ALU.add))
            link(nc.vector.reduce_max(m2, T1, AX.X))
            nc.vector.tensor_tensor(dlt, m2, m1, ALU.subtract).then_inc(s["exp_arg"], 1)
            link(nc.vector.tensor_tensor(T0, T1, bt(m2), ALU.is_ge))
            link(nc.vector.tensor_tensor(T0, T0, be(rev), ALU.mult))
            link(nc.vector.reduce_max(k2, T0, AX.X))
            link(nc.vector.tensor_tensor(OH2, be(rev), bt(k2), ALU.is_equal))
            nc.vector.tensor_tensor(OHS, OH1, OH2, ALU.add).then_inc(s["ohs"], 1)
            dve.wait_ge(s["exp_done"], 1)
            link(nc.vector.tensor_scalar(w1, ew, 1.0, None, ALU.add))
            link(nc.vector.reciprocal(w1, w1))
            link(nc.vector.tensor_tensor(w2, ew, w1, ALU.mult))
            link(nc.vector.tensor_scalar(rt[:, 5:7, :], rt[:, 5:7, :], DEPTH_SCALE, None, ALU.mult))
            link(nc.vector.tensor_tensor(T0, OH1, bt(w1), ALU.mult))
            link(nc.vector.tensor_tensor(T1, OH2, bt(w2), ALU.mult))
            nc.vector.tensor_tensor(XW[:, :, D:ROW], T0, T1, ALU.add).then_inc(s["comb"], 1)
            dve.wait_ge(s["prefix"], 1)
            link(nc.vector.tensor_copy(T2, PS[:, 4, 0:T * E].rearrange("p (t e) -> p t e", e=E)))
            src, dst = T2, CA
            for step in (1, 2, 4, 8):
                nc.vector.tensor_copy(dst[:, 0:step, :], src[:, 0:step, :])
                link(nc.vector.tensor_tensor(dst[:, step:T, :], src[:, step:T, :], src[:, 0:T - step, :], ALU.add))
                src, dst = dst, (CB if dst is CA else CA)
            cum = src
            link(nc.vector.tensor_tensor(SLOT, cum, T2, ALU.subtract))
            link(nc.vector.tensor_tensor(SLOT, SLOT, PS[:, 3, 0:T * E].rearrange("p (t e) -> p t e", e=E), ALU.add))
            nt, ea, eb, base, end, _ = (ex[:, i, :] for i in range(6))
            link(nc.vector.tensor_tensor(T0.rearrange("p t e -> p (t e)").rearrange("p (e j) -> p e j", e=E),
                                         cum[:, T - 1, :].unsqueeze(2).to_broadcast([P, E, T]),
                                         tile_starts.unsqueeze(1).to_broadcast([P, E, T]), ALU.is_gt))
            link(nc.vector.reduce_sum(nt, T0.rearrange("p t e -> p (t e)").rearrange("p (e j) -> p e j", e=E), AX.X))
            src = nt
            for step, dst in ((1, ea), (2, eb), (4, end)):
                nc.vector.tensor_copy(dst[:, 0:step], src[:, 0:step])
                link(nc.vector.tensor_tensor(dst[:, step:E], src[:, step:E], src[:, 0:E - step], ALU.add))
                src = dst
            link(nc.vector.tensor_tensor(base, end, nt, ALU.subtract))
            link(nc.vector.tensor_scalar(base, base, float(P), None, ALU.mult))
            link(nc.vector.tensor_tensor(SLOT, SLOT, be(base), ALU.add))
            link(nc.vector.tensor_tensor(T0, OH1, SLOT, ALU.mult))
            link(nc.vector.tensor_tensor(T1, OH2, SLOT, ALU.mult))
            link(nc.vector.reduce_sum(slots_f[:, 0, :], T0, AX.X))
            link(nc.vector.reduce_sum(slots_f[:, 1, :], T1, AX.X))
            si, hi_i, lo_i = (slots_i[:, i, :] for i in range(3))
            link(nc.vector.tensor_copy(si, slots_f[:, :, :].rearrange("p c t -> p (c t)")))
            link(nc.vector.tensor_scalar(hi_i, si, 7, None, ALU.logical_shift_right))
            link(nc.vector.tensor_scalar(lo_i, si, P - 1, None, ALU.bitwise_and))
            link(nc.vector.tensor_copy(hi_lo[:, :, :].rearrange("p k c -> p (k c)"),
                                       slots_i[:, 1:3, :].rearrange("p k c -> p (k c)")))
            C = 2 * T // NCH
            for c in range(NCH):
                cs = slice(C * c, C * c + C)
                nc.vector.tensor_tensor(OHLO[:, cs, :], iota128.unsqueeze(1).to_broadcast([P, C, P]),
                                        hi_lo[:, 1, cs].unsqueeze(2).to_broadcast([P, C, P]), ALU.is_equal)
                link(nc.vector.tensor_tensor(RHS[:, cs, 0, :], iota40.unsqueeze(1).to_broadcast([P, C, N_SLOT_TILES]),
                                             hi_lo[:, 0, cs].unsqueeze(2).to_broadcast([P, C, N_SLOT_TILES]),
                                             ALU.is_equal))
                nc.vector.tensor_tensor(RHS[:, cs, 1, :], RHS[:, cs, 0, :],
                                        tcol[:, cs].unsqueeze(2).to_broadcast([P, C, N_SLOT_TILES]), ALU.mult)
                nc.vector.tensor_scalar(RHS[:, cs, 2, :], RHS[:, cs, 0, :], pcol, None, ALU.mult).then_inc(s["onehots"], 1)
            link(nc.vector.tensor_tensor(tmap[:, :, :], iota40.unsqueeze(2).to_broadcast([P, N_SLOT_TILES, E]),
                                         end.unsqueeze(1).to_broadcast([P, N_SLOT_TILES, E]), ALU.is_ge))
            link(nc.vector.reduce_sum(te[:, :], tmap[:, :, :], AX.X))
            link(nc.vector.tensor_scalar(te[:, :], te[:, :], float(E - 1), None, ALU.min))
            link(nc.vector.tensor_tensor(tsel[:, :, :], eidx.unsqueeze(1).to_broadcast([P, N_SLOT_TILES, E]),
                                         te[:, :].unsqueeze(2).to_broadcast([P, N_SLOT_TILES, E]), ALU.is_equal))
            nc.vector.tensor_scalar(te_off[:, :], te[:, :], float(HID), None, ALU.mult).then_inc(s["toff"], 1)
            dve.wait_ge(s["tokens"], 1)
            link(nc.vector.tensor_copy(occ_tok[:, :, :].rearrange("p k n -> p (k n)"), PS[:, 5, 0:3 * N_SLOT_TILES]))
            link(nc.vector.scalar_tensor_tensor(tok[:, 0, :], occ_tok[:, 1, :], float(P), occ_tok[:, 2, :],
                                                ALU.mult, ALU.add))
            link(nc.vector.tensor_scalar(tok[:, 1, :], occ_tok[:, 0, :], -1.0, 1.0, ALU.mult, ALU.add))
            link(nc.vector.scalar_tensor_tensor(tok[:, 2, :], tok[:, 1, :], padrow, tok[:, 0, :], ALU.mult, ALU.add))
            nc.vector.tensor_copy(gidx[:, :], tok[:, 0, :]).then_inc(s["y"], 1)
            nc.vector.tensor_copy(sidx[:, :], tok[:, 2, :]).then_inc(s["idx"], 1)

        def ffn_tensor(pe, f):
            s = FS[f]
            for t in range(T):
                if t % BT == 0:
                    pe.wait_ge(xnt_ready, 4 * (1 + 2 * f) + t // BT + 1)
                last = nc.tensor.matmul(PS[:, 2, E * t:E * t + E], XNT[:, P * t:P * t + P], WR[:, :],
                                        start=True, stop=True)
            last.then_inc(s["logits"], 1)
            pe.wait_ge(s["ohs"], 1)
            flat = OHS.rearrange("p t e -> p (t e)")
            nc.tensor.matmul(PS[:, 3, 0:T * E], upper1, flat, start=True, stop=True)
            nc.tensor.matmul(PS[:, 4, 0:T * E], ones[:, :], flat, start=True, stop=True).then_inc(s["prefix"], 1)
            for c in range(2 * T):
                if c % (2 * T // NCH) == 0:
                    pe.wait_ge(s["onehots"], c // (2 * T // NCH) + 1)
                last = nc.tensor.matmul(PS[:, 5, 0:3 * N_SLOT_TILES], OHLO[:, c, :],
                                        RHS[:, c].rearrange("p k n -> p (k n)"), start=(c == 0), stop=(c == 2 * T - 1))
            last.then_inc(s["tokens"], 1)
            pe.wait_ge(s["toff"], 1)
            if f == 0:
                pe.wait_ge(ld_experts, 16 * 3 * E)
            gath = [s["gath0"], s["gath1"], s["gath2"], s["gath3"]]

            def transpose_x(q, rnd, n):
                pe.wait_ge(gath[q], 16 * (rnd + 1))
                if not isinstance(n, int) or n:
                    pe.wait_ge(s["xt"], n)
                nc.tensor.transpose(PS[:, 0, 0:P], G[q][:, 0:D], ident).then_inc(s["xT"], 1)

            def gate(par, n, off):
                pe.wait_ge(s["xt"], n + 1)
                if not isinstance(n, int) or n:
                    pe.wait_ge(s["silu"], n)
                nc.tensor.matmul(PS[:, 1 + par, :], xt[par][:, :], WG[:, ds(off, HID)],
                                 start=True, stop=True).then_inc(s["gate"], 1)

            def up(par, n, off):
                if not isinstance(n, int) or n:
                    pe.wait_ge(s["h"], n)
                nc.tensor.matmul(PS[:, 3 + par, :], xt[par][:, :], WU[:, ds(off, HID)],
                                 start=True, stop=True).then_inc(s["up"], 1)

            def transpose_h(par, n):
                pe.wait_ge(s["h"], n + 1)
                for j in range(NJ):
                    last = nc.tensor.transpose(PS[:, 5, P * j:P * j + P], hs[par][:, P * j:P * j + P], ident)
                last.then_inc(s["hT"], 1)

            def down(par, n, off):
                pe.wait_ge(s["ht"], n + 1)
                pe.wait_ge(s["y"], n + 1)
                for j in range(NJ):
                    last = nc.tensor.matmul(PS[:, 6, 0:D], ht[par][:, P * j:P * j + P], WD[:, ds(off + P * j, P)],
                                            start=(j == 0), stop=(j == NJ - 1))
                last.then_inc(s["down"], 1)

            def offset(n):
                return pe.value_load(te_off[0:1, n], min_val=0, max_val=HID * (E - 1))

            def tiles(r, ahead=2):
                left = [min(2, 3 - q) if ahead == 0 else 2 for q in range(4)]
                offs = {1: offset(ds(r * 4 + 1, 1))}
                for q in range(4):
                    n, par, nxt = r * 4 + q, q % 2, (q + 1) % 2
                    if left[q] >= 1:
                        gate(nxt, n + 1, offs[q + 1])
                    if q == 0:
                        offs[0] = offset(ds(r * 4, 1))
                    transpose_h(par, n)
                    if left[q] >= 2:
                        transpose_x((q + 2) % 4, r + (q + 2) // 4, n + 2)
                    if left[q] >= 1:
                        up(nxt, n + 1, offs[q + 1])
                    if q < 2 or (q == 2 and ahead):
                        offs[q + 2] = offset(ds(r * 4 + q + 2, 1))
                    down(par, n, offs[q])

            off0 = offset(slice(0, 1))
            transpose_x(0, 0, 0)
            transpose_x(1, 0, 1)
            gate(0, 0, off0)
            up(0, 0, off0)
            with pe.Fori(0, N_SLOT_TILES // 4 - 1) as r:
                tiles(r)
            tiles(N_SLOT_TILES // 4 - 1, ahead=0)

        def ffn_scalar_route(act, f):
            s = FS[f]
            act.wait_ge(s["exp_arg"], 1)
            nc.scalar.activation(rt[:, 7, :], rt[:, 4, :], ACT.Exp).then_inc(s["exp_done"], 1)

        def ffn_scalar(act, f):
            s = FS[f]

            def xt_copy(par, n):
                act.wait_ge(s["xT"], n + 1)
                nc.scalar.activation(xt[par][:, :], PS[:, 0, 0:P], ACT.Copy).then_inc(s["xt"], 1)

            def silu(par, n):
                act.wait_ge(s["gate"], n + 1)
                nc.scalar.activation(hs[par][:, :], PS[:, 1 + par, :], ACT.Silu).then_inc(s["silu"], 1)

            def ht_copy(par, n):
                act.wait_ge(s["hT"], n + 1)
                nc.scalar.activation(ht[par][:, :], PS[:, 5, :], ACT.Copy).then_inc(s["ht"], 1)
            def tiles(r, last=False):
                for q in range(2):
                    n = r * 2 + q
                    if not (last and q == 1):
                        silu((q + 1) % 2, n + 1)
                    ht_copy(q, n)
                    if not last:
                        xt_copy(q, n + 2)
            xt_copy(0, 0)
            xt_copy(1, 1)
            silu(0, 0)
            with act.Fori(0, N_SLOT_TILES // 2 - 1) as r:
                tiles(r)
            tiles(N_SLOT_TILES // 2 - 1, last=True)

        def ffn_vector(dve, f):
            s = FS[f]
            gath = [s["gath0"], s["gath1"], s["gath2"], s["gath3"]]

            def hprod(par, n):
                dve.wait_ge(s["silu"], n + 1)
                dve.wait_ge(s["up"], n + 1)
                nc.vector.tensor_tensor(hs[par][:, :], hs[par][:, :], PS[:, 3 + par, :], ALU.mult).then_inc(s["h"], 1)

            def weight(q, rnd, n):
                dve.wait_ge(gath[q], 16 * (rnd + 1))
                nc.vector.tensor_tensor(wsel[q % 2][:, :], G[q][:, D:ROW], tsel[:, ds(n, 1), :].rearrange("p a e -> p (a e)"),
                                        ALU.mult).then_inc(s["wsel"], 1)
                dve.wait_ge(s["wsel"], 2 * n + 1)
                nc.vector.reduce_sum(wslot[q][:, :], wsel[q % 2][:, :], AX.X).then_inc(s["wsel"], 1)

            def result(par, q, n):
                dve.wait_ge(s["down"], n + 1)
                dve.wait_ge(s["wsel"], 2 * n + 2)
                if not isinstance(n, int) or n >= 2:
                    dve.wait_ge([s["scat0"], s["scat1"]][par], (n - par) * 8)
                nc.vector.tensor_scalar(ytile[par][:, :], PS[:, 6, 0:D], wslot[q][:, 0:1], None,
                                        ALU.mult).then_inc(s["y"], 1)

            def tiles(r, last=False):
                for q in range(4):
                    n = r * 4 + q
                    if not (last and q >= 2):
                        weight((q + 2) % 4, r + (q + 2) // 4, n + 2)
                    if not (last and q == 3):
                        hprod((q + 1) % 2, n + 1)
                    result(q % 2, q, n)
            weight(0, 0, 0)
            weight(1, 0, 1)
            hprod(0, 0)
            tiles(0)
            with dve.Fori(1, N_SLOT_TILES // 4 - 1) as r:
                tiles(r)
            tiles(N_SLOT_TILES // 4 - 1, last=True)

        def ffn_pool(pool, f):
            s = FS[f]
            gath = [s["gath0"], s["gath1"], s["gath2"], s["gath3"]]
            scat = [s["scat0"], s["scat1"]]
            pool.wait_ge(s["idx"], 1)
            pool.wait_ge(s["xn_stored"], 16)
            pool.wait_ge(s["y_init"], 48)

            def carry_wait():
                nc.gpsimd.tensor_tensor(carrier[:, :], zeros16[:, 0:1], zeros16[:, 0:1], ALU.add)

            def gather(par, q, rnd, n):
                nc.gpsimd.tensor_copy(gcur[par][:, :], gidx[:, ds(n, 1)]).then_inc(s["gcopied"], 1)
                pool.wait_ge(s["gcopied"], n + 1)
                carry_wait()
                nc.gpsimd.indirect_dma_start(G[q][:, :], None, xn_dram[f],
                                             bass.IndirectOffsetOnAxis(gcur[par][:, 0:1], axis=0),
                                             bounds_check=T * P - 1, oob_is_err=False).then_inc(gath[q], 16)

            def scatter(par, n):
                if not isinstance(n, int) or n >= 2:
                    pool.wait_ge(scat[par], (n - par) * 8)
                nc.gpsimd.tensor_copy(scur[par][:, :], sidx[:, ds(n, 1)]).then_inc(s["scopied"], 1)
                pool.wait_ge(s["scopied"], n + 1)
                pool.wait_ge(s["y"], n + 2)
                carry_wait()
                nc.gpsimd.indirect_dma_start(y_dram[f][par], bass.IndirectOffsetOnAxis(scur[par][:, 0:1], axis=0),
                                             ytile[par][:, :], None, bounds_check=(T + 1) * P - 1, oob_is_err=True,
                                             compute_op=ALU.add).then_inc(scat[par], 16)
            for n in range(4):
                if n >= 2:
                    pool.wait_ge(gath[n - 2], 16)
                gather(n % 2, n, 0, n)

            def tiles(r, last=False):
                for q in range(4):
                    n = r * 4 + q
                    if not last:
                        pool.wait_ge(gath[(q + 2) % 4], 16 * (r + (q + 2) // 4 + 1))
                        pool.wait_ge(s["xT"], n + 1)
                        pool.wait_ge(s["wsel"], 2 * n + 2)
                        gather(q % 2, q, r + 1, n + 4)
                    scatter(q % 2, n)
            tiles(0)
            with pool.Fori(1, N_SLOT_TILES // 4 - 1) as r:
                tiles(r)
            tiles(N_SLOT_TILES // 4 - 1, last=True)

        def ffn_sync(sp, f):
            s = FS[f]
            sp.wait_ge(ln_done, 4 * (1 + 2 * f) + 4)
            rows = "(t p) d -> p t d"
            sp.dma_start(y_dram[f][0][0:T * P, :].rearrange(rows, p=P), X[:, :, :]).then_inc(s["y_init"], 16)
            sp.wait_ge(s["comb"], 1)
            sp.dma_start(xn_dram[f].rearrange(rows, p=P), XW[:, :, :]).then_inc(s["xn_stored"], 16)
            sp.wait_ge(s["scat0"], 16 * (N_SLOT_TILES // 2))
            sp.dma_start(Y0, y_dram[f][0][0:T * P, :].rearrange(rows, p=P)).then_inc(s["y_loaded"], 16)
            sp.wait_ge(s["scat1"], 16 * (N_SLOT_TILES // 2))
            sp.dma_start(Y1, y_dram[f][1][0:T * P, :].rearrange(rows, p=P)).then_inc(s["y_loaded"], 16)

        y_zeroed, out_stored, cchain, rden_ready, ld_pos = (
            sem("y_zeroed"), sem("out_stored"), sem("cchain"), sem("rden_ready"), sem("ld_pos"))
        block = ctx.enter_context(nc.Block())

        ta = SCR[0:K2, 0:2048].bitcast(f32).rearrange("p (a n) -> p a n", a=2)
        FE = SCR[0:K2, 2048:4096].bitcast(f32).rearrange("p (a n) -> p a n", a=2)
        FQK = SCR[0:K2, 4096:6144].bitcast(f32).rearrange("p (a n) -> p a n", a=2)
        AT = SCR[:, 6144:6144 + 2560].bitcast(f32)
        NT = SCR[0:K2 + 1, 8704:8704 + 1024].bitcast(f32)
        V1 = sb("V1", [P, BT, K2 + 1])
        v1_ones, wo_ready = sem("v1_ones"), sem("wo_ready")
        la = {n: sem("la_" + n) for n in ("proj", "vproj", "min", "exp", "feat", "v", "a", "at", "num", "nt",
                                          "fin", "x")}

        def la_tensor(pe):
            for b in range(B):
                pe.wait_ge(xnt_ready, 8 + b + 1)
                if b:
                    pe.wait_ge(la["feat"], b)
                xb = XNT[:, S * b:S * b + S]
                nc.tensor.matmul(PS[0:K2, 2, :], WQ2[:, :], xb, start=True, stop=True)
                nc.tensor.matmul(PS[0:K2, 3, :], WK2[:, :], xb, start=True, stop=True).then_inc(la["proj"], 1)
                if b:
                    pe.wait_ge(la["v"], b)
                    pe.wait_ge(la["x"], b)
                for t in range(BT):
                    last = nc.tensor.matmul(PS[:, 7, K2 * t:K2 * t + K2], XNT[:, S * b + P * t:S * b + P * t + P],
                                            WV2[:, :], start=True, stop=True)
                last.then_inc(la["vproj"], 1)
                pe.wait_ge(la["feat"], b + 1)
                pe.wait_ge(la["v"], b + 1)
                for kb in range(BT):
                    if b * BT + kb >= 2:
                        pe.wait_ge(la["at"], b * BT + kb - 1)
                    n = S - P * kb
                    nc.tensor.matmul(PS[:, 4 + kb % 2, 0:n], FQK[:, 1, P * kb:P * kb + P], FQK[:, 0, P * kb:S],
                                     start=True, stop=True).then_inc(la["a"], 1)
                if b:
                    pe.wait_ge(la["nt"], b)
                for kb in range(BT):
                    pe.wait_ge(la["at"], b * BT + kb + 1)
                    last = nc.tensor.matmul(PS[0:K2 + 1, 6, P * kb:S], V1[:, kb, :], AT[:, SEG[kb]:SEG[kb] + S - P * kb],
                                            start=(kb == 0), stop=(kb == BT - 1))
                last.then_inc(la["num"], 1)
                pe.wait_ge(la["nt"], b + 1)
                pe.wait_ge(xnt_ready, 12)
                for qb in range(BT):
                    last = nc.tensor.matmul(PS[:, 7 if qb < 2 else 1, (D + 1) * (qb % 2):(D + 1) * (qb % 2 + 1)],
                                            NT[:, P * qb:P * qb + P], WO2[:, :], start=True, stop=True)
                last.then_inc(la["fin"], 1)

        def la_scalar(act):
            for b in range(B):
                act.wait_ge(la["min"], b + 1)
                nc.scalar.activation(FE, ta, ACT.Exp).then_inc(la["exp"], 1)
                act.wait_ge(la["vproj"], b + 1)
                if b:
                    act.wait_ge(la["num"], b)
                nc.scalar.activation(V1[:, :, 0:K2], PS[:, 7, 0:BT * K2].rearrange("p (t m) -> p t m", m=K2),
                                     ACT.Copy).then_inc(la["v"], 1)
                act.wait_ge(la["num"], b + 1)
                if b:
                    act.wait_ge(la["fin"], b)
                nc.scalar.activation(NT, PS[0:K2 + 1, 6, :], ACT.Copy).then_inc(la["nt"], 1)

        def la_vector(dve, link):
            for b in range(B):
                dve.wait_ge(la["proj"], b + 1)
                nc.vector.tensor_scalar(ta, PS[0:K2, 2:4, :], 0.0, None, ALU.min).then_inc(la["min"], 1)
                dve.wait_ge(la["exp"], b + 1)
                nc.vector.scalar_tensor_tensor(FQK.rearrange("p a n -> p (a n)"),
                                               PS[0:K2, 2:4, :].rearrange("p a n -> p (a n)"), 0.0,
                                               FE.rearrange("p a n -> p (a n)"), ALU.max,
                                               ALU.add).then_inc(la["feat"], 1)
                for kb in range(BT):
                    n = S - P * kb
                    dve.wait_ge(la["a"], b * BT + kb + 1)
                    if b:
                        dve.wait_ge(la["num"], b)
                    at = AT[:, SEG[kb]:SEG[kb] + n]
                    diag = nc.vector.tensor_tensor(at[:, 0:P], PS[:, 4 + kb % 2, 0:P], causal1, ALU.mult)
                    if n > P:
                        diag = nc.vector.tensor_copy(at[:, P:n], PS[:, 4 + kb % 2, P:n])
                    diag.then_inc(la["at"], 1)
                dve.wait_ge(la["fin"], b + 1)
                den = stat[:, 4, 0:BT]
                for qb in range(BT):
                    ps = PS[:, 7 if qb < 2 else 1, (D + 1) * (qb % 2):(D + 1) * (qb % 2 + 1)]
                    link(nc.vector.tensor_scalar(den[:, qb:qb + 1], ps[:, D:D + 1], 1e-6, None, ALU.add))
                    link(nc.vector.reciprocal(den[:, qb:qb + 1], den[:, qb:qb + 1]))
                    last = nc.vector.scalar_tensor_tensor(X[:, BT * b + qb, :], ps[:, 0:D], den[:, qb:qb + 1],
                                                          X[:, BT * b + qb, :], ALU.mult, ALU.add)
                last.then_inc(la["x"], 1)

        @block.sync
        def _(sp):
            for g in range(B):
                sp.dma_start(X[:, BT * g:BT * g + BT, :],
                             x[g].rearrange("(t p) d -> p t d", p=P)).then_inc(ld_x[g], 16)
                if g == 0:
                    sp.dma_start(CON[:, :], consts[:, :]).then_inc(ld_const, 16)
            sp.dma_start(WQK[:, :], wqk).then_inc(ld_wqkv, 16)
            sp.dma_start(WV[:, :], wv).then_inc(ld_wqkv, 16)
            sp.wait_ge(slopes_spread, NPART)
            sp.wait_ge(bias_built, 6)
            bias_view = bias_dram.rearrange("r h t -> h r t")
            lo_hi = BIAS[:, 0:2, :]
            for i in range(NPART):
                sp.dma_start(bias_view[:, 4 * i:4 * i + 2, :],
                             BIAS[:, 2 + i:3 + i, :].to_broadcast([H, 2, S])).then_inc(bias_stored, 16)
                sp.dma_start(bias_view[:, 14 + 4 * i:16 + 4 * i, :],
                             BIAS[:, 5 + i:6 + i, :].to_broadcast([H, 2, S])).then_inc(bias_stored, 16)
            for r0 in (2, 12):
                for i in range(NPART):
                    sp.dma_start(bias_view[:, r0 + 4 * i:r0 + 4 * i + 2, :], lo_hi).then_inc(bias_stored, 16)
            sp.dma_start(bias_view[:, 24:26, :], BIAS[:, 8:10, :]).then_inc(bias_stored, 16)
            sp.wait_ge(bias_stored, 16 * 13)
            for hg in range(HG):
                heads = slice(GH * hg, GH * hg + GH)
                for i, A in enumerate((QA, KA)):
                    loaded = crows_loaded[hg] if i == 0 and hg < 2 else bias_loaded
                    sp.dma_start(A[hg][0:12, :].rearrange("r (h t) -> r h t", h=GH),
                                 bias_dram[12 * i:12 * i + 12, heads, :]).then_inc(loaded, 16)
                    sp.dma_start(A[hg][ZERO0:KROWS, :].rearrange("r (h t) -> r h t", h=GH),
                                 bias_dram[24:25, heads, :].to_broadcast([KROWS - ZERO0, GH, S])).then_inc(bias_loaded, 16)
                sp.dma_start(KA[hg][KROWS:MROWS, :].rearrange("r (h t) -> r h t", h=GH),
                             bias_dram[25:26, heads, :].to_broadcast([NPART, GH, S])).then_inc(bias_loaded, 16)
            for g in range(B):
                sp.wait_ge(part3, g + 1)
                stored = parts_stored[g % 2]
                for dst, n, side in ((q_parts_dram[g, 0:3], 3, 0), (q_parts_dram[g, 3:5], 2, 0), (k_parts_dram[g], 3, 1)):
                    sp.dma_start(dst.rearrange("i p t -> p i t"), QKP[g % 2][:, 0:n, side, :]).then_inc(stored, 16)
            for i in range(2):
                sp.wait_ge(parts_stored[i], 2 * 3 * 16)
            for w, d in ((WQ2, wq2), (WK2, wk2), (WV2, wv2), (WR, wr)):
                sp.dma_start(w[:, :], d).then_inc(ld_small, 16)
            sp.wait_ge(vu_cleared, 1)
            sp.dma_start(WO2[0:K2, 0:D], wo2).then_inc(ld_small, 16)
            sp.wait_ge(y_zeroed, 1)
            for f in range(2):
                sp.dma_start(y_dram[f][1].rearrange("(t p) d -> p t d", p=P), zrow[:, :, :].to_broadcast([P, T + 1, D])).then_inc(FS[f]["y_init"], 16)
                sp.dma_start(y_dram[f][0][T * P:(T + 1) * P, :], zrow[:, 0, :]).then_inc(FS[f]["y_init"], 16)

            def load_operands(b, hg):
                for a in range(3):
                    r0 = PROD0 + 24 * a
                    sp.dma_start(QA[hg][r0:r0 + 24, :],
                                 q_rows_dram[ds(b, 1), HD * a:HD * a + 24, UC * hg:UC * hg + UC]
                                 .rearrange("o r n -> (o r) n")).then_inc(qk_loaded[hg], 16)
                    sp.dma_start(KA[hg][r0:r0 + 24, :],
                                 k_rows_dram[ds(b, 1), :, UC * hg:UC * hg + UC]
                                 .rearrange("o r n -> (o r) n")).then_inc(qk_loaded[hg], 16)

            def load_max(u, hg):
                sp.wait_ge(cparts_ready, u + 1)
                for i in range(NPART):
                    sp.dma_start(QA[hg][KROWS + i:KROWS + i + 1, :].rearrange("o (k t) -> o k t", t=P),
                                 cparts[hg % 2][:, i, :]).then_inc(crows_loaded[hg % 2], 16)

            for hg in range(3):
                load_operands(0, hg)
            load_max(0, 0)
            with sp.Fori(0, B - 1) as b:
                for j in range(HG):
                    u = b * HG + j
                    sp.wait_ge(exp_done, NX * u + 2)
                    load_operands(b + (j + 3) // HG, (j + 3) % HG)
                    load_max(u + 1, (j + 1) % HG)
            b = B - 1
            for j in range(HG):
                u = b * HG + j
                if j == 0:
                    sp.wait_ge(exp_done, NX * u + 2)
                    load_operands(b, 3)
                if j < 3:
                    load_max(u + 1, j + 1)
            ffn_sync(sp, 0)
            ffn_sync(sp, 1)
            sp.wait_ge(FS[1]["out_sum"], 1)
            sp.dma_start(out.rearrange("b (t p) d -> p b t d", p=P),
                         X[:, :, :].rearrange("p (b t) d -> p b t d", b=B)).then_inc(out_stored, 16)
            sp.wait_ge(out_stored, 16)

        @block.gpsimd
        def _(pool):
            count = [0]

            def link(ins):
                count[0] += 1
                ins.then_inc(pool_chain, 1)
                pool.wait_ge(pool_chain, count[0])
            pool.dma_start(POS[:, :], pos_in).then_inc(ld_pos, 16)
            pool.dma_start(slope[:, :], slopes).then_inc(ld_pos, 16)
            pool.wait_ge(ld_pos, 32)
            link(nc.gpsimd.tensor_copy(slope_pb[:, 0:1], slope[:, :]))
            link(nc.gpsimd.tensor_tensor(slope_r[:, 0:1], slope[:, :], slope_pb[:, 0:1], ALU.subtract))
            link(nc.gpsimd.tensor_copy(slope_pb[:, 1:2], slope_r[:, 0:1]))
            link(nc.gpsimd.tensor_tensor(slope_r[:, 1:2], slope_r[:, 0:1], slope_pb[:, 1:2], ALU.subtract))
            link(nc.gpsimd.tensor_copy(slope_pb[:, 2:3], slope_r[:, 1:2]))
            nc.gpsimd.tensor_copy(slope_p[:, :], slope_pb[:, :]).then_inc(slope_split, 1)
            pos = POS[:, :].rearrange("h (k t) -> h k t", k=2)
            nc.gpsimd.tensor_copy(BIAS[:, 0:2, :], pos).then_inc(bias_built, 1)
            nc.gpsimd.memset(BIAS[:, 8, :].bitcast(f32), 0.0).then_inc(bias_built, 1)
            nc.gpsimd.memset(zeros16[:, :], 0.0)
            for i in range(2):
                link(nc.gpsimd.memset(VU[i][:, :, :, :], 0.0))
                link(nc.gpsimd.memset(VU[i][:, :, :, HD:HD + 1], 1.0))
            link(nc.gpsimd.memset(WO2[:, :], 0.0))
            link(nc.gpsimd.memset(WO2[K2:K2 + 1, D:D + 1], 1.0))
            link(nc.gpsimd.memset(V1[:, :, K2:K2 + 1], 1.0))
            nc.gpsimd.memset(zrow[:, :, :], 0.0).then_inc(y_zeroed, 1)
            nc.gpsimd.memset(tok[:, :, :], 0.0).then_inc(vu_cleared, 1)

            def split_max(u, par):
                pool.wait_ge(negc_ready, u + 1)
                if not isinstance(u, int) or u >= 2:
                    pool.wait_ge(crows_loaded[par], 24 * (u - par) + 16)
                nc.gpsimd.tensor_tensor(cparts[par][:, 0, :], negc[par][:, :], zeros16[:, :],
                                        ALU.subtract).then_inc(cchain, 1)
                pool.wait_ge(cchain, 3 * u + 1)
                nc.gpsimd.tensor_tensor(negr[:, 0, :], negc[par][:, :], cparts[par][:, 0, :],
                                        ALU.subtract).then_inc(cchain, 1)
                pool.wait_ge(cchain, 3 * u + 2)
                nc.gpsimd.tensor_tensor(cparts[par][:, 1, :], negr[:, 0, :], zeros16[:, :],
                                        ALU.subtract).then_inc(cchain, 1)
                pool.wait_ge(cchain, 3 * u + 3)
                nc.gpsimd.tensor_tensor(cparts[par][:, 2, :], negr[:, 0, :], cparts[par][:, 1, :],
                                        ALU.subtract).then_inc(cparts_ready, 1)

            def unit_values(u, par, b, hg):
                pool.wait_ge(pv_done, u + 1)
                nc.gpsimd.tensor_copy(VU[par][:, :, :, 0:HD],
                                      V[:, ds(b * BT, BT), 32 * hg:32 * hg + 32]
                                      .rearrange("p t (a d) -> p t a d", a=GH)).then_inc(vu_ready, 1)

            def add_unit(u, par, b, hg):
                pool.wait_ge(normed, u + 2)
                xs = X[:, ds(b * BT, BT), 32 * hg:32 * hg + 32].rearrange("p t (a d) -> p t a d", a=GH)
                nc.gpsimd.tensor_tensor(xs, xs, NRM[par][:, :, :, :], ALU.add).then_inc(x_added, 1)

            nc.gpsimd.memset(gcur[0][:, :], 0).then_inc(x_added, 1)
            nc.gpsimd.memset(gcur[1][:, :], 0).then_inc(x_added, 1)
            pool.wait_ge(v_copied, B)
            unit_values(0, 0, 0, 0)
            split_max(0, 0)
            with pool.Fori(0, B - 1) as b:
                for j in range(HG):
                    u = b * HG + j
                    split_max(u + 1, (j + 1) % 2)
                    unit_values(u + 1, (j + 1) % 2, b + (j + 1) // HG, (j + 1) % HG)
                    add_unit(u, j % 2, b, j)
            b = B - 1
            for j in range(HG):
                u = b * HG + j
                if j < HG - 1:
                    split_max(u + 1, (j + 1) % 2)
                    unit_values(u + 1, (j + 1) % 2, b, j + 1)
                add_unit(u, j % 2, b, j)
            ffn_pool(pool, 0)
            ffn_pool(pool, 1)

        @block.scalar
        def _(act):
            act.wait_ge(slope_split, 1)
            pos_lo = POS[:, 0:S]
            for i in range(NPART):
                nc.scalar.activation(BIAS[:, 2 + i, :], pos_lo, ACT.Identity, bias=slope_p[:, i:i + 1],
                                     scale=0.0).then_inc(slopes_spread, 1)
            act.wait_ge(slopes_spread, NPART)
            for i in range(NPART):
                nc.scalar.activation(BIAS[:, 5 + i, :], BIAS[:, 2 + i, :], ACT.Copy,
                                     scale=-1.0).then_inc(bias_built, 1)
            nc.scalar.activation(BIAS[:, 9, :], pos_lo, ACT.Copy, scale=0.0, bias=1.0).then_inc(bias_built, 1)
            ln_scalar_stats(act, 0)
            for g in range(B):
                ln_scalar_copy(act, 0, g)
            for g in range(B):
                act.wait_ge(qk_proj, g + 1)
                if g:
                    act.wait_ge(part3, g)
                nc.scalar.activation(QK[:, 0, :], PS[:, 2, :], ACT.Copy, scale=float(D) ** -0.5)
                nc.scalar.activation(QK[:, 1, :], PS[:, 3, :], ACT.Copy).then_inc(qk_copied, 1)
                act.wait_ge(qk_copied, g + 1)
                if g >= 2:
                    act.wait_ge(parts_stored[g % 2], 3 * 16)
                nc.scalar.activation(QKP[g % 2][:, 0], QK, ACT.Copy).then_inc(part1, 1)
                act.wait_ge(rest1, g + 1)
                nc.scalar.activation(QKP[g % 2][:, 1], QKR, ACT.Copy).then_inc(part2, 1)

            def exps(u, par):
                act.wait_ge(pv_done, u + 1)
                for k, (a0, na, per, kb) in enumerate(XGROUPS):
                    n = S - P * kb
                    act.wait_ge(st_ready, NX * u + k + 1)
                    bank = 2 + 2 * (k % 2)
                    nb = na // per
                    src = (PS[:, bank, 0:na * n].rearrange("p (a n) -> p a n", a=na) if nb == 1 else
                           PS[:, bank:bank + nb, 0:per * n] if per == 1 else
                           PS[:, bank:bank + nb, :].rearrange("p k (a n) -> p (k a) n", a=per))
                    nc.scalar.activation(PT[par][:, a0:a0 + na, SEG[kb]:SEG[kb] + n], src,
                                         ACT.Exp).then_inc(exp_done, 1)

            def evacuate(u):
                act.wait_ge(pv_done, u + 3)
                act.wait_ge(to_ready, u + 1)
                nc.scalar.activation(OT[:, :], PS[:, 6, :], ACT.Copy).then_inc(ot_ready, 1)

            act.wait_ge(bias_stored, 16 * 13)
            for e in range(E):
                cols = slice(HID * e, HID * e + HID)
                act.dma_start(WG[:, cols], wg[e]).then_inc(ld_experts, 16)
                act.dma_start(WU[:, cols], wu[e]).then_inc(ld_experts, 16)
                act.dma_start(WD[:, cols].rearrange("p (j c) -> p j c", j=NJ),
                              wd[e].rearrange("(j p) c -> p j c", p=P)).then_inc(ld_experts, 16)

            with act.Fori(0, B) as b:
                for j in range(HG):
                    exps(b * HG + j, j % 2)
                    evacuate(b * HG + j)
            for f in range(2):
                ln_scalar_stats(act, 1 + 2 * f)
                for g in range(B):
                    ln_scalar_copy(act, 1 + 2 * f, g)
                ffn_scalar_route(act, f)
                ffn_scalar(act, f)
                if f == 0:
                    ln_scalar_stats(act, 2)
                    for g in range(B):
                        ln_scalar_copy(act, 2, g)
                    la_scalar(act)

        @block.tensor
        def _(pe):
            pe.wait_ge(ld_const, 16)
            for g in range(B):
                ln_tensor(pe, 0, g)
            pe.wait_ge(ld_wqkv, 32)
            for g in range(B):
                pe.wait_ge(xnt_ready, g + 1)
                if g:
                    pe.wait_ge(qk_copied, g)
                xg = XNT[:, S * g:S * g + S]
                nc.tensor.matmul(PS[:, 2, :], WQK[:, 0:D], xg, start=True, stop=True)
                nc.tensor.matmul(PS[:, 3, :], WQK[:, D:2 * D], xg, start=True, stop=True).then_inc(qk_proj, 1)
                if g >= 2:
                    pe.wait_ge(v_copied, g - 1)
                for t in range(BT):
                    last = nc.tensor.matmul(PS[:, 4 + g % 2, P * t:P * t + P], XNT[:, S * g + P * t:S * g + P * t + P],
                                            WV[:, :], start=True, stop=True)
                last.then_inc(v_proj, 1)
            pe.wait_ge(consts_cast, 1)

            def max_bank(u, hg, k, index, first):
                a0, na, i = MBANKS[k]
                n = P * (i + 1)
                bank = (NM * hg + k) % 2
                if not (first and index < 2):
                    pe.wait_ge(max_used, index - 1)
                for a in range(a0, a0 + na):
                    seg = PS[:, bank, (a - a0) * n:(a - a0) * n + n]
                    nc.tensor.matmul(seg, QA[hg][0:KROWS, S * a + P * i:S * a + P * i + P],
                                     KA[hg][0:KROWS, S * a:S * a + n], start=(a == a0), stop=False,
                                     skip_group_check=True)
                diag = PS[:, bank, 0:na * n].rearrange("p (a n) -> p a n", a=na)[:, :, n - P:n]
                nc.tensor.matmul(diag, ident_b[:, :], mask_qk4[:, 0:na, :], start=False, stop=True,
                                 skip_group_check=True).then_inc(max_ready, 1)

            def transpose_max(u, par):
                pe.wait_ge(max_used, NM * (u + 1))
                if not isinstance(u, int) or u:
                    pe.wait_ge(normed, u)
                nc.tensor.transpose(PS[0:GH * BT, 7, 0:P], cmax[par][:, :, :].rearrange("p a i -> p (a i)"),
                                    ident).then_inc(cmax_transposed, 1)

            def scores_t(u, hg, k):
                a0, na, per, kb = XGROUPS[k]
                n = S - P * kb
                pe.wait_ge(exp_done, NX * u + k + 1)
                for a in range(a0, a0 + na):
                    bank = 2 + 2 * (k % 2) + (a - a0) // per
                    c = (a - a0) % per * n
                    nc.tensor.matmul(PS[:, bank, c:c + n], KA[hg][0:MROWS, S * a + P * kb:S * a + P * kb + P],
                                     QA[hg][0:MROWS, S * a + P * kb:S * a + S], start=(c == 0), stop=False,
                                     skip_group_check=True)
                for bk in range(na // per):
                    bank = 2 + 2 * (k % 2) + bk
                    diag = PS[:, bank, 0:per * n].rearrange("p (a n) -> p a n", a=per)[:, :, 0:P]
                    last = nc.tensor.matmul(diag, ident_b[:, :], mask_kq[:, 0:per, :], start=False, stop=True,
                                            skip_group_check=True)
                last.then_inc(st_ready, 1)

            def values(u, par, kb):
                pe.wait_ge(exp_done, NX * u + GROUPS_OF_KB[kb] + 2)
                if kb == 0:
                    pe.wait_ge(vu_ready, u + 1)
                    pe.wait_ge(ot_ready, u + 1)
                for a in range(GH):
                    last = nc.tensor.matmul(PS[32 * a:32 * a + 32, 6, P * kb:S], VU[par][:, kb, a, :],
                                            PT[par][:, a, SEG[kb]:SEG[kb] + S - P * kb],
                                            start=(kb == 0), stop=(kb == BT - 1), skip_group_check=True)
                if kb == BT - 1:
                    last.then_inc(pv_done, 1)

            def transpose_out(u):
                pe.wait_ge(ot_ready, u + 2)
                for t in range(BT):
                    last = nc.tensor.transpose(PS[:, 7, P * t:P * t + P], OT[:, P * t:P * t + P], ident)
                last.then_inc(to_ready, 1)

            def step(u, j, lookahead=2):
                mb = [lambda k=k: max_bank(u + 2, (j + 2) % HG, k, NM * (u + 2) + k, False) if lookahead == 2 else None
                      for k in range(NM)]
                if lookahead == 2:
                    pe.wait_ge(qk_loaded[(j + 2) % HG], 96 * (batch_of(u, j, 2) + 1))
                mb[0](), mb[1]()
                if lookahead >= 1:
                    transpose_max(u + 1, (j + 1) % 2)
                pe.wait_ge(crows_loaded[j % 2], 24 * (u - j % 2) + 64)
                scores_t(u, j, 0)
                mb[2](), mb[3]()
                scores_t(u, j, 1)
                mb[4]()
                scores_t(u, j, 2)
                mb[5]()
                scores_t(u, j, 3)
                mb[6]()
                scores_t(u, j, 4)
                mb[7]()
                scores_t(u, j, 5)
                mb[8]()
                if lookahead >= 1:
                    pe.wait_ge(negc_ready, u + 2)
                else:
                    pe.wait_ge(normed, u + 1)
                values(u, j % 2, 0)
                values(u, j % 2, 1)
                mb[9]()
                values(u, j % 2, 2)
                values(u, j % 2, 3)
                mb[10]()
                transpose_out(u)

            def batch_of(u, j, ahead):
                return cur_b[0] + (j + ahead) // HG
            cur_b = [0]
            pe.wait_ge(bias_loaded, (6 + 8 + 4) * 16)
            for i in range(2):
                pe.wait_ge(crows_loaded[i], 16)
            pe.wait_ge(exp_done, 2)
            for u in range(2):
                pe.wait_ge(qk_loaded[u], 96)
                for k in range(NM):
                    max_bank(u, u, k, NM * u + k, True)
                if u == 0:
                    transpose_max(0, 0)
            with pe.Fori(0, B - 1) as b:
                cur_b[0] = b
                for j in range(HG):
                    step(b * HG + j, j)
            cur_b[0] = B - 1
            for j in range(HG):
                step((B - 1) * HG + j, j, lookahead=min(2, HG - 1 - j))
            for f in range(2):
                for g in range(B):
                    ln_tensor(pe, 1 + 2 * f, g)
                if f == 0:
                    pe.wait_ge(ld_small, 16 * 5)
                ffn_tensor(pe, f)
                if f == 0:
                    for g in range(B):
                        ln_tensor(pe, 2, g)
                    la_tensor(pe)

        @block.vector
        def _(dve):
            count = [0]

            def link(ins):
                count[0] += 1
                ins.then_inc(dve_chain, 1)
                dve.wait_ge(dve_chain, count[0])
            ln_vector(dve, link, 0, lambda e, g: e.wait_ge(ld_x[g], 16))
            dve.wait_ge(ld_const, 16)
            nc.vector.memset(ones[:, :], 1.0)
            nc.vector.tensor_copy(ident_b[:, :], ident)
            for a in range(GH):
                nc.vector.tensor_scalar(mask_kq[:, a, :], causal1, -NEG, NEG, ALU.mult,
                                        ALU.add).then_inc(exp_done if a < 2 else pv_done, 1)
            for a in range(GH):
                nc.vector.tensor_scalar(mask_qk4[:, a, :], upper1, NEG, None,
                                        ALU.mult).then_inc((normed, ot_ready, to_ready, consts_cast)[a], 1)
            for g in range(B):
                dve.wait_ge(v_proj, g + 1)
                nc.vector.tensor_copy(V[:, BT * g:BT * g + BT, :],
                                      PS[:, 4 + g % 2, :].rearrange("p (t n) -> p t n", t=BT)).then_inc(v_copied, 1)
                dve.wait_ge(part1, g + 1)
                if g:
                    dve.wait_ge(part2, g)
                nc.vector.tensor_tensor(QKR, QK, QKP[g % 2][:, 0], ALU.subtract).then_inc(rest1, 1)
                dve.wait_ge(part2, g + 1)
                nc.vector.tensor_tensor(QKP[g % 2][:, 2], QKR, QKP[g % 2][:, 1], ALU.subtract).then_inc(part3, 1)

            def reduce(u, hg, k, index):
                a0, na, i = MBANKS[k]
                n = P * (i + 1)
                dve.wait_ge(max_ready, index + 1)
                nc.vector.reduce_max(cmax[hg % 2][:, a0:a0 + na, i],
                                     PS[:, (NM * hg + k) % 2, 0:na * n].rearrange("p (a n) -> p a n", a=na),
                                     AX.X).then_inc(max_used, 1)

            def negate(u, par):
                dve.wait_ge(cmax_transposed, u + 1)
                if not isinstance(u, int) or u:
                    dve.wait_ge(cparts_ready, u)
                nc.vector.tensor_scalar(negc[par][:, :], PS[0:GH * BT, 7, 0:P], -1.0, None,
                                        ALU.mult).then_inc(negc_ready, 1)

            def normalise(u, par):
                dve.wait_ge(to_ready, u + 2)
                o = PS[:, 7, :].rearrange("p (t a m) -> p t a m", t=BT, a=GH)
                nc.vector.reciprocal(rden[:, :, :], o[:, :, :, HD]).then_inc(rden_ready, 1)
                dve.wait_ge(rden_ready, u + 1)
                dve.wait_ge(x_added, u + 1)
                nc.vector.tensor_tensor(NRM[par][:, :, :, :].rearrange("p t a d -> p (t a) d"),
                                        PS[:, 7, :].rearrange("p (g m) -> p g m", m=32)[:, :, 0:HD],
                                        rden[:, :, :].rearrange("p t a -> p (t a)").unsqueeze(2)
                                        .to_broadcast([P, BT * GH, HD]), ALU.mult).then_inc(normed, 1)

            def step(u, j, lookahead=2):
                def red(k):
                    if lookahead == 2:
                        reduce(u + 2, (j + 2) % HG, k, NM * (u + 2) + k)
                red(0)
                red(1)
                if lookahead >= 1:
                    negate(u + 1, (j + 1) % 2)
                for k in range(2, NM):
                    red(k)
                normalise(u, j % 2)

            for u in range(2):
                for k in range(NM):
                    reduce(u, u, k, NM * u + k)
                if u == 0:
                    negate(0, 0)
            with dve.Fori(0, B - 1) as b:
                for j in range(HG):
                    step(b * HG + j, j)
            for j in range(HG):
                step((B - 1) * HG + j, j, lookahead=min(2, HG - 1 - j))
            for f in range(2):
                s = FS[f]
                if f == 0:
                    ln_vector(dve, link, 1, lambda e, g: e.wait_ge(x_added, 2 + HG * (g + 1)))
                else:
                    ln_vector(dve, link, 3, lambda e, g: None)
                route_vector(dve, link, f)
                ffn_vector(dve, f)
                dve.wait_ge(s["y_loaded"], 32)
                nc.vector.tensor_tensor(X[:, :, :], Y0, Y1, ALU.add).then_inc(s["out_sum"], 1)
                if f == 0:
                    dve.wait_ge(s["out_sum"], 1)
                    ln_vector(dve, link, 2, lambda e, g: None)
                    la_vector(dve, link)
                    dve.wait_ge(la["x"], B)


def kernel(**inputs):
    import numpy as np
    import concourse.bacc as bacc
    from concourse.bass_utils import run_bass_kernel_spmd

    f = {n: np.asarray(a) for n, a in inputs.items()}
    w = f["L0_attn_a_W_kqv"]
    by_place = [np.ascontiguousarray(w[:, i * D:(i + 1) * D].reshape(D, H, HD).transpose(0, 2, 1).reshape(D, D))
                for i in (1, 0)]
    p, c = np.arange(P)[:, None], np.arange(P)[None, :]
    row = lambda v: np.broadcast_to(np.asarray(v, np.float32), (P, len(v)))
    consts = np.concatenate([
        (p == c), (c > p), (c >= p), row(128 * np.arange(T)), row(E - np.arange(E)), row(np.arange(E)),
        row(np.arange(N_SLOT_TILES)), p, T * P + p, row(np.tile(np.arange(T), 2)), row(np.arange(P))],
        axis=1).astype(np.float32)
    t = np.arange(S)
    pos = np.broadcast_to(np.concatenate([t % 256, t - t % 256]).astype(np.float32), (H, 2 * S))
    arrays = {
        "x": f["L0_attn_a_x"], "wqk": np.concatenate(by_place, axis=1), "wv": w[:, 2 * D:],
        "slopes": f["L0_attn_a_m"].reshape(H, 1), "wq2": f["L0_attn_b_Wq"].T, "wk2": f["L0_attn_b_Wk"].T,
        "wv2": f["L0_attn_b_Wv"].T, "wo2": f["L0_attn_b_Wo"].T, "wr": f["L0_ffn_Wr"], "wg": f["L0_ffn_Wg"],
        "wu": f["L0_ffn_Wu"], "wd": f["L0_ffn_Wd"], "consts": consts, "pos_in": pos}
    arrays = {n: np.ascontiguousarray(a) for n, a in arrays.items()}
    nc = bacc.Bacc("TRN2", target_bir_lowering=False, num_devices=1)
    args = {n: nc.dram_tensor(n, a.shape, mybir.dt.from_np(a.dtype), kind="ExternalInput").ap()
            for n, a in arrays.items()}
    args["out"] = nc.dram_tensor("out", (B, S, D), mybir.dt.float32, kind="ExternalOutput").ap()
    build(nc, **args)
    r = run_bass_kernel_spmd(nc, [arrays], core_ids=[0])
    return r.results[0]["out"]
```

```python
import concourse.bass as bass
from concourse import mybir
from contextlib import ExitStack

B, S, D = 4, 512, 128
P = 128
T = B * S // P
BT = S // P
H, HD = 16, 8
HG, GH = 4, 4
U = B * HG
E, HID = 8, 512
NJ = HID // P
K2 = 64
N_SLOT_TILES = 40
ROW = D + E
NPART = 3
KROWS = 96
PROD0 = KROWS - NPART * NPART * HD
MROWS = KROWS + NPART
UC = GH * S
NEG = -1.0e30
EPS = 1e-5
SEG = [0, S, S + 384, S + 384 + 256]
PCOLS = 1280

MBANKS = [(0, 4, 0), (0, 2, 1), (2, 2, 1)] + [(a, 1, 2) for a in range(4)] + [(a, 1, 3) for a in range(4)]
NM = len(MBANKS)
XGROUPS = [(0, 2, 1, 0), (2, 2, 1, 0), (0, 2, 1, 1), (2, 2, 1, 1), (0, 4, 2, 2), (0, 4, 4, 3)]
NX = len(XGROUPS)
GROUPS_OF_KB = [2, 4, 5, 6]


def build(nc, x, wqk, wv, slopes, wq2, wk2, wv2, wo2, wr, wg, wu, wd, consts, pos_in, out):
    f32, bf16, i32 = mybir.dt.float32, mybir.dt.bfloat16, mybir.dt.int32
    ALU, ACT, AX = mybir.AluOpType, mybir.ActivationFunctionType, mybir.AxisListType
    ds = bass.ds
    ctx = ExitStack()
    with ctx:
        def sb(name, shape, dt=f32):
            return ctx.enter_context(nc.sbuf_tensor(name, shape, dt))

        def sem(name):
            return ctx.enter_context(nc.semaphore(name))

        def dram(name, shape, dt=f32):
            return nc.dram_tensor(name, shape, dt, kind="Internal").ap()

        parts_dram = dram("parts_dram", (B, 2, NPART, P, S), bf16)
        rows_dram = parts_dram.rearrange("b a i (d h) t -> b a i d (h t)", h=H)
        bias_dram = dram("bias_dram", (2, PROD0, H, S), bf16)
        xn_dram = [dram(f"xn_dram{f}", (T * P, ROW)) for f in range(2)]
        y_dram = [[dram(f"y_dram{f}_{i}", ((T + 1) * P, D)) for i in range(2)] for f in range(2)]

        X = sb("X", [P, T, D])
        XW = sb("XW", [P, T, ROW])
        XNT = sb("XNT", [P, T * P])
        CON = sb("CON", [P, consts.shape[1]])
        ident = CON[:, 0:128]
        upper1 = CON[:, 128:256]
        causal1 = CON[:, 256:384]
        tile_starts = CON[:, 384:400]
        rev = CON[:, 400:408]
        eidx = CON[:, 408:416]
        iota40 = CON[:, 416:456]
        pcol = CON[:, 456:457]
        padrow = CON[:, 457:458]
        tcol = CON[:, 458:490]
        iota128 = CON[:, 490:618]
        slots_before = CON[:, 618:682].rearrange("p (e k) -> p e k", e=E)
        up_to = CON[:, 682:746].rearrange("p (e k) -> p e k", e=E)
        ones_b = sb("ones_b", [P, P], bf16)
        upper_b = sb("upper_b", [P, P], bf16)
        stat = sb("stat", [P, 3, T])
        half_stat = sb("half_stat", [P, T, 6])
        mean_var = sb("mean_var", [P, T, 2])
        eps = sb("eps", [P, 1])
        ident_b = sb("ident_b", [P, P], bf16)
        mask_kq = sb("mask_kq", [P, GH, P], bf16)
        mask_qk4 = sb("mask_qk4", [P, GH, P], bf16)
        WQK = sb("WQK", [P, 2 * D])
        WV = sb("WV", [P, D])
        WQ2 = sb("WQ2", [P, 2, K2])
        WK2 = sb("WK2", [P, 2, K2])
        WV2 = sb("WV2", [P, K2])
        WO2 = sb("WO2", [P, D + 1])
        WR = sb("WR", [P, E])
        WE = sb("WE", [P, 3, E * HID])
        WG, WU, WD = WE[:, 0], WE[:, 1], WE[:, 2]
        V = sb("V", [P, T, D])
        SCR = sb("SCR", [P, 5 * 4096], bf16)
        early = WE.rearrange("p k n -> p (k n)")
        BIAS = early[0:H, 0:5 * S].bitcast(bf16).rearrange("p (r t) -> p r t", r=10)
        POS = early[0:H, 5 * S:7 * S]
        QKR = [early[:, (7 + 2 * i) * S:(9 + 2 * i) * S].rearrange("p (a n) -> p a n", a=2) for i in range(2)]
        QKP = [early[:, (11 + 3 * g) * S:(14 + 3 * g) * S].bitcast(bf16).rearrange("p (c a n) -> p c a n", c=NPART, a=2)
               for g in range(B)]
        slope = sb("slope", [H, 1])
        slope_r = sb("slope_r", [H, 2])
        slope_p = sb("slope_p", [H, 3])
        slope_pb = sb("slope_pb", [H, 3], bf16)
        QA = [sb(f"QA{i}", [MROWS, UC], bf16) for i in range(HG)]
        KA = [sb(f"KA{i}", [MROWS, UC], bf16) for i in range(HG)]
        PT = [SCR[:, 10240 * i:10240 * (i + 1)].bitcast(f32).rearrange("p (a n) -> p a n", a=GH)
              for i in range(2)]
        VU = [sb(f"VU{i}", [P, BT, GH, 32]) for i in range(2)]
        cmax = [sb(f"cmax{i}", [P, GH, BT]) for i in range(2)]
        negc = [sb(f"negc{i}", [GH * BT, P]) for i in range(2)]
        negr = sb("negr", [GH * BT, 1, P])
        zeros16 = sb("zeros16", [GH * BT, P])
        carrier = sb("carrier", [GH * BT, 1])
        cparts = [sb(f"cparts{i}", [GH * BT, NPART, P], bf16) for i in range(2)]
        OT = sb("OT", [P, S])
        rden = sb("rden", [P, BT, GH])
        NRM = [sb(f"NRM{i}", [P, BT, GH, HD]) for i in range(2)]

        PS = ctx.enter_context(nc.psum_tensor("PS", [P, 8, 512], f32))

        ld_x = [sem(f"ld_x{g}") for g in range(B)]
        ld_const, ld_wqkv, ld_small, ld_experts = sem("ld_const"), sem("ld_wqkv"), sem("ld_small"), sem("ld_experts")
        dve_chain, pool_chain, act_chain = sem("dve_chain"), sem("pool_chain"), sem("act_chain")
        ln_var, ln_centred, ln_std = sem("ln_var"), sem("ln_centred"), sem("ln_std")
        ln_done, ln_transposed, xnt_ready = sem("ln_done"), sem("ln_transposed"), sem("xnt_ready")
        consts_cast = sem("consts_cast")
        wq_scaled, k_ones, qk_proj, v_proj, v_copied = (
            sem("wq_scaled"), sem("k_ones"), sem("qk_proj"), sem("v_proj"), sem("v_copied"))
        part1, rest1, part2, part3 = sem("part1"), sem("rest1"), sem("part2"), sem("part3")
        parts_stored = [sem(f"parts_stored{g}") for g in range(B)]
        slopes_spread = sem("slopes_spread")
        bias_built, bias_stored, bias_loaded, slope_split = (
            sem("bias_built"), sem("bias_stored"), sem("bias_loaded"), sem("slope_split"))
        eps_ready = sem("eps_ready")
        vu_cleared = sem("vu_cleared")
        qk_loaded = [sem(f"qk_loaded{i}") for i in range(HG)]
        max_ready, max_used, st_ready, exp_done = (
            sem("max_ready"), sem("max_used"), sem("st_ready"), sem("exp_done"))
        cmax_transposed, negc_ready, cparts_ready, crows_loaded = (
            sem("cmax_transposed"), sem("negc_ready"), sem("cparts_ready"), [sem("crows_loaded0"), sem("crows_loaded1")])
        vu_ready, pv_done, ot_ready, to_ready, normed, x_added = (
            sem("vu_ready"), sem("pv_done"), sem("ot_ready"), sem("to_ready"), sem("normed"), sem("x_added"))

        std, rstd = stat[:, 0, :], stat[:, 1, :]

        def ln_stats(dve, link, LN, g):
            gs = slice(BT * g, BT * g + BT)
            for t in range(BT * g, BT * g + BT):
                last = nc.vector.bn_stats(half_stat[:, t, :], X[:, t, :])
            link(last)
            for t in range(BT * g, BT * g + BT):
                last = nc.vector.bn_aggr(mean_var[:, t, :], half_stat[:, t, :])
            last.then_inc(ln_var, 1)
            dve.wait_ge(ln_var, 4 * LN + g + 1)
            nc.vector.tensor_tensor(XW[:, gs, 0:D], X[:, gs, :], mean_var[:, gs, 0:1].to_broadcast([P, BT, D]),
                                    ALU.subtract).then_inc(ln_centred, 1)

        def ln_scale(dve, link, LN, g):
            gs = slice(BT * g, BT * g + BT)
            dve.wait_ge(ln_std, 4 * LN + g + 1)
            link(nc.vector.reciprocal(rstd[:, gs], std[:, gs]))
            dve.wait_ge(ln_centred, 4 * LN + g + 1)
            nc.vector.tensor_tensor(XW[:, gs, 0:D], XW[:, gs, 0:D], rstd[:, gs].unsqueeze(2).to_broadcast([P, BT, D]),
                                    ALU.mult).then_inc(ln_done, 1)

        def ln_scalar_std(act, LN, g):
            gs = slice(BT * g, BT * g + BT)
            act.wait_ge(ln_var, 4 * LN + g + 1)
            nc.scalar.activation(std[:, gs], mean_var[:, gs, 1], ACT.Sqrt, bias=eps[:, 0:1]).then_inc(ln_std, 1)

        def ln_scalar_copy(act, LN, g):
            act.wait_ge(ln_transposed, 4 * LN + g + 1)
            nc.scalar.activation(XNT[:, S * g:S * g + S], PS[:, g % 2, :], ACT.Copy).then_inc(xnt_ready, 1)

        def ln_tensor(pe, LN, g):
            pe.wait_ge(ln_done, 4 * LN + g + 1)
            if g >= 2:
                pe.wait_ge(xnt_ready, 4 * LN + g - 1)
            for t in range(BT):
                last = nc.tensor.transpose(PS[:, g % 2, P * t:P * t + P], XW[:, BT * g + t, 0:D], ident)
            last.then_inc(ln_transposed, 1)

        lg = sb("lg", [P, 10, T, E])
        (LOG, OH1, OH2, T0, T1, SLOT, C0, C1) = (lg[:, i] for i in range(8))
        OH12, T01 = lg[:, 1:3], lg[:, 3:5]
        OHS = sb("OHS", [P, T, E], bf16)[:, :, :]
        rt = sb("rt", [P, 8, T])
        ex = sb("ex", [P, 3, E])
        slots_i = sb("slots_i", [P, 3, 2 * T], i32)
        ee = sb("ee", [P, E, E])
        OHLO = SCR[:, 0:4096].rearrange("p (c n) -> p c n", n=P)
        RHS = SCR[:, 4096:4096 + 3840].rearrange("p (c k n) -> p c k n", c=2 * T, k=3)
        tmap = sb("tmap", [P, N_SLOT_TILES, E])
        tsel = sb("tsel", [P, N_SLOT_TILES, E])
        te = sb("te", [P, N_SLOT_TILES])
        te_off = sb("te_off", [P, N_SLOT_TILES], i32)
        tok = sb("tok", [P, 3, N_SLOT_TILES])
        occ_tok = sb("occ_tok", [P, 3, N_SLOT_TILES])
        gidx = sb("gidx", [P, N_SLOT_TILES], i32)
        sidx = sb("sidx", [P, N_SLOT_TILES], i32)
        gcur = [sb(f"gcur{i}", [P, 1], i32) for i in range(2)]
        scur = [sb(f"scur{i}", [P, 1], i32) for i in range(2)]
        G = [sb(f"G{i}", [P, ROW]) for i in range(4)]
        xt = [sb(f"xt{i}", [P, P]) for i in range(2)]
        hs = [sb(f"hs{i}", [P, HID]) for i in range(2)]
        ht = [sb(f"ht{i}", [P, HID]) for i in range(2)]
        y_free = sb("y_free", [1, 1])
        wsel = [sb(f"wsel{i}", [P, E]) for i in range(2)]
        wslot = [sb(f"wslot{i}", [P, 1]) for i in range(4)]
        ytile = [sb(f"ytile{i}", [P, D]) for i in range(2)]
        zrow = sb("zrow", [P, 1, D])
        Y0 = SCR[:, 0:4096].bitcast(f32).rearrange("p (t d) -> p t d", d=D)
        Y1 = SCR[:, 4096:8192].bitcast(f32).rearrange("p (t d) -> p t d", d=D)

        def ffn_sems(f):
            names = ("onehots oh_tile oh_place xn_stored y_init gath0 gath1 gath2 gath3 gcopied xT xt gate up silu "
                     "h hT ht down wsel y scat0 scat1 scopied y_loaded0 y_loaded1 y_loaded2 y_loaded3 out_sum")
            return {**{n: sem(f"f{f}_{n}") for n in names.split()}, **ROUTE_SEMS}

        ROUTE_SEMS = {n: sem(n) for n in ("logits", "exp_arg", "pair_exp", "w1", "comb", "ohs", "totals", "prefix",
                                          "tokens", "gidx", "idx", "toff")}
        FS = [ffn_sems(0), ffn_sems(1)]
        DEPTH_SCALE = 12.0 ** -0.5
        NCH = 4

        def route_vector(dve, link, f):
            s = FS[f]
            m1, m2, k1, k2, dlt, w1, w2, ew = (rt[:, i, :] for i in range(8))

            def bt(a):
                return a.unsqueeze(2).to_broadcast([P, T, E])

            def be(a):
                return a.unsqueeze(1).to_broadcast([P, T, E])
            dve.wait_ge(s["logits"], f + 1)
            nc.vector.memset(y_free[:, :], 0.0).then_inc(s["y"], 1)
            link(nc.vector.tensor_copy(LOG, PS[:, 2, 0:T * E].rearrange("p (t e) -> p t e", e=E)))
            link(nc.vector.reduce_max(m1, LOG, AX.X))
            link(nc.vector.tensor_tensor(T0, LOG, bt(m1), ALU.is_ge))
            link(nc.vector.tensor_tensor(T0, T0, be(rev), ALU.mult))
            link(nc.vector.reduce_max(k1, T0, AX.X))
            link(nc.vector.tensor_tensor(OH1, be(rev), bt(k1), ALU.is_equal))
            link(nc.vector.scalar_tensor_tensor(T1, OH1, NEG, LOG, ALU.mult, ALU.add))
            link(nc.vector.reduce_max(m2, T1, AX.X))
            nc.vector.tensor_tensor(dlt, m2, m1, ALU.subtract).then_inc(s["exp_arg"], 1)
            link(nc.vector.tensor_tensor(T0, T1, bt(m2), ALU.is_ge))
            link(nc.vector.tensor_tensor(T0, T0, be(rev), ALU.mult))
            link(nc.vector.reduce_max(k2, T0, AX.X))
            link(nc.vector.tensor_tensor(OH2, be(rev), bt(k2), ALU.is_equal))
            nc.vector.tensor_tensor(OHS, OH1, OH2, ALU.add).then_inc(s["ohs"], 1)
            dve.wait_ge(s["pair_exp"], f + 1)
            link(nc.vector.tensor_scalar(w1, ew, 1.0, None, ALU.add))
            nc.vector.reciprocal(w1, w1).then_inc(s["w1"], 1)
            nt, base, end = (ex[:, i, :] for i in range(3))
            starts = T0.rearrange("p t e -> p (t e)").rearrange("p (e j) -> p e j", e=E)
            dve.wait_ge(s["totals"], f + 1)
            link(nc.vector.tensor_tensor(starts, PS[:, 4, 0:E].unsqueeze(2).to_broadcast([P, E, T]),
                                         tile_starts.unsqueeze(1).to_broadcast([P, E, T]), ALU.is_gt))
            link(nc.vector.reduce_sum(nt, starts, AX.X))
            link(nc.vector.tensor_tensor(ee[:, :, :], nt.unsqueeze(1).to_broadcast([P, E, E]), slots_before, ALU.mult))
            link(nc.vector.reduce_sum(base, ee[:, :, :], AX.X))
            dve.wait_ge(s["prefix"], f + 1)
            link(nc.vector.tensor_tensor(SLOT, PS[:, 3, 0:T * E].rearrange("p (t e) -> p t e", e=E), be(base), ALU.add))
            link(nc.vector.tensor_tensor(T01, OH12, SLOT.unsqueeze(1).to_broadcast([P, 2, T, E]), ALU.mult))
            si, hi_i, lo_i = (slots_i[:, i, :] for i in range(3))
            link(nc.vector.reduce_max(si.rearrange("p (c t) -> p c t", c=2), T01, AX.X))
            nc.vector.tensor_scalar(hi_i, si, 7, None, ALU.logical_shift_right)
            link(nc.vector.tensor_scalar(lo_i, si, P - 1, None, ALU.bitwise_and))
            C = 2 * T // NCH
            for c in range(NCH):
                cs = slice(C * c, C * c + C)
                nc.vector.tensor_tensor(RHS[:, cs, 0, :], iota40.unsqueeze(1).to_broadcast([P, C, N_SLOT_TILES]),
                                        hi_i[:, cs].unsqueeze(2).to_broadcast([P, C, N_SLOT_TILES]),
                                        ALU.is_equal).then_inc(s["onehots"], 1)
                nc.vector.tensor_tensor(OHLO[:, cs, :], iota128.unsqueeze(1).to_broadcast([P, C, P]),
                                        lo_i[:, cs].unsqueeze(2).to_broadcast([P, C, P]),
                                        ALU.is_equal).then_inc(s["onehots"], 1)
            dve.wait_ge(s["tokens"], f + 1)
            link(nc.vector.tensor_copy(occ_tok[:, :, :].rearrange("p k n -> p (k n)"), PS[:, 5, 0:3 * N_SLOT_TILES]))
            nc.vector.scalar_tensor_tensor(gidx[:, :], occ_tok[:, 1, :], float(P), occ_tok[:, 2, :],
                                           ALU.mult, ALU.add).then_inc(s["gidx"], 1)
            link(nc.vector.tensor_scalar(tok[:, 0, :], occ_tok[:, 0, :], -1.0, 1.0, ALU.mult, ALU.add))
            dve.wait_ge(s["gidx"], f + 1)
            nc.vector.scalar_tensor_tensor(sidx[:, :], tok[:, 0, :], padrow, gidx[:, :],
                                           ALU.mult, ALU.add).then_inc(s["idx"], 1)
            link(nc.vector.tensor_tensor(ee[:, :, :], nt.unsqueeze(1).to_broadcast([P, E, E]), up_to, ALU.mult))
            link(nc.vector.reduce_sum(end, ee[:, :, :], AX.X))
            link(nc.vector.tensor_tensor(tmap[:, :, :], iota40.unsqueeze(2).to_broadcast([P, N_SLOT_TILES, E]),
                                         end.unsqueeze(1).to_broadcast([P, N_SLOT_TILES, E]), ALU.is_ge))
            link(nc.vector.reduce_sum(te[:, :], tmap[:, :, :], AX.X))
            link(nc.vector.tensor_scalar(te[:, :], te[:, :], float(E - 1), None, ALU.min))
            nc.vector.tensor_scalar(te_off[:, :], te[:, :], float(HID), None, ALU.mult).then_inc(s["toff"], 1)
            link(nc.vector.tensor_tensor(tsel[:, :, :], eidx.unsqueeze(1).to_broadcast([P, N_SLOT_TILES, E]),
                                         te[:, :].unsqueeze(2).to_broadcast([P, N_SLOT_TILES, E]), ALU.is_equal))

        def route_pool(pool, link, f):
            s = FS[f]
            w1, w2, ew = (rt[:, i, :] for i in (5, 6, 7))
            pool.wait_ge(s["w1"], f + 1)
            link(nc.gpsimd.tensor_tensor(w2, ew, w1, ALU.mult))
            link(nc.gpsimd.tensor_scalar(rt[:, 5:7, :], rt[:, 5:7, :], DEPTH_SCALE, None, ALU.mult))
            link(nc.gpsimd.tensor_tensor(C0, OH1, w1.unsqueeze(2).to_broadcast([P, T, E]), ALU.mult))
            link(nc.gpsimd.tensor_tensor(C1, OH2, w2.unsqueeze(2).to_broadcast([P, T, E]), ALU.mult))
            nc.gpsimd.tensor_tensor(XW[:, :, D:ROW], C0, C1, ALU.add).then_inc(s["comb"], 1)
            C = 2 * T // NCH
            for c in range(NCH):
                cs = slice(C * c, C * c + C)
                pool.wait_ge(s["onehots"], 2 * c + 1)
                nc.gpsimd.tensor_tensor(RHS[:, cs, 1, :], RHS[:, cs, 0, :],
                                        tcol[:, cs].unsqueeze(2).to_broadcast([P, C, N_SLOT_TILES]),
                                        ALU.mult).then_inc(s["oh_tile"], 1)

        def ffn_tensor(pe, f):
            s = FS[f]
            if f == 0:
                pe.wait_ge(ld_small, 16 * 5)
            for g in range(B + 1):
                if g < B:
                    ln_tensor(pe, 1 + 2 * f, g)
                if g:
                    pe.wait_ge(xnt_ready, 4 * (1 + 2 * f) + g)
                    for t in range(BT * g - BT, BT * g):
                        last = nc.tensor.matmul(PS[:, 2, E * t:E * t + E], XNT[:, P * t:P * t + P], WR[:, :],
                                                start=True, stop=True)
            last.then_inc(s["logits"], 1)
            pe.wait_ge(s["ohs"], f + 1)
            flat = OHS.rearrange("p t e -> p (t e)")
            for t in range(T):
                last = nc.tensor.matmul(PS[:, 4, 0:E], ones_b[:, :], OHS[:, t, :], start=(t == 0), stop=(t == T - 1))
            last.then_inc(s["totals"], 1)
            nc.tensor.matmul(PS[:, 3, 0:T * E], upper_b[:, :], flat, start=True, stop=False, skip_group_check=True)
            for d in range(1, T):
                last = nc.tensor.matmul(PS[:, 3, E * d:T * E], ones_b[:, :], flat[:, 0:(T - d) * E], start=False,
                                        stop=(d == T - 1), skip_group_check=True)
            last.then_inc(s["prefix"], 1)
            for c in range(2 * T):
                if c % (2 * T // NCH) == 0:
                    chunk = c // (2 * T // NCH)
                    pe.wait_ge(s["onehots"], 2 * chunk + 2)
                    pe.wait_ge(s["oh_tile"], chunk + 1)
                    pe.wait_ge(s["oh_place"], chunk + 1)
                last = nc.tensor.matmul(PS[:, 5, 0:3 * N_SLOT_TILES], OHLO[:, c, :],
                                        RHS[:, c].rearrange("p k n -> p (k n)"), start=(c == 0), stop=(c == 2 * T - 1))
            last.then_inc(s["tokens"], 1)
            pe.wait_ge(s["toff"], f + 1)
            if f == 0:
                pe.wait_ge(ld_experts, 16 * 3 * E)
            gath = [s["gath0"], s["gath1"], s["gath2"], s["gath3"]]

            def transpose_x(q, rnd, n):
                pe.wait_ge(gath[q], 16 * (rnd + 1))
                if not isinstance(n, int) or n:
                    pe.wait_ge(s["xt"], n)
                nc.tensor.transpose(PS[:, 0, 0:P], G[q][:, 0:D], ident).then_inc(s["xT"], 1)

            def gate(par, n, off):
                pe.wait_ge(s["xt"], n + 1)
                if not isinstance(n, int) or n:
                    pe.wait_ge(s["silu"], n)
                nc.tensor.matmul(PS[:, 1 + par, :], xt[par][:, :], WG[:, ds(off, HID)],
                                 start=True, stop=True).then_inc(s["gate"], 1)

            def up(par, n, off):
                if not isinstance(n, int) or n:
                    pe.wait_ge(s["h"], n)
                nc.tensor.matmul(PS[:, 3 + par, :], xt[par][:, :], WU[:, ds(off, HID)],
                                 start=True, stop=True).then_inc(s["up"], 1)

            def transpose_h(par, n):
                pe.wait_ge(s["h"], n + 1)
                for j in range(NJ):
                    last = nc.tensor.transpose(PS[:, 5, P * j:P * j + P], hs[par][:, P * j:P * j + P], ident)
                last.then_inc(s["hT"], 1)

            def down(par, n, off):
                pe.wait_ge(s["ht"], n + 1)
                pe.wait_ge(s["y"], n + 1)
                for j in range(NJ):
                    last = nc.tensor.matmul(PS[:, 6, 0:D], ht[par][:, P * j:P * j + P], WD[:, ds(off + P * j, P)],
                                            start=(j == 0), stop=(j == NJ - 1))
                last.then_inc(s["down"], 1)

            def offset(n):
                return pe.value_load(te_off[0:1, n], min_val=0, max_val=HID * (E - 1))

            def tiles(r, ahead=2):
                left = [min(2, 3 - q) if ahead == 0 else 2 for q in range(4)]
                offs = {1: offset(ds(r * 4 + 1, 1))}
                for q in range(4):
                    n, par, nxt = r * 4 + q, q % 2, (q + 1) % 2
                    if left[q] >= 1:
                        gate(nxt, n + 1, offs[q + 1])
                    if q == 0:
                        offs[0] = offset(ds(r * 4, 1))
                    transpose_h(par, n)
                    if left[q] >= 2:
                        transpose_x((q + 2) % 4, r + (q + 2) // 4, n + 2)
                    if left[q] >= 1:
                        up(nxt, n + 1, offs[q + 1])
                    if q < 2 or (q == 2 and ahead):
                        offs[q + 2] = offset(ds(r * 4 + q + 2, 1))
                    down(par, n, offs[q])

            off0 = offset(slice(0, 1))
            transpose_x(0, 0, 0)
            transpose_x(1, 0, 1)
            gate(0, 0, off0)
            up(0, 0, off0)
            with pe.Fori(0, N_SLOT_TILES // 4 - 1) as r:
                tiles(r)
            tiles(N_SLOT_TILES // 4 - 1, ahead=0)

        def ffn_scalar_route(act, f):
            s = FS[f]
            act.wait_ge(s["exp_arg"], f + 1)
            nc.scalar.activation(rt[:, 7, :], rt[:, 4, :], ACT.Exp).then_inc(s["pair_exp"], 1)
            C = 2 * T // NCH
            for c in range(NCH):
                cs = slice(C * c, C * c + C)
                act.wait_ge(s["onehots"], 2 * c + 1)
                nc.scalar.activation(RHS[:, cs, 2, :], RHS[:, cs, 0, :], ACT.Copy, scale=pcol).then_inc(s["oh_place"], 1)

        def ffn_scalar(act, f):
            s = FS[f]

            def xt_copy(par, n):
                act.wait_ge(s["xT"], n + 1)
                nc.scalar.activation(xt[par][:, :], PS[:, 0, 0:P], ACT.Copy).then_inc(s["xt"], 1)

            def silu(par, n):
                act.wait_ge(s["gate"], n + 1)
                nc.scalar.activation(hs[par][:, :], PS[:, 1 + par, :], ACT.Silu).then_inc(s["silu"], 1)

            def ht_copy(par, n):
                act.wait_ge(s["hT"], n + 1)
                nc.scalar.activation(ht[par][:, :], PS[:, 5, :], ACT.Copy).then_inc(s["ht"], 1)
            def tiles(r, last=False):
                for q in range(2):
                    n = r * 2 + q
                    if not (last and q == 1):
                        silu((q + 1) % 2, n + 1)
                    ht_copy(q, n)
                    if not last:
                        xt_copy(q, n + 2)
            xt_copy(0, 0)
            xt_copy(1, 1)
            silu(0, 0)
            with act.Fori(0, N_SLOT_TILES // 2 - 1) as r:
                tiles(r)
            tiles(N_SLOT_TILES // 2 - 1, last=True)

        def ffn_vector(dve, f):
            s = FS[f]
            gath = [s["gath0"], s["gath1"], s["gath2"], s["gath3"]]

            def hprod(par, n):
                dve.wait_ge(s["silu"], n + 1)
                dve.wait_ge(s["up"], n + 1)
                nc.vector.tensor_tensor(hs[par][:, :], hs[par][:, :], PS[:, 3 + par, :], ALU.mult).then_inc(s["h"], 1)

            def weight(q, rnd, n):
                dve.wait_ge(gath[q], 16 * (rnd + 1))
                nc.vector.tensor_tensor(wsel[q % 2][:, :], G[q][:, D:ROW], tsel[:, ds(n, 1), :].rearrange("p a e -> p (a e)"),
                                        ALU.mult).then_inc(s["wsel"], 1)
                dve.wait_ge(s["wsel"], 2 * n + 1)
                nc.vector.reduce_sum(wslot[q][:, :], wsel[q % 2][:, :], AX.X).then_inc(s["wsel"], 1)

            def result(par, q, n):
                dve.wait_ge(s["down"], n + 1)
                dve.wait_ge(s["wsel"], 2 * n + 2)
                if not isinstance(n, int) or n >= 2:
                    dve.wait_ge([s["scat0"], s["scat1"]][par], (n - par) * 8)
                nc.vector.tensor_scalar(ytile[par][:, :], PS[:, 6, 0:D], wslot[q][:, 0:1], None,
                                        ALU.mult).then_inc(s["y"], 1)

            def tiles(r, last=False):
                for q in range(4):
                    n = r * 4 + q
                    if not (last and q >= 2):
                        weight((q + 2) % 4, r + (q + 2) // 4, n + 2)
                    if not (last and q == 3):
                        hprod((q + 1) % 2, n + 1)
                    result(q % 2, q, n)
            weight(0, 0, 0)
            weight(1, 0, 1)
            hprod(0, 0)
            tiles(0)
            with dve.Fori(1, N_SLOT_TILES // 4 - 1) as r:
                tiles(r)
            tiles(N_SLOT_TILES // 4 - 1, last=True)

        def carry_wait():
            nc.gpsimd.tensor_tensor(carrier[:, :], zeros16[:, 0:1], zeros16[:, 0:1], ALU.add)

        def ffn_pool(pool, f):
            s = FS[f]
            gath = [s["gath0"], s["gath1"], s["gath2"], s["gath3"]]
            scat = [s["scat0"], s["scat1"]]
            pool.wait_ge(s["gidx"], f + 1)
            pool.wait_ge(s["xn_stored"], 16)

            def gather(par, q, rnd, n):
                nc.gpsimd.tensor_copy(gcur[par][:, :], gidx[:, ds(n, 1)]).then_inc(s["gcopied"], 1)
                pool.wait_ge(s["gcopied"], n + 1)
                carry_wait()
                nc.gpsimd.indirect_dma_start(G[q][:, :], None, xn_dram[f],
                                             bass.IndirectOffsetOnAxis(gcur[par][:, 0:1], axis=0),
                                             bounds_check=T * P - 1, oob_is_err=False).then_inc(gath[q], 16)

            def scatter(par, n):
                if not isinstance(n, int) or n >= 2:
                    pool.wait_ge(scat[par], (n - par) * 8)
                nc.gpsimd.tensor_copy(scur[par][:, :], sidx[:, ds(n, 1)]).then_inc(s["scopied"], 1)
                pool.wait_ge(s["scopied"], n + 1)
                pool.wait_ge(s["y"], n + 2)
                carry_wait()
                nc.gpsimd.indirect_dma_start(y_dram[f][par], bass.IndirectOffsetOnAxis(scur[par][:, 0:1], axis=0),
                                             ytile[par][:, :], None, bounds_check=(T + 1) * P - 1, oob_is_err=True,
                                             compute_op=ALU.add).then_inc(scat[par], 16)
            for n in range(4):
                if n >= 2:
                    pool.wait_ge(gath[n - 2], 16)
                gather(n % 2, n, 0, n)

            def tiles(r, last=False):
                for q in range(4):
                    n = r * 4 + q
                    if not last:
                        pool.wait_ge(gath[(q + 2) % 4], 16 * (r + (q + 2) // 4 + 1))
                        pool.wait_ge(s["xT"], n + 1)
                        pool.wait_ge(s["wsel"], 2 * n + 2)
                        gather(q % 2, q, r + 1, n + 4)
                    scatter(q % 2, n)
            pool.wait_ge(s["idx"], f + 1)
            pool.wait_ge(s["y_init"], 48)
            tiles(0)
            with pool.Fori(1, N_SLOT_TILES // 4 - 1) as r:
                tiles(r)
            tiles(N_SLOT_TILES // 4 - 1, last=True)

        def ffn_sync(sp, f):
            s = FS[f]
            sp.wait_ge(ln_done, 4 * (1 + 2 * f) + 4)
            rows = "(t p) d -> p t d"
            sp.dma_start(y_dram[f][0][0:T * P, :].rearrange(rows, p=P), X[:, :, :]).then_inc(s["y_init"], 16)
            sp.wait_ge(s["comb"], f + 1)
            sp.dma_start(xn_dram[f].rearrange(rows, p=P), XW[:, :, :]).then_inc(s["xn_stored"], 16)
            for i in range(2):
                sp.wait_ge(s[f"scat{i}"], 16 * (N_SLOT_TILES // 2))
            for g in range(B):
                for Y, y in ((Y0, y_dram[f][0]), (Y1, y_dram[f][1])):
                    sp.dma_start(Y[:, BT * g:BT * g + BT, :],
                                 y[S * g:S * g + S, :].rearrange(rows, p=P)).then_inc(s[f"y_loaded{g}"], 16)

        def sum_outputs(dve, f, g):
            dve.wait_ge(FS[f][f"y_loaded{g}"], 32)
            gs = slice(BT * g, BT * g + BT)
            nc.vector.tensor_tensor(X[:, gs, :], Y0[:, gs, :], Y1[:, gs, :], ALU.add).then_inc(FS[f]["out_sum"], 1)
            dve.wait_ge(FS[f]["out_sum"], g + 1)

        y_zeroed, out_stored, cchain, rden_ready, ld_pos = (
            sem("y_zeroed"), sem("out_stored"), sem("cchain"), sem("rden_ready"), sem("ld_pos"))
        block = ctx.enter_context(nc.Block())

        RN = SCR[:, 8192:10240].bitcast(f32).rearrange("p (a n) -> p a n", a=2)
        FE = SCR[:, 10240:12288].bitcast(f32).rearrange("p (a n) -> p a n", a=2)
        FQK = SCR[:, 12288:14336].bitcast(f32).rearrange("p (a n) -> p a n", a=2)
        AT = SCR[:, 14336:14336 + 2 * PCOLS].bitcast(f32)
        NT = SCR[:, 16896:16896 + 2 * S].bitcast(f32)
        V1 = sb("V1", [P, 2, BT, P])
        la = {n: sem("la_" + n) for n in ("proj", "vproj", "relu", "exp", "feat", "v", "a", "diag", "rest", "num", "nt",
                                          "fin", "den", "x")}

        def la_tensor(pe):
            def project(b):
                pe.wait_ge(xnt_ready, 8 + b + 1)
                xb = XNT[:, S * b:S * b + S]
                nc.tensor.matmul(PS[:, 2, :], WQ2[:, :, :].rearrange("p i k -> p (i k)"), xb, start=True, stop=True)
                nc.tensor.matmul(PS[:, 3, :], WK2[:, :, :].rearrange("p i k -> p (i k)"), xb, start=True,
                                 stop=True).then_inc(la["proj"], 1)

            def project_values(b):
                if b:
                    pe.wait_ge(la["v"], b)
                for t in range(BT):
                    last = nc.tensor.matmul(PS[:, 0, K2 * t:K2 * t + K2], XNT[:, S * b + P * t:S * b + P * t + P],
                                            WV2[:, :], start=True, stop=True)
                last.then_inc(la["vproj"], 1)

            def scores(b):
                pe.wait_ge(la["feat"], b + 1)
                for kb in range(BT):
                    if b or kb >= 2:
                        pe.wait_ge(la["diag"], BT * b + kb - 1)
                        if kb != 1:
                            pe.wait_ge(la["rest"], 3 * b + max(kb - 1, 0))
                    n = S - P * kb
                    nc.tensor.matmul(PS[:, 4 + kb % 2, 0:n], FQK[:, 1, P * kb:P * kb + P], FQK[:, 0, P * kb:S],
                                     start=True, stop=True).then_inc(la["a"], 1)

            def numerator(b):
                pe.wait_ge(la["v"], b + 1)
                if b:
                    pe.wait_ge(la["nt"], b)
                for kb in range(BT):
                    pe.wait_ge(la["diag"], BT * b + kb + 1)
                    pe.wait_ge(la["rest"], 3 * b + min(kb + 1, 3))
                    last = nc.tensor.matmul(PS[:, 1, P * kb:S], V1[:, b % 2, kb, :], AT[:, SEG[kb]:SEG[kb] + S - P * kb],
                                            start=(kb == 0), stop=(kb == BT - 1), skip_group_check=True)
                last.then_inc(la["num"], 1)

            def output(b):
                pe.wait_ge(la["nt"], b + 1)
                if b:
                    pe.wait_ge(la["x"], b)
                for qb in range(BT):
                    last = nc.tensor.matmul(PS[:, 6 + qb // 2, (D + 1) * (qb % 2):(D + 1) * (qb % 2 + 1)],
                                            NT[:, P * qb:P * qb + P], WO2[:, :], start=True, stop=True)
                last.then_inc(la["fin"], 1)

            ln_tensor(pe, 2, 0)
            ln_tensor(pe, 2, 1)
            project(0)
            ln_tensor(pe, 2, 2)
            ln_tensor(pe, 2, 3)
            pe.wait_ge(xnt_ready, 12)
            project_values(0)
            for b in range(B):
                scores(b)
                if b + 1 < B:
                    project(b + 1)
                if b:
                    output(b - 1)
                if b + 1 < B:
                    project_values(b + 1)
                numerator(b)
            output(B - 1)

        def la_scalar(act):
            def exponential(b):
                act.wait_ge(la["proj"], b + 1)
                nc.scalar.activation(RN, PS[:, 2:4, :], ACT.Relu, scale=-1.0).then_inc(la["relu"], 1)
                act.wait_ge(la["relu"], b + 1)
                nc.scalar.activation(FE, RN, ACT.Exp, scale=-1.0).then_inc(la["exp"], 1)

            def values(b):
                act.wait_ge(la["vproj"], b + 1)
                if b >= 2:
                    act.wait_ge(la["num"], b - 1)
                nc.scalar.activation(V1[:, b % 2, :, 0:K2], PS[:, 0, 0:BT * K2].rearrange("p (t m) -> p t m", m=K2),
                                     ACT.Copy).then_inc(la["v"], 1)

            def scores(b):
                for kb in range(BT - 1):
                    act.wait_ge(la["diag"], BT * b + kb + 1)
                    n = S - P * kb
                    nc.scalar.activation(AT[:, SEG[kb] + P:SEG[kb] + n], PS[:, 4 + kb % 2, P:n],
                                         ACT.Copy).then_inc(la["rest"], 1)

            exponential(0)
            ln_scalar_copy(act, 2, B - 1)
            values(0)
            for b in range(B):
                scores(b)
                if b + 1 < B:
                    exponential(b + 1)
                    values(b + 1)
                act.wait_ge(la["num"], b + 1)
                if b:
                    act.wait_ge(la["fin"], b)
                nc.scalar.activation(NT, PS[:, 1, :], ACT.Copy).then_inc(la["nt"], 1)

        def la_vector(dve, link):
            def features(b):
                dve.wait_ge(la["exp"], b + 1)
                nc.vector.scalar_tensor_tensor(FQK.rearrange("p a n -> p (a n)"),
                                               PS[:, 2:4, :].rearrange("p a n -> p (a n)"), 0.0,
                                               FE.rearrange("p a n -> p (a n)"), ALU.max,
                                               ALU.add).then_inc(la["feat"], 1)

            def output(b):
                dve.wait_ge(la["fin"], b + 1)
                o = PS[:, 6:8, 0:2 * (D + 1)].rearrange("p k (i n) -> p k i n", i=2)
                den = stat[:, 2, 0:BT].rearrange("p (k i) -> p k i", k=2)
                nc.vector.tensor_scalar(den, o[:, :, :, D], 2e-6, None, ALU.add).then_inc(la["den"], 1)
                dve.wait_ge(la["den"], 2 * b + 1)
                nc.vector.reciprocal(den, den).then_inc(la["den"], 1)
                dve.wait_ge(la["den"], 2 * b + 2)
                for qb in range(BT):
                    x_rows = X[:, BT * b + qb, :]
                    last = nc.vector.scalar_tensor_tensor(x_rows, o[:, qb // 2, qb % 2, 0:D], stat[:, 2, qb:qb + 1],
                                                          x_rows, ALU.mult, ALU.add)
                last.then_inc(la["x"], 1)

            def stats(b):
                dve.wait_ge(la["x"], b + 1)
                ln_stats(dve, link, 3, b)

            features(0)
            for b in range(B):
                if b:
                    dve.wait_ge(la["num"], b)
                for kb in range(BT):
                    dve.wait_ge(la["a"], BT * b + kb + 1)
                    nc.vector.tensor_tensor(AT[:, SEG[kb]:SEG[kb] + P], PS[:, 4 + kb % 2, 0:P], causal1,
                                            ALU.mult).then_inc(la["diag"], 1)
                if b:
                    output(b - 1)
                if b + 1 < B:
                    features(b + 1)
                if b:
                    stats(b - 1)
            output(B - 1)
            stats(B - 1)

        @block.sync
        def _(sp):
            for g in range(B):
                sp.dma_start(X[:, BT * g:BT * g + BT, :],
                             x[g].rearrange("(t p) d -> p t d", p=P)).then_inc(ld_x[g], 16)
            sp.dma_start(CON[:, :], consts[:, :]).then_inc(ld_const, 16)
            sp.dma_start(WQK[:, :], wqk).then_inc(ld_wqkv, 16)
            sp.dma_start(WV[:, :], wv).then_inc(ld_wqkv, 16)
            sp.wait_ge(slopes_spread, NPART)
            sp.wait_ge(bias_built, 5)
            for side in range(2):
                view = bias_dram[side].rearrange("r h t -> h r t")
                for k in range(2):
                    m_row, p_row = NPART * (k + 2 * side), NPART * (k + 2 - 2 * side)
                    m0 = 2 + NPART * side
                    sp.dma_start(view[:, m_row:m_row + NPART, :], BIAS[:, m0:m0 + NPART, :]).then_inc(bias_stored, 16)
                    sp.dma_start(view[:, p_row:p_row + NPART, :],
                                 BIAS[:, k:k + 1, :].to_broadcast([H, NPART, S])).then_inc(bias_stored, 16)
                sp.dma_start(view[:, 4 * NPART:PROD0, :],
                             BIAS[:, 8:9, :].to_broadcast([H, PROD0 - 4 * NPART, S])).then_inc(bias_stored, 16)
            sp.wait_ge(bias_stored, 16 * 10)
            for hg in range(HG):
                for side, A in enumerate((QA, KA)):
                    loaded = crows_loaded[hg] if side == 0 and hg < 2 else bias_loaded
                    sp.dma_start(A[hg][0:PROD0, :].rearrange("r (h t) -> r h t", h=GH),
                                 bias_dram[side, :, GH * hg:GH * hg + GH, :]).then_inc(loaded, 16)

            def load_operands(b, hg):
                cols = slice(UC * hg, UC * hg + UC)
                b1 = ds(b, 1)
                for i in range(NPART):
                    r0 = PROD0 + NPART * HD * i
                    sp.dma_start(QA[hg][r0:r0 + NPART * HD, :],
                                 rows_dram[b1, 0, i, :, cols].to_broadcast([NPART, HD, UC])).then_inc(qk_loaded[hg], 16)
                sp.dma_start(KA[hg][PROD0:KROWS, :],
                             rows_dram[b1, 1, :, :, cols].rearrange("o i d n -> o (i d) n")
                             .to_broadcast([NPART, NPART * HD, UC])).then_inc(qk_loaded[hg], 16)

            for g in range(B):
                sp.wait_ge(part3, g + 1)
                for a in range(2):
                    sp.dma_start(parts_dram[g, a].rearrange("i p t -> p i t"),
                                 QKP[g][:, :, a, :]).then_inc(parts_stored[g], 16)
                if g == 0:
                    sp.wait_ge(parts_stored[0], 32)
                    for hg in range(3):
                        load_operands(0, hg)
            for g in range(1, B):
                sp.wait_ge(parts_stored[g], 32)
            for w, d in ((WQ2, wq2), (WK2, wk2)):
                sp.dma_start(w[:, :, :], d.unsqueeze(1).to_broadcast([P, 2, K2])).then_inc(ld_small, 16)
            for w, d in ((WV2, wv2), (WR, wr)):
                sp.dma_start(w[:, :], d).then_inc(ld_small, 16)
            sp.wait_ge(vu_cleared, 1)
            sp.dma_start(WO2[0:K2, 0:D], wo2).then_inc(ld_small, 16)
            sp.wait_ge(y_zeroed, 1)
            for f in range(2):
                sp.dma_start(y_dram[f][1].rearrange("(t p) d -> p t d", p=P), zrow[:, :, :].to_broadcast([P, T + 1, D])).then_inc(FS[f]["y_init"], 16)
                sp.dma_start(y_dram[f][0][T * P:(T + 1) * P, :], zrow[:, 0, :]).then_inc(FS[f]["y_init"], 16)

            def load_max(u, hg):
                sp.wait_ge(cparts_ready, u + 1)
                for i in range(NPART):
                    sp.dma_start(QA[hg][KROWS + i:KROWS + i + 1, :].rearrange("o (k t) -> o k t", t=P),
                                 cparts[hg % 2][:, i, :]).then_inc(crows_loaded[hg % 2], 16)

            def load_expert_part(b, j):
                e = b * 2 + j // 2
                cols = ds(e * HID, HID)
                if j % 2 == 0:
                    for W, w in ((WG, wg), (WU, wu)):
                        sp.dma_start(W[:, cols], w[ds(e, 1)].rearrange("o p c -> (o p) c")).then_inc(ld_experts, 16)
                else:
                    sp.dma_start(WD[:, cols].rearrange("p (j c) -> p j c", j=NJ),
                                 wd[ds(e, 1)].rearrange("o (j p) c -> p (o j) c", p=P)).then_inc(ld_experts, 16)

            load_max(0, 0)
            with sp.Fori(0, B - 1) as b:
                for j in range(HG):
                    u = b * HG + j
                    sp.wait_ge(exp_done, NX * u + 2)
                    load_operands(b + (j + 3) // HG, (j + 3) % HG)
                    load_max(u + 1, (j + 1) % HG)
                    load_expert_part(b, j)
            b = B - 1
            for j in range(HG):
                u = b * HG + j
                if j == 0:
                    sp.wait_ge(exp_done, NX * u + 2)
                    load_operands(b, 3)
                if j < 3:
                    load_max(u + 1, j + 1)
                load_expert_part(b, j)
            ffn_sync(sp, 0)
            ffn_sync(sp, 1)
            for g in range(B):
                sp.wait_ge(FS[1]["out_sum"], g + 1)
                sp.dma_start(out[g].rearrange("(t p) d -> p t d", p=P), X[:, BT * g:BT * g + BT, :]).then_inc(out_stored, 16)
            sp.wait_ge(out_stored, 16 * B)

        @block.gpsimd
        def _(pool):
            count = [0]

            def link(ins):
                count[0] += 1
                ins.then_inc(pool_chain, 1)
                pool.wait_ge(pool_chain, count[0])
            pool.dma_start(POS, pos_in).then_inc(ld_pos, 16)
            pool.dma_start(slope[:, :], slopes).then_inc(ld_pos, 16)
            pool.wait_ge(ld_pos, 32)
            link(nc.gpsimd.tensor_copy(slope_pb[:, 0:1], slope[:, :]))
            link(nc.gpsimd.tensor_tensor(slope_r[:, 0:1], slope[:, :], slope_pb[:, 0:1], ALU.subtract))
            link(nc.gpsimd.tensor_copy(slope_pb[:, 1:2], slope_r[:, 0:1]))
            link(nc.gpsimd.tensor_tensor(slope_r[:, 1:2], slope_r[:, 0:1], slope_pb[:, 1:2], ALU.subtract))
            link(nc.gpsimd.tensor_copy(slope_pb[:, 2:3], slope_r[:, 1:2]))
            nc.gpsimd.tensor_copy(slope_p[:, :], slope_pb[:, :]).then_inc(slope_split, 1)
            pos = POS.rearrange("h (k t) -> h k t", k=2)
            nc.gpsimd.tensor_copy(BIAS[:, 0:2, :], pos).then_inc(bias_built, 1)
            nc.gpsimd.memset(BIAS[:, 8, :].bitcast(f32), 0.0).then_inc(bias_built, 1)
            nc.gpsimd.memset(zeros16[:, :], 0.0)
            pool.wait_ge(ld_wqkv, 32)
            nc.gpsimd.tensor_scalar(WQK[:, 0:D], WQK[:, 0:D], float(D) ** -0.5, None, ALU.mult).then_inc(wq_scaled, 1)
            pool.wait_ge(wq_scaled, 1)
            for hg in range(HG):
                nc.gpsimd.memset(KA[hg][KROWS:MROWS, :], 1.0).then_inc(k_ones, 1)
            pool.wait_ge(k_ones, HG)
            for i in range(2):
                link(nc.gpsimd.memset(VU[i][:, :, :, :], 0.0))
                link(nc.gpsimd.memset(VU[i][:, :, :, HD:HD + 1], 1.0))
            link(nc.gpsimd.memset(WO2[:, :], 0.0))
            link(nc.gpsimd.memset(WO2[K2:K2 + 1, D:D + 1], 1.0))
            link(nc.gpsimd.memset(V1[:, :, :, :], 0.0))
            link(nc.gpsimd.memset(V1[:, :, :, K2:K2 + 1], 1.0))
            nc.gpsimd.memset(zrow[:, :, :], 0.0).then_inc(y_zeroed, 1)
            nc.gpsimd.memset(tok[:, :, :], 0.0).then_inc(vu_cleared, 1)

            def split_max(u, par):
                pool.wait_ge(negc_ready, u + 1)
                if not isinstance(u, int) or u >= 2:
                    pool.wait_ge(crows_loaded[par], 24 * (u - par) + 16)
                nc.gpsimd.tensor_tensor(cparts[par][:, 0, :], negc[par][:, :], zeros16[:, :],
                                        ALU.subtract).then_inc(cchain, 1)
                pool.wait_ge(cchain, 3 * u + 1)
                nc.gpsimd.tensor_tensor(negr[:, 0, :], negc[par][:, :], cparts[par][:, 0, :],
                                        ALU.subtract).then_inc(cchain, 1)
                pool.wait_ge(cchain, 3 * u + 2)
                nc.gpsimd.tensor_tensor(cparts[par][:, 1, :], negr[:, 0, :], zeros16[:, :],
                                        ALU.subtract).then_inc(cchain, 1)
                pool.wait_ge(cchain, 3 * u + 3)
                nc.gpsimd.tensor_tensor(cparts[par][:, 2, :], negr[:, 0, :], cparts[par][:, 1, :],
                                        ALU.subtract).then_inc(cparts_ready, 1)

            def unit_values(u, par, b, hg):
                pool.wait_ge(pv_done, u + 1)
                nc.gpsimd.tensor_copy(VU[par][:, :, :, 0:HD],
                                      V[:, ds(b * BT, BT), 32 * hg:32 * hg + 32]
                                      .rearrange("p t (a d) -> p t a d", a=GH)).then_inc(vu_ready, 1)

            def add_unit(u, par, b, hg):
                pool.wait_ge(normed, u + 2)
                xs = X[:, ds(b * BT, BT), 32 * hg:32 * hg + 32].rearrange("p t (a d) -> p t a d", a=GH)
                nc.gpsimd.tensor_tensor(xs, xs, NRM[par][:, :, :, :], ALU.add).then_inc(x_added, 1)

            def step(u, batch, hg, previous_batch, last=False):
                if not last:
                    split_max(u + 1, (hg + 1) % 2)
                unit_values(u, hg % 2, batch, hg)
                if previous_batch is not None:
                    add_unit(u - 1, (hg + 1) % 2, previous_batch, (hg + 3) % HG)

            nc.gpsimd.memset(gcur[0][:, :], 0).then_inc(x_added, 1)
            nc.gpsimd.memset(gcur[1][:, :], 0).then_inc(x_added, 1)
            pool.wait_ge(v_copied, B)
            split_max(0, 0)
            step(0, 0, 0, None)
            with pool.Fori(0, B - 1) as b:
                for j in range(1, HG + 1):
                    step(b * HG + j, b + j // HG, j % HG, b)
            for u in range(U - 3, U):
                step(u, B - 1, u % HG, B - 1, last=(u == U - 1))
            add_unit(U - 1, 1, B - 1, HG - 1)
            for f in range(2):
                route_pool(pool, link, f)
                ffn_pool(pool, f)

        @block.scalar
        def _(act):
            act.wait_ge(slope_split, 1)
            pos_lo = POS[:, 0:S]
            for i in range(NPART):
                nc.scalar.activation(BIAS[:, 2 + i, :], pos_lo, ACT.Identity, bias=slope_p[:, i:i + 1],
                                     scale=0.0).then_inc(slopes_spread, 1)
            act.wait_ge(slopes_spread, NPART)
            for i in range(NPART):
                nc.scalar.activation(BIAS[:, 5 + i, :], BIAS[:, 2 + i, :], ACT.Copy,
                                     scale=-1.0).then_inc(bias_built, 1)
            act.wait_ge(eps_ready, 1)
            for g in range(B):
                ln_scalar_std(act, 0, g)
            def first_part(g):
                act.wait_ge(qk_proj, g + 1)
                nc.scalar.activation(QKP[g][:, 0], PS[:, 2 + 2 * (g % 2):4 + 2 * (g % 2), :], ACT.Copy).then_inc(part1, 1)

            ln_scalar_copy(act, 0, 0)
            ln_scalar_copy(act, 0, 1)
            first_part(0)
            for g in range(B):
                if g + 2 < B:
                    ln_scalar_copy(act, 0, g + 2)
                if g + 1 < B:
                    first_part(g + 1)
                act.wait_ge(rest1, g + 1)
                nc.scalar.activation(QKP[g][:, 1], QKR[g % 2], ACT.Copy).then_inc(part2, 1)

            def step(u, par, first=False):
                act.wait_ge(pv_done, u + 1)
                for k, (a0, na, per, kb) in enumerate(XGROUPS):
                    n = S - P * kb
                    act.wait_ge(st_ready, NX * u + k + 1)
                    bank = 2 + 2 * (k % 2)
                    nb = na // per
                    src = (PS[:, bank, 0:na * n].rearrange("p (a n) -> p a n", a=na) if nb == 1 else
                           PS[:, bank:bank + nb, 0:per * n] if per == 1 else
                           PS[:, bank:bank + nb, :].rearrange("p k (a n) -> p (k a) n", a=per))
                    nc.scalar.activation(PT[par][:, a0:a0 + na, SEG[kb]:SEG[kb] + n], src,
                                         ACT.Exp).then_inc(exp_done, 1)
                    if k == 3 and not first:
                        evacuate(u - 1)

            def evacuate(u):
                act.wait_ge(pv_done, u + 3)
                act.wait_ge(to_ready, u + 1)
                nc.scalar.activation(OT[:, :], PS[:, 6, :], ACT.Copy).then_inc(ot_ready, 1)

            step(0, 0, first=True)
            with act.Fori(0, B - 1) as b:
                for j in range(1, HG + 1):
                    step(b * HG + j, j % 2)
            for u in range(U - 3, U):
                step(u, u % 2)
            for g in range(B - 1):
                ln_scalar_std(act, 1, g)
            evacuate(U - 1)
            for g in range(B - 1):
                ln_scalar_copy(act, 1, g)
            ln_scalar_std(act, 1, B - 1)
            ln_scalar_copy(act, 1, B - 1)
            ffn_scalar_route(act, 0)
            ffn_scalar(act, 0)
            for g in range(B):
                ln_scalar_std(act, 2, g)
                if g:
                    ln_scalar_copy(act, 2, g - 1)
            la_scalar(act)
            for g in range(B):
                ln_scalar_std(act, 3, g)
            for g in range(B):
                ln_scalar_copy(act, 3, g)
            ffn_scalar_route(act, 1)
            ffn_scalar(act, 1)

        @block.tensor
        def _(pe):
            pe.wait_ge(ld_const, 16)
            for g in range(B):
                ln_tensor(pe, 0, g)
            pe.wait_ge(wq_scaled, 1)
            for g in range(B):
                pe.wait_ge(xnt_ready, g + 1)
                if g >= 2:
                    pe.wait_ge(rest1, g - 1)
                xg = XNT[:, S * g:S * g + S]
                nc.tensor.matmul(PS[:, 2 + 2 * (g % 2), :], WQK[:, 0:D], xg, start=True, stop=True)
                nc.tensor.matmul(PS[:, 3 + 2 * (g % 2), :], WQK[:, D:2 * D], xg, start=True, stop=True).then_inc(qk_proj, 1)
                if g >= 2:
                    pe.wait_ge(v_copied, g - 1)
                for t in range(BT):
                    last = nc.tensor.matmul(PS[:, 6 + g % 2, P * t:P * t + P], XNT[:, S * g + P * t:S * g + P * t + P],
                                            WV[:, :], start=True, stop=True)
                last.then_inc(v_proj, 1)
            pe.wait_ge(consts_cast, 1)

            def max_bank(u, hg, k, index, first):
                a0, na, i = MBANKS[k]
                n = P * (i + 1)
                bank = (NM * hg + k) % 2
                if not (first and index < 2):
                    pe.wait_ge(max_used, index - 1)
                for a in range(a0, a0 + na):
                    seg = PS[:, bank, (a - a0) * n:(a - a0) * n + n]
                    nc.tensor.matmul(seg, QA[hg][0:KROWS, S * a + P * i:S * a + P * i + P],
                                     KA[hg][0:KROWS, S * a:S * a + n], start=(a == a0), stop=False,
                                     skip_group_check=True)
                diag = PS[:, bank, 0:na * n].rearrange("p (a n) -> p a n", a=na)[:, :, n - P:n]
                nc.tensor.matmul(diag, ident_b[:, :], mask_qk4[:, 0:na, :], start=False, stop=True,
                                 skip_group_check=True).then_inc(max_ready, 1)

            def transpose_max(u, par):
                pe.wait_ge(max_used, NM * (u + 1))
                if not isinstance(u, int) or u:
                    pe.wait_ge(negc_ready, u)
                if not isinstance(u, int) or u >= 2:
                    pe.wait_ge(normed, u - 1)
                nc.tensor.transpose(PS[0:GH * BT, 7, 0:P], cmax[par][:, :, :].rearrange("p a i -> p (a i)"),
                                    ident).then_inc(cmax_transposed, 1)

            def scores_t(u, hg, k):
                a0, na, per, kb = XGROUPS[k]
                n = S - P * kb
                pe.wait_ge(exp_done, NX * u + k + 1)
                for a in range(a0, a0 + na):
                    bank = 2 + 2 * (k % 2) + (a - a0) // per
                    c = (a - a0) % per * n
                    nc.tensor.matmul(PS[:, bank, c:c + n], KA[hg][0:MROWS, S * a + P * kb:S * a + P * kb + P],
                                     QA[hg][0:MROWS, S * a + P * kb:S * a + S], start=(c == 0), stop=False,
                                     skip_group_check=True)
                for bk in range(na // per):
                    bank = 2 + 2 * (k % 2) + bk
                    diag = PS[:, bank, 0:per * n].rearrange("p (a n) -> p a n", a=per)[:, :, 0:P]
                    last = nc.tensor.matmul(diag, ident_b[:, :], mask_kq[:, 0:per, :], start=False, stop=True,
                                            skip_group_check=True)
                last.then_inc(st_ready, 1)

            def values(u, par, kb):
                pe.wait_ge(exp_done, NX * u + GROUPS_OF_KB[kb] + 2)
                if kb == 0:
                    pe.wait_ge(vu_ready, u + 1)
                    pe.wait_ge(ot_ready, u + 1)
                for a in range(GH):
                    last = nc.tensor.matmul(PS[32 * a:32 * a + 32, 6, P * kb:S], VU[par][:, kb, a, :],
                                            PT[par][:, a, SEG[kb]:SEG[kb] + S - P * kb],
                                            start=(kb == 0), stop=(kb == BT - 1), skip_group_check=True)
                if kb == BT - 1:
                    last.then_inc(pv_done, 1)

            def transpose_out(u):
                pe.wait_ge(ot_ready, u + 2)
                for t in range(BT):
                    last = nc.tensor.transpose(PS[:, 7, P * t:P * t + P], OT[:, P * t:P * t + P], ident)
                last.then_inc(to_ready, 1)

            def step(u, batch, hg, lookahead=2, first=False):
                def maximum(*ks):
                    if lookahead == 2:
                        for k in ks:
                            max_bank(u + 2, (hg + 2) % HG, k, NM * (u + 2) + k, False)

                def previous(kb):
                    if not first:
                        values(u - 1, (hg + 1) % 2, kb)
                if lookahead == 2:
                    pe.wait_ge(qk_loaded[(hg + 2) % HG], 64 * (batch + (hg + 2) // HG + 1))
                maximum(0, 1)
                if lookahead >= 1:
                    transpose_max(u + 1, (hg + 1) % 2)
                pe.wait_ge(crows_loaded[hg % 2], 24 * (u - hg % 2) + 64)
                scores_t(u, hg, 0)
                maximum(2)
                scores_t(u, hg, 1)
                maximum(3)
                previous(0)
                maximum(4)
                scores_t(u, hg, 2)
                maximum(5)
                previous(1)
                maximum(6)
                scores_t(u, hg, 3)
                maximum(7)
                previous(2)
                previous(3)
                maximum(8)
                scores_t(u, hg, 4)
                maximum(9)
                scores_t(u, hg, 5)
                maximum(10)
                if not first:
                    if lookahead >= 1:
                        pe.wait_ge(negc_ready, u + 2)
                    else:
                        pe.wait_ge(normed, u)
                    transpose_out(u - 1)

            pe.wait_ge(bias_loaded, 6 * 16)
            pe.wait_ge(k_ones, HG)
            for i in range(2):
                pe.wait_ge(crows_loaded[i], 16)
            pe.wait_ge(exp_done, 2)
            for u in range(2):
                pe.wait_ge(qk_loaded[u], 64)
                for k in range(NM):
                    max_bank(u, u, k, NM * u + k, True)
                if u == 0:
                    transpose_max(0, 0)
            step(0, 0, 0, first=True)
            with pe.Fori(0, B - 1) as b:
                for j in range(1, HG + 1):
                    step(b * HG + j, b + j // HG, j % HG)
            for u in range(U - 3, U):
                step(u, B - 1, u % HG, lookahead=min(2, U - 1 - u))
            for kb in range(BT):
                values(U - 1, 1, kb)
            pe.wait_ge(normed, U)
            transpose_out(U - 1)
            for f in range(2):
                ffn_tensor(pe, f)
                if f == 0:
                    la_tensor(pe)

        @block.vector
        def _(dve):
            count = [0]

            def link(ins):
                count[0] += 1
                ins.then_inc(dve_chain, 1)
                dve.wait_ge(dve_chain, count[0])
            nc.vector.memset(eps[:, :], EPS).then_inc(eps_ready, 1)
            for g in range(B):
                dve.wait_ge(ld_x[g], 16)
                ln_stats(dve, link, 0, g)
            for g in range(B):
                ln_scale(dve, link, 0, g)
            dve.wait_ge(ld_const, 16)
            nc.vector.memset(ones_b[:, :], 1.0).then_inc(exp_done, 2)
            nc.vector.tensor_copy(upper_b[:, :], upper1)
            nc.vector.tensor_copy(ident_b[:, :], ident).then_inc(pv_done, 2)
            for a in range(GH):
                nc.vector.tensor_scalar(mask_kq[:, a, :], causal1, -NEG, NEG, ALU.mult, ALU.add)
            for a in range(GH):
                nc.vector.tensor_scalar(mask_qk4[:, a, :], upper1, NEG, None,
                                        ALU.mult).then_inc((normed, ot_ready, to_ready, consts_cast)[a], 1)
            for g in range(B):
                dve.wait_ge(part1, g + 1)
                if g >= 2:
                    dve.wait_ge(part2, g - 1)
                nc.vector.tensor_tensor(QKR[g % 2], PS[:, 2 + 2 * (g % 2):4 + 2 * (g % 2), :], QKP[g][:, 0],
                                        ALU.subtract).then_inc(rest1, 1)
                dve.wait_ge(v_proj, g + 1)
                nc.vector.tensor_copy(V[:, BT * g:BT * g + BT, :],
                                      PS[:, 6 + g % 2, :].rearrange("p (t n) -> p t n", t=BT)).then_inc(v_copied, 1)
                dve.wait_ge(part2, g + 1)
                nc.vector.tensor_tensor(QKP[g][:, 2], QKR[g % 2], QKP[g][:, 1], ALU.subtract).then_inc(part3, 1)

            def reduce(u, hg, k, index):
                a0, na, i = MBANKS[k]
                n = P * (i + 1)
                dve.wait_ge(max_ready, index + 1)
                nc.vector.reduce_max(cmax[hg % 2][:, a0:a0 + na, i],
                                     PS[:, (NM * hg + k) % 2, 0:na * n].rearrange("p (a n) -> p a n", a=na),
                                     AX.X).then_inc(max_used, 1)

            def negate(u, par):
                dve.wait_ge(cmax_transposed, u + 1)
                if not isinstance(u, int) or u:
                    dve.wait_ge(cparts_ready, u)
                nc.vector.tensor_scalar(negc[par][:, :], PS[0:GH * BT, 7, 0:P], -1.0, None,
                                        ALU.mult).then_inc(negc_ready, 1)

            def normalise(u, par):
                dve.wait_ge(to_ready, u + 2)
                o = PS[:, 7, :].rearrange("p (t a m) -> p t a m", t=BT, a=GH)
                nc.vector.reciprocal(rden[:, :, :], o[:, :, :, HD]).then_inc(rden_ready, 1)
                dve.wait_ge(rden_ready, u + 1)
                dve.wait_ge(x_added, u + 1)
                nc.vector.tensor_tensor(NRM[par][:, :, :, :].rearrange("p t a d -> p (t a) d"),
                                        PS[:, 7, :].rearrange("p (g m) -> p g m", m=32)[:, :, 0:HD],
                                        rden[:, :, :].rearrange("p t a -> p (t a)").unsqueeze(2)
                                        .to_broadcast([P, BT * GH, HD]), ALU.mult).then_inc(normed, 1)

            def step(u, hg, lookahead=2, first=False):
                for k in range(NM):
                    if lookahead == 2:
                        reduce(u + 2, (hg + 2) % HG, k, NM * (u + 2) + k)
                    if k == 1 and lookahead >= 1:
                        negate(u + 1, (hg + 1) % 2)
                if not first:
                    normalise(u - 1, (hg + 1) % 2)

            for u in range(2):
                for k in range(NM):
                    reduce(u, u, k, NM * u + k)
                if u == 0:
                    negate(0, 0)
            step(0, 0, first=True)
            with dve.Fori(0, B - 1) as b:
                for j in range(1, HG + 1):
                    step(b * HG + j, j % HG)
            step(U - 3, 1)
            step(U - 2, 2, lookahead=1)
            for g in range(B - 1):
                dve.wait_ge(x_added, 2 + HG * (g + 1))
                ln_stats(dve, link, 1, g)
            step(U - 1, 3, lookahead=0)
            ln_scale(dve, link, 1, 0)
            ln_scale(dve, link, 1, 1)
            normalise(U - 1, 1)
            ln_scale(dve, link, 1, 2)
            dve.wait_ge(x_added, 2 + U)
            ln_stats(dve, link, 1, B - 1)
            ln_scale(dve, link, 1, B - 1)
            route_vector(dve, link, 0)
            ffn_vector(dve, 0)
            for g in range(B):
                sum_outputs(dve, 0, g)
                ln_stats(dve, link, 2, g)
                if g:
                    ln_scale(dve, link, 2, g - 1)
            ln_scale(dve, link, 2, B - 1)
            la_vector(dve, link)
            for g in range(B):
                ln_scale(dve, link, 3, g)
            route_vector(dve, link, 1)
            ffn_vector(dve, 1)
            for g in range(B):
                sum_outputs(dve, 1, g)


def kernel(**inputs):
    import numpy as np
    import concourse.bacc as bacc
    from concourse.bass_utils import run_bass_kernel_spmd

    f = {n: np.asarray(a) for n, a in inputs.items()}
    w = f["L0_attn_a_W_kqv"]
    by_place = [np.ascontiguousarray(w[:, i * D:(i + 1) * D].reshape(D, H, HD).transpose(0, 2, 1).reshape(D, D))
                for i in (1, 0)]
    p, c = np.arange(P)[:, None], np.arange(P)[None, :]
    row = lambda v: np.broadcast_to(np.asarray(v, np.float32), (P, len(v)))
    consts = np.concatenate([
        (p == c), (c > p), (c >= p), row(128 * np.arange(T)), row(E - np.arange(E)), row(np.arange(E)),
        row(np.arange(N_SLOT_TILES)), p, T * P + p, row(np.tile(np.arange(T), 2)), row(np.arange(P)),
        row(P * np.tri(E, k=-1).ravel()), row(np.tri(E).ravel())],
        axis=1).astype(np.float32)
    t = np.arange(S)
    pos = np.broadcast_to(np.concatenate([t % 256, t - t % 256]).astype(np.float32), (H, 2 * S))
    arrays = {
        "x": f["L0_attn_a_x"], "wqk": np.concatenate(by_place, axis=1), "wv": w[:, 2 * D:],
        "slopes": f["L0_attn_a_m"].reshape(H, 1), "wq2": f["L0_attn_b_Wq"].T, "wk2": f["L0_attn_b_Wk"].T,
        "wv2": f["L0_attn_b_Wv"].T, "wo2": f["L0_attn_b_Wo"].T, "wr": f["L0_ffn_Wr"], "wg": f["L0_ffn_Wg"],
        "wu": f["L0_ffn_Wu"], "wd": f["L0_ffn_Wd"], "consts": consts, "pos_in": pos}
    arrays = {n: np.ascontiguousarray(a) for n, a in arrays.items()}
    nc = bacc.Bacc("TRN2", target_bir_lowering=False, num_devices=1)
    args = {n: nc.dram_tensor(n, a.shape, mybir.dt.from_np(a.dtype), kind="ExternalInput").ap()
            for n, a in arrays.items()}
    args["out"] = nc.dram_tensor("out", (B, S, D), mybir.dt.float32, kind="ExternalOutput").ap()
    build(nc, **args)
    r = run_bass_kernel_spmd(nc, [arrays], core_ids=[0])
    return r.results[0]["out"]
```

```python
import concourse.bass as bass
from concourse import mybir
from contextlib import ExitStack

B, S, D = 4, 512, 128
P = 128
T = B * S // P
BT = S // P
H, HD = 16, 8
HG, GH = 4, 4
U = B * HG
E, HID = 8, 512
NJ = HID // P
K2 = 64
N_SLOT_TILES = (2 * B * S + E * (P - 1)) // P
ROW = D + E
NPART = 3
KROWS = 96
PROD0 = KROWS - NPART * NPART * HD
MROWS = KROWS + NPART
UC = GH * S
NEG = -1.0e30
EPS = 1e-5
SEG = [0, S, S + 384, S + 384 + 256]
PCOLS = 1280

MBANKS = [(0, 4, 0), (0, 2, 1), (2, 2, 1)] + [(a, 1, 2) for a in range(4)] + [(a, 1, 3) for a in range(4)]
NM = len(MBANKS)
XGROUPS = [(0, 2, 1, 0), (2, 2, 1, 0), (0, 2, 1, 1), (2, 2, 1, 1), (0, 4, 2, 2), (0, 4, 4, 3)]
NX = len(XGROUPS)
GROUPS_OF_KB = [2, 4, 5, 6]


def build(nc, x, wqk, wv, slopes, wq2, wk2, wv2, wo2, wr, wg, wu, wd, consts, pos_in, out):
    f32, bf16, i32 = mybir.dt.float32, mybir.dt.bfloat16, mybir.dt.int32
    ALU, ACT, AX = mybir.AluOpType, mybir.ActivationFunctionType, mybir.AxisListType
    ds = bass.ds
    ctx = ExitStack()
    with ctx:
        def sb(name, shape, dt=f32):
            return ctx.enter_context(nc.sbuf_tensor(name, shape, dt))

        def sem(name):
            return ctx.enter_context(nc.semaphore(name))

        def dram(name, shape, dt=f32):
            return nc.dram_tensor(name, shape, dt, kind="Internal").ap()

        parts_dram = dram("parts_dram", (B, 2, NPART, P, S), bf16)
        rows_dram = parts_dram.rearrange("b a i (d h) t -> b a i d (h t)", h=H)
        bias_dram = dram("bias_dram", (2, PROD0, H, S), bf16)
        xn_dram = [dram(f"xn_dram{f}", (T * P, ROW)) for f in range(2)]
        y_dram = [dram(f"y_dram{f}", ((2 * T + 2) * P, D)) for f in range(2)]

        X = sb("X", [P, T, D])
        XW = sb("XW", [P, T, ROW])
        XNT = sb("XNT", [P, T * P])
        CON = sb("CON", [P, consts.shape[1]])
        ident = CON[:, 0:128]
        upper1 = CON[:, 128:256]
        causal1 = CON[:, 256:384]
        tile_starts = CON[:, 384:400]
        rev = CON[:, 400:408]
        eidx = CON[:, 408:416]
        tile_iota = CON[:, 416:416 + N_SLOT_TILES]
        pcol = CON[:, 456:457]
        tcol = CON[:, 458:490]
        iota128 = CON[:, 490:618]
        slots_before = CON[:, 618:682].rearrange("p (e k) -> p e k", e=E)
        up_to = CON[:, 682:746].rearrange("p (e k) -> p e k", e=E)
        pcol2 = CON[:, 746:747]
        padrow = CON[:, 747:747 + N_SLOT_TILES]
        ones_b = sb("ones_b", [P, P], bf16)
        upper_b = sb("upper_b", [P, P], bf16)
        stat = sb("stat", [P, 3, T])
        half_stat = sb("half_stat", [P, T, 6])
        mean_var = sb("mean_var", [P, T, 2])
        eps = sb("eps", [P, 1])
        table_in = sb("table_in", [1, 1])
        table_out = sb("table_out", [1, 1])
        ident_b = sb("ident_b", [P, P], bf16)
        mask_kq = sb("mask_kq", [P, GH, P], bf16)
        mask_qk4 = sb("mask_qk4", [P, GH, P], bf16)
        WQK = sb("WQK", [P, 2 * D])
        WV = sb("WV", [P, D])
        WQ2 = sb("WQ2", [P, 2, K2])
        WK2 = sb("WK2", [P, 2, K2])
        WV2 = sb("WV2", [P, K2])
        WO2 = sb("WO2", [P, D + 1])
        WR = sb("WR", [P, E])
        WE = sb("WE", [P, 3, E * HID])
        WGU = WE[:, 0:2].rearrange("p i n -> p (i n)")
        WD = WE[:, 2]
        V = sb("V", [P, T, D])
        SCR = sb("SCR", [P, 5 * 4096], bf16)
        early = WE.rearrange("p k n -> p (k n)")
        BIAS = early[0:H, 0:5 * S].bitcast(bf16).rearrange("p (r t) -> p r t", r=10)
        POS = early[0:H, 5 * S:7 * S]
        QKR = [early[:, (7 + 2 * i) * S:(9 + 2 * i) * S].rearrange("p (a n) -> p a n", a=2) for i in range(2)]
        QKP = [early[:, (11 + 3 * g) * S:(14 + 3 * g) * S].bitcast(bf16).rearrange("p (c a n) -> p c a n", c=NPART, a=2)
               for g in range(B)]
        slope = sb("slope", [H, 1])
        slope_r = sb("slope_r", [H, 2])
        slope_p = sb("slope_p", [H, 3])
        slope_pb = sb("slope_pb", [H, 3], bf16)
        QA = [sb(f"QA{i}", [MROWS, UC], bf16) for i in range(HG)]
        KA = [sb(f"KA{i}", [MROWS, UC], bf16) for i in range(HG)]
        PT = [SCR[:, 10240 * i:10240 * (i + 1)].bitcast(f32).rearrange("p (a n) -> p a n", a=GH)
              for i in range(2)]
        VU = [sb(f"VU{i}", [P, BT, GH, 32]) for i in range(2)]
        cmax = [sb(f"cmax{i}", [P, GH, BT]) for i in range(2)]
        negc = [sb(f"negc{i}", [GH * BT, P]) for i in range(2)]
        negr = sb("negr", [GH * BT, 1, P])
        zeros16 = sb("zeros16", [GH * BT, P])
        carrier = sb("carrier", [GH * BT, 1])
        cparts = [sb(f"cparts{i}", [GH * BT, NPART, P], bf16) for i in range(2)]
        OT = sb("OT", [P, S])
        rden = sb("rden", [P, BT, GH])
        NRM = [sb(f"NRM{i}", [P, BT, GH, HD]) for i in range(2)]

        PS = ctx.enter_context(nc.psum_tensor("PS", [P, 8, 512], f32))

        ld_x = [sem(f"ld_x{g}") for g in range(B)]
        ld_const, ld_wqkv, ld_small, ld_experts = sem("ld_const"), sem("ld_wqkv"), sem("ld_small"), sem("ld_experts")
        dve_chain, pool_chain = sem("dve_chain"), sem("pool_chain")
        ln_var, ln_centred, ln_std, ln_inverse = sem("ln_var"), sem("ln_centred"), sem("ln_std"), sem("ln_inverse")
        ln_done, ln_transposed, xnt_ready = sem("ln_done"), sem("ln_transposed"), sem("xnt_ready")
        consts_cast = sem("consts_cast")
        wq_scaled, k_ones, qk_proj, v_proj, v_copied = (
            sem("wq_scaled"), sem("k_ones"), sem("qk_proj"), sem("v_proj"), sem("v_copied"))
        part1, rest1, part2, part3, part3_pool = (
            sem("part1"), sem("rest1"), sem("part2"), sem("part3"), sem("part3_pool"))
        parts_stored = [sem(f"parts_stored{g}") for g in range(B)]
        slopes_spread = sem("slopes_spread")
        bias_built, bias_stored, bias_loaded, slope_split = (
            sem("bias_built"), sem("bias_stored"), sem("bias_loaded"), sem("slope_split"))
        eps_ready = sem("eps_ready")
        vu_cleared = sem("vu_cleared")
        qk_loaded = [sem(f"qk_loaded{i}") for i in range(HG)]
        max_ready, max_used, st_ready, exp_done = (
            sem("max_ready"), sem("max_used"), sem("st_ready"), sem("exp_done"))
        cmax_transposed, negc_ready, cparts_ready = sem("cmax_transposed"), sem("negc_ready"), sem("cparts_ready")
        crows_loaded = [sem(f"crows_loaded{i}") for i in range(2)]
        vu_ready, pv_done, ot_ready, to_ready, normed, x_added = (
            sem("vu_ready"), sem("pv_done"), sem("ot_ready"), sem("to_ready"), sem("normed"), sem("x_added"))

        std, rstd = stat[:, 0, :], stat[:, 1, :]

        def ln_stats(dve, link, LN, g):
            gs = slice(BT * g, BT * g + BT)
            for t in range(BT * g, BT * g + BT):
                last = nc.vector.bn_stats(half_stat[:, t, :], X[:, t, :])
            link(last)
            for t in range(BT * g, BT * g + BT):
                last = nc.vector.bn_aggr(mean_var[:, t, :], half_stat[:, t, :])
            last.then_inc(ln_var, 1)
            dve.wait_ge(ln_var, 4 * LN + g + 1)
            nc.vector.tensor_tensor(XW[:, gs, 0:D], X[:, gs, :], mean_var[:, gs, 0:1].to_broadcast([P, BT, D]),
                                    ALU.subtract).then_inc(ln_centred, 1)

        def ln_scale(dve, link, LN, g):
            gs = slice(BT * g, BT * g + BT)
            dve.wait_ge(ln_std, 4 * LN + g + 1)
            link(nc.vector.reciprocal(rstd[:, gs], std[:, gs]))
            dve.wait_ge(ln_centred, 4 * LN + g + 1)
            nc.vector.tensor_tensor(XW[:, gs, 0:D], XW[:, gs, 0:D], rstd[:, gs].unsqueeze(2).to_broadcast([P, BT, D]),
                                    ALU.mult).then_inc(ln_done, 1)

        def la_pool(pool):
            for g in range(2):
                gs = slice(BT * g, BT * g + BT)
                pool.wait_ge(ln_inverse, g + 1)
                pool.wait_ge(ln_centred, 12 + g + 1)
                nc.gpsimd.tensor_tensor(XW[:, gs, 0:D], XW[:, gs, 0:D],
                                        rstd[:, gs].unsqueeze(2).to_broadcast([P, BT, D]), ALU.mult).then_inc(ln_done, 1)

        def ln_scalar_std(act, LN, g):
            gs = slice(BT * g, BT * g + BT)
            act.wait_ge(ln_var, 4 * LN + g + 1)
            nc.scalar.activation(std[:, gs], mean_var[:, gs, 1], ACT.Sqrt, bias=eps[:, 0:1]).then_inc(ln_std, 1)

        def ln_scalar_copy(act, LN, g):
            act.wait_ge(ln_transposed, 4 * LN + g + 1)
            nc.scalar.activation(XNT[:, S * g:S * g + S], PS[:, g % 2, :], ACT.Copy).then_inc(xnt_ready, 1)

        def ln_tensor(pe, LN, g):
            pe.wait_ge(ln_done, 4 * LN + g + 1)
            if g >= 2:
                pe.wait_ge(xnt_ready, 4 * LN + g - 1)
            for t in range(BT):
                last = nc.tensor.transpose(PS[:, g % 2, P * t:P * t + P], XW[:, BT * g + t, 0:D], ident)
            last.then_inc(ln_transposed, 1)

        lg = sb("lg", [P, 8, T, E])
        (OH1, OH2, T0, T1, SLOT, C0, C1) = (lg[:, i] for i in range(1, 8))
        OH12, T01 = lg[:, 1:3], lg[:, 3:5]
        OHS = sb("OHS", [P, T, E], bf16)[:, :, :]
        rt = sb("rt", [P, 8, T])
        ex = sb("ex", [P, 3, E])
        slots_i = sb("slots_i", [P, 3, 2 * T], i32)
        ee = sb("ee", [P, E, E])
        OHLO = SCR[:, 0:4096].rearrange("p (c n) -> p c n", n=P)
        RHS = SCR[:, 4096:4096 + 6 * T * N_SLOT_TILES].rearrange("p (c k n) -> p c k n", c=2 * T, k=3)
        tmap = sb("tmap", [P, N_SLOT_TILES, E])
        tsel = sb("tsel", [P, N_SLOT_TILES, E])
        te = sb("te", [P, N_SLOT_TILES])
        te_off = sb("te_off", [P, N_SLOT_TILES], i32)
        te_off2 = sb("te_off2", [P, N_SLOT_TILES], i32)
        tok = sb("tok", [P, 2, N_SLOT_TILES])
        occ_tok = sb("occ_tok", [P, 3, N_SLOT_TILES])
        row_i = sb("row_i", [P, N_SLOT_TILES], i32)
        gidx = sb("gidx", [P, N_SLOT_TILES], i32)
        sidx = sb("sidx", [P, N_SLOT_TILES], i32)
        gcur = [sb(f"gcur{i}", [P, 1], i32) for i in range(4)]
        scur = [sb(f"scur{i}", [P, 1], i32) for i in range(2)]
        G = [sb(f"G{i}", [P, ROW]) for i in range(4)]
        xt = [sb(f"xt{i}", [P, P]) for i in range(2)]
        hs = [sb(f"hs{i}", [P, HID]) for i in range(2)]
        wcur = [sb(f"wcur{i}", [P, 2 * HID]) for i in range(2)]
        y_free = sb("y_free", [1, 1])
        wsel = [sb(f"wsel{i}", [P, E]) for i in range(2)]
        wslot = [sb(f"wslot{i}", [P, 1]) for i in range(4)]
        ytile = [sb(f"ytile{i}", [P, D]) for i in range(2)]
        Y0 = SCR[:, 0:4096].bitcast(f32).rearrange("p (t d) -> p t d", d=D)
        Y1 = SCR[:, 4096:8192].bitcast(f32).rearrange("p (t d) -> p t d", d=D)

        def ffn_sems(f):
            names = ("onehots oh_tile oh_place xn_stored gath0 gath1 gath2 gath3 gcopied xT xt w gate up silu "
                     "h down wsel y scat0 scat1 carried y_loaded0 y_loaded1 y_loaded2 y_loaded3 out_sum pair_sum")
            return {**{n: sem(f"f{f}_{n}") for n in names.split()}, **ROUTE_SEMS}

        ROUTE_SEMS = {n: sem(n) for n in ("logits", "exp_arg", "pair_exp", "w1", "comb", "ohs", "totals", "prefix",
                                          "tokens", "gidx", "idx", "toff")}
        FS = [ffn_sems(0), ffn_sems(1)]
        DEPTH_SCALE = 12.0 ** -0.5
        NCH = 4

        def route_vector(dve, link, f):
            s = FS[f]
            m1, m2, k1, k2, dlt, w1, w2, ew = (rt[:, i, :] for i in range(8))

            def bt(a):
                return a.unsqueeze(2).to_broadcast([P, T, E])

            def be(a):
                return a.unsqueeze(1).to_broadcast([P, T, E])
            dve.wait_ge(s["logits"], f + 1)
            nc.vector.memset(y_free[:, :], 0.0).then_inc(s["y"], 1)
            LOG = PS[:, 2, 0:T * E].rearrange("p (t e) -> p t e", e=E)
            link(nc.vector.reduce_max(m1, LOG, AX.X))
            link(nc.vector.tensor_tensor(T0, LOG, bt(m1), ALU.is_ge))
            link(nc.vector.tensor_tensor(T0, T0, be(rev), ALU.mult))
            link(nc.vector.reduce_max(k1, T0, AX.X))
            link(nc.vector.tensor_tensor(OH1, be(rev), bt(k1), ALU.is_equal))
            link(nc.vector.scalar_tensor_tensor(T1, OH1, NEG, LOG, ALU.mult, ALU.add))
            link(nc.vector.reduce_max(m2, T1, AX.X))
            nc.vector.tensor_tensor(dlt, m2, m1, ALU.subtract).then_inc(s["exp_arg"], 1)
            link(nc.vector.tensor_tensor(T0, T1, bt(m2), ALU.is_ge))
            link(nc.vector.tensor_tensor(T0, T0, be(rev), ALU.mult))
            link(nc.vector.reduce_max(k2, T0, AX.X))
            link(nc.vector.tensor_tensor(OH2, be(rev), bt(k2), ALU.is_equal))
            nc.vector.tensor_tensor(OHS, OH1, OH2, ALU.add).then_inc(s["ohs"], 1)
            dve.wait_ge(s["pair_exp"], f + 1)
            link(nc.vector.tensor_scalar(w1, ew, 1.0, None, ALU.add))
            nc.vector.reciprocal(w1, w1).then_inc(s["w1"], 1)
            nt, base, end = (ex[:, i, :] for i in range(3))
            starts = T0.rearrange("p t e -> p (t e)").rearrange("p (e j) -> p e j", e=E)
            dve.wait_ge(s["totals"], f + 1)
            link(nc.vector.tensor_tensor(starts, PS[:, 4, 0:E].unsqueeze(2).to_broadcast([P, E, T]),
                                         tile_starts.unsqueeze(1).to_broadcast([P, E, T]), ALU.is_gt))
            link(nc.vector.reduce_sum(nt, starts, AX.X))
            link(nc.vector.tensor_tensor(ee[:, :, :], nt.unsqueeze(1).to_broadcast([P, E, E]), slots_before, ALU.mult))
            link(nc.vector.reduce_sum(base, ee[:, :, :], AX.X))
            dve.wait_ge(s["prefix"], f + 1)
            link(nc.vector.tensor_tensor(SLOT, PS[:, 3, 0:T * E].rearrange("p (t e) -> p t e", e=E), be(base), ALU.add))
            link(nc.vector.tensor_tensor(T01, OH12, SLOT.unsqueeze(1).to_broadcast([P, 2, T, E]), ALU.mult))
            si, hi_i, lo_i = (slots_i[:, i, :] for i in range(3))
            link(nc.vector.reduce_max(si.rearrange("p (c t) -> p c t", c=2), T01, AX.X))
            nc.vector.tensor_scalar(hi_i, si, 7, None, ALU.logical_shift_right)
            link(nc.vector.tensor_scalar(lo_i, si, P - 1, None, ALU.bitwise_and))
            C = 2 * T // NCH
            for c in range(NCH):
                cs = slice(C * c, C * c + C)
                nc.vector.tensor_tensor(RHS[:, cs, 0, :], tile_iota.unsqueeze(1).to_broadcast([P, C, N_SLOT_TILES]),
                                        hi_i[:, cs].unsqueeze(2).to_broadcast([P, C, N_SLOT_TILES]),
                                        ALU.is_equal).then_inc(s["onehots"], 1)
                nc.vector.tensor_tensor(OHLO[:, cs, :], iota128.unsqueeze(1).to_broadcast([P, C, P]),
                                        lo_i[:, cs].unsqueeze(2).to_broadcast([P, C, P]),
                                        ALU.is_equal).then_inc(s["onehots"], 1)
            dve.wait_ge(s["tokens"], f + 1)
            link(nc.vector.tensor_copy(occ_tok[:, :, :].rearrange("p k n -> p (k n)"), PS[:, 5, 0:3 * N_SLOT_TILES]))
            link(nc.vector.scalar_tensor_tensor(row_i[:, :], occ_tok[:, 2, :], float(T), occ_tok[:, 1, :],
                                                ALU.mult, ALU.add))
            nc.vector.tensor_scalar(gidx[:, :], row_i[:, :], T * P - 1, None, ALU.bitwise_and).then_inc(s["gidx"], 1)
            link(nc.vector.tensor_scalar(tok[:, 0, :], occ_tok[:, 0, :], -1.0, 1.0, ALU.mult, ALU.add))
            link(nc.vector.tensor_tensor(tok[:, 1, :], tok[:, 0, :], padrow, ALU.mult))
            nc.vector.tensor_tensor(sidx[:, :], tok[:, 1, :], row_i[:, :], ALU.add).then_inc(s["idx"], 1)
            link(nc.vector.tensor_tensor(ee[:, :, :], nt.unsqueeze(1).to_broadcast([P, E, E]), up_to, ALU.mult))
            link(nc.vector.reduce_sum(end, ee[:, :, :], AX.X))
            link(nc.vector.tensor_tensor(tmap[:, :, :], tile_iota.unsqueeze(2).to_broadcast([P, N_SLOT_TILES, E]),
                                         end.unsqueeze(1).to_broadcast([P, N_SLOT_TILES, E]), ALU.is_ge))
            link(nc.vector.reduce_sum(te[:, :], tmap[:, :, :], AX.X))
            link(nc.vector.tensor_scalar(te[:, :], te[:, :], float(E - 1), None, ALU.min))
            nc.vector.tensor_scalar(te_off2[:, :], te[:, :], float(2 * HID), None, ALU.mult)
            nc.vector.tensor_scalar(te_off[:, :], te[:, :], float(HID), None, ALU.mult).then_inc(s["toff"], 1)
            link(nc.vector.tensor_tensor(tsel[:, :, :], eidx.unsqueeze(1).to_broadcast([P, N_SLOT_TILES, E]),
                                         te[:, :].unsqueeze(2).to_broadcast([P, N_SLOT_TILES, E]), ALU.is_equal))

        def route_pool(pool, link, f):
            s = FS[f]
            w1, w2, ew = (rt[:, i, :] for i in (5, 6, 7))
            pool.wait_ge(s["w1"], f + 1)
            link(nc.gpsimd.tensor_tensor(w2, ew, w1, ALU.mult))
            link(nc.gpsimd.tensor_scalar(rt[:, 5:7, :], rt[:, 5:7, :], DEPTH_SCALE, None, ALU.mult))
            link(nc.gpsimd.tensor_tensor(C0, OH1, w1.unsqueeze(2).to_broadcast([P, T, E]), ALU.mult))
            link(nc.gpsimd.tensor_tensor(C1, OH2, w2.unsqueeze(2).to_broadcast([P, T, E]), ALU.mult))
            nc.gpsimd.tensor_tensor(XW[:, :, D:ROW], C0, C1, ALU.add).then_inc(s["comb"], 1)
            C = 2 * T // NCH
            for c in range(NCH):
                cs = slice(C * c, C * c + C)
                pool.wait_ge(s["onehots"], 2 * c + 1)
                nc.gpsimd.tensor_tensor(RHS[:, cs, 1, :], RHS[:, cs, 0, :],
                                        tcol[:, cs].unsqueeze(2).to_broadcast([P, C, N_SLOT_TILES]),
                                        ALU.mult).then_inc(s["oh_tile"], 1)

        def ffn_tensor(pe, f):
            s = FS[f]
            if f == 0:
                pe.wait_ge(ld_small, 16 * 5)
            for g in range(B + 1):
                if g < B:
                    ln_tensor(pe, 1 + 2 * f, g)
                if g:
                    pe.wait_ge(xnt_ready, 4 * (1 + 2 * f) + g)
                    for t in range(BT * g - BT, BT * g):
                        last = nc.tensor.matmul(PS[:, 2, E * t:E * t + E], XNT[:, P * t:P * t + P], WR[:, :],
                                                start=True, stop=True)
            last.then_inc(s["logits"], 1)
            pe.wait_ge(s["ohs"], f + 1)
            flat = OHS.rearrange("p t e -> p (t e)")
            for t in range(T):
                last = nc.tensor.matmul(PS[:, 4, 0:E], ones_b[:, :], OHS[:, t, :], start=(t == 0), stop=(t == T - 1))
            last.then_inc(s["totals"], 1)
            nc.tensor.matmul(PS[:, 3, 0:T * E], upper_b[:, :], flat, start=True, stop=False, skip_group_check=True)
            for d in range(1, T):
                last = nc.tensor.matmul(PS[:, 3, E * d:T * E], ones_b[:, :], flat[:, 0:(T - d) * E], start=False,
                                        stop=(d == T - 1), skip_group_check=True)
            last.then_inc(s["prefix"], 1)
            for c in range(2 * T):
                if c % (2 * T // NCH) == 0:
                    chunk = c // (2 * T // NCH)
                    pe.wait_ge(s["onehots"], 2 * chunk + 2)
                    pe.wait_ge(s["oh_tile"], chunk + 1)
                    pe.wait_ge(s["oh_place"], chunk + 1)
                last = nc.tensor.matmul(PS[:, 5, 0:3 * N_SLOT_TILES], OHLO[:, c, :],
                                        RHS[:, c].rearrange("p k n -> p (k n)"), start=(c == 0), stop=(c == 2 * T - 1))
            last.then_inc(s["tokens"], 1)
            pe.wait_ge(s["toff"], f + 1)
            if f == 0:
                pe.wait_ge(ld_experts, 16 * 3 * E)
            gath = [s["gath0"], s["gath1"], s["gath2"], s["gath3"]]

            def transpose_x(q, rnd, n):
                pe.wait_ge(gath[q], 16 * (rnd + 1))
                if not isinstance(n, int) or n:
                    pe.wait_ge(s["xt"], n)
                nc.tensor.transpose(PS[:, 0, 0:P], G[q][:, 0:D], ident).then_inc(s["xT"], 1)

            def gate(par, n):
                pe.wait_ge(s["xt"], n + 1)
                pe.wait_ge(s["w"], n + 1)
                if not isinstance(n, int) or n:
                    pe.wait_ge(s["silu"], n)
                for j in range(NJ):
                    last = nc.tensor.matmul(PS[:, 1 + par, P * j:P * j + P], wcur[par][:, P * j:P * j + P],
                                            xt[par][:, :], start=True, stop=True)
                last.then_inc(s["gate"], 1)

            def up(par, n):
                if not isinstance(n, int) or n:
                    pe.wait_ge(s["h"], n)
                for j in range(NJ):
                    last = nc.tensor.matmul(PS[:, 3 + par, P * j:P * j + P], wcur[par][:, HID + P * j:HID + P * j + P],
                                            xt[par][:, :], start=True, stop=True)
                last.then_inc(s["up"], 1)

            def down(par, n, off):
                pe.wait_ge(s["h"], n + 1)
                pe.wait_ge(s["y"], n + 1)
                for j in range(NJ):
                    last = nc.tensor.matmul(PS[:, 6, 0:D], hs[par][:, P * j:P * j + P], WD[:, ds(off + P * j, P)],
                                            start=(j == 0), stop=(j == NJ - 1))
                last.then_inc(s["down"], 1)

            def tiles(r, left=None):
                for q in range(4 if left is None else left):
                    n, par, nxt = r * 4 + q, q % 2, (q + 1) % 2
                    if left is None or q + 1 < left:
                        gate(nxt, n + 1)
                    off = pe.value_load(te_off[0:1, ds(n, 1)], min_val=0, max_val=HID * (E - 1))
                    if left is None or q + 2 < left:
                        transpose_x((q + 2) % 4, r + (q + 2) // 4, n + 2)
                    if left is None or q + 1 < left:
                        up(nxt, n + 1)
                    down(par, n, off)

            transpose_x(0, 0, 0)
            transpose_x(1, 0, 1)
            gate(0, 0)
            up(0, 0)
            with pe.Fori(0, N_SLOT_TILES // 4) as r:
                tiles(r)
            tiles(N_SLOT_TILES // 4, left=N_SLOT_TILES % 4)

        def ffn_scalar_route(act, f):
            s = FS[f]
            act.wait_ge(s["exp_arg"], f + 1)
            nc.scalar.activation(rt[:, 7, :], rt[:, 4, :], ACT.Exp).then_inc(s["pair_exp"], 1)
            C = 2 * T // NCH
            for c in range(NCH):
                cs = slice(C * c, C * c + C)
                act.wait_ge(s["onehots"], 2 * c + 1)
                nc.scalar.activation(RHS[:, cs, 2, :], RHS[:, cs, 0, :], ACT.Copy,
                                     scale=pcol if c < NCH // 2 else pcol2).then_inc(s["oh_place"], 1)

        def load_table(function):
            nc.scalar.activation(table_out[:, :], table_in[:, :], function)

        def ffn_scalar(act, f):
            s = FS[f]

            def xt_copy(par, n):
                act.wait_ge(s["xT"], n + 1)
                nc.scalar.activation(xt[par][:, :], PS[:, 0, 0:P], ACT.Copy).then_inc(s["xt"], 1)

            def weights(par, n):
                off = act.value_load(te_off2[0:1, ds(n, 1)], min_val=0, max_val=2 * HID * (E - 1))
                if not isinstance(n, int) or n >= 2:
                    act.wait_ge(s["up"], n - 1)
                nc.scalar.activation(wcur[par][:, :], WGU[:, ds(off, 2 * HID)], ACT.Copy).then_inc(s["w"], 1)

            def silu(par, n):
                act.wait_ge(s["gate"], n + 1)
                if not isinstance(n, int) or n >= 2:
                    act.wait_ge(s["down"], n - 1)
                nc.scalar.activation(hs[par][:, :], PS[:, 1 + par, :], ACT.Silu).then_inc(s["silu"], 1)

            def tiles(r, left=None):
                for q in range(2 if left is None else left):
                    n = r * 2 + q
                    if left is None or q + 2 < left:
                        weights(q % 2, n + 2)
                    if left is None or q + 1 < left:
                        silu((q + 1) % 2, n + 1)
                    if left is None or q + 2 < left:
                        xt_copy(q % 2, n + 2)
            load_table(ACT.Silu)
            act.wait_ge(s["toff"], f + 1)
            if f == 0:
                act.wait_ge(ld_experts, 16 * 3 * E)
            weights(0, 0)
            xt_copy(0, 0)
            weights(1, 1)
            xt_copy(1, 1)
            silu(0, 0)
            tiles(0)
            with act.Fori(1, N_SLOT_TILES // 4 * 2) as r:
                tiles(r)
            tiles(N_SLOT_TILES // 4 * 2, left=N_SLOT_TILES % 4)

        def ffn_vector(dve, f):
            s = FS[f]
            gath = [s["gath0"], s["gath1"], s["gath2"], s["gath3"]]

            def hprod(par, n):
                dve.wait_ge(s["silu"], n + 1)
                dve.wait_ge(s["up"], n + 1)
                nc.vector.tensor_tensor(hs[par][:, :], hs[par][:, :], PS[:, 3 + par, :], ALU.mult).then_inc(s["h"], 1)

            def weight(q, rnd, n):
                dve.wait_ge(gath[q], 16 * (rnd + 1))
                nc.vector.tensor_tensor(wsel[q % 2][:, :], G[q][:, D:ROW], tsel[:, ds(n, 1), :].rearrange("p a e -> p (a e)"),
                                        ALU.mult).then_inc(s["wsel"], 1)
                dve.wait_ge(s["wsel"], 2 * n + 1)
                nc.vector.reduce_sum(wslot[q][:, :], wsel[q % 2][:, :], AX.X).then_inc(s["wsel"], 1)

            def result(par, q, n):
                dve.wait_ge(s["down"], n + 1)
                dve.wait_ge(s["wsel"], 2 * n + 2)
                if not isinstance(n, int) or n >= 2:
                    dve.wait_ge([s["scat0"], s["scat1"]][par], (n - par) * 8)
                nc.vector.tensor_copy(scur[par][:, :], sidx[:, ds(n, 1)])
                nc.vector.tensor_scalar(ytile[par][:, :], PS[:, 6, 0:D], wslot[q][:, 0:1], None,
                                        ALU.mult).then_inc(s["y"], 1)

            def tiles(r, left=None, gathers=4):
                for q in range(4 if left is None else left):
                    n = r * 4 + q
                    if left is None or q + 2 < left:
                        weight((q + 2) % 4, r + (q + 2) // 4, n + 2)
                    if q < gathers:
                        nc.vector.tensor_copy(gcur[q][:, :], gidx[:, ds(n + 4, 1)]).then_inc(s["gcopied"], 1)
                    if left is None or q + 1 < left:
                        hprod((q + 1) % 2, n + 1)
                    result(q % 2, q, n)
            weight(0, 0, 0)
            weight(1, 0, 1)
            hprod(0, 0)
            tiles(0)
            groups, rest = N_SLOT_TILES // 4, N_SLOT_TILES % 4
            with dve.Fori(1, groups - 1) as r:
                tiles(r)
            tiles(groups - 1, gathers=rest)
            tiles(groups, left=rest, gathers=0)

        def carry_wait(pool, s, before):
            if not isinstance(before, int) or before:
                pool.wait_ge(s["carried"], before)
            nc.gpsimd.tensor_tensor(carrier[:, :], zeros16[:, 0:1], zeros16[:, 0:1], ALU.add).then_inc(s["carried"], 1)

        def ffn_pool(pool, f):
            s = FS[f]
            gath = [s["gath0"], s["gath1"], s["gath2"], s["gath3"]]
            scat = [s["scat0"], s["scat1"]]
            pool.wait_ge(s["gidx"], f + 1)
            pool.wait_ge(s["xn_stored"], 16)

            def gather(q, indices):
                nc.gpsimd.indirect_dma_start(G[q][:, :], None, xn_dram[f], bass.IndirectOffsetOnAxis(indices, axis=0),
                                             bounds_check=T * P - 1, oob_is_err=False).then_inc(gath[q], 16)

            def scatter(par, n, before):
                pool.wait_ge(s["y"], n + 2)
                carry_wait(pool, s, before)
                nc.gpsimd.indirect_dma_start(y_dram[f], bass.IndirectOffsetOnAxis(scur[par][:, 0:1], axis=0),
                                             ytile[par][:, :], None, bounds_check=(2 * T + 2) * P - 1,
                                             oob_is_err=True).then_inc(scat[par], 16)
            for n in range(4):
                gather(n, gidx[:, n:n + 1])

            def tiles(r, count=4, gathers=4):
                for q in range(count):
                    n = r * 4 + q
                    if q < gathers:
                        pool.wait_ge(s["xT"], n + 1)
                        pool.wait_ge(s["gcopied"], n + 1)
                        carry_wait(pool, s, 2 * n)
                        gather(q, gcur[q][:, 0:1])
                    scatter(q % 2, n, 2 * n + 1 if q < gathers else n + N_SLOT_TILES - 4)
            pool.wait_ge(s["idx"], f + 1)
            groups, rest = N_SLOT_TILES // 4, N_SLOT_TILES % 4
            tiles(0)
            with pool.Fori(1, groups - 1) as r:
                tiles(r)
            tiles(groups - 1, gathers=rest)
            tiles(groups, count=rest, gathers=0)

        def ffn_sync(sp, f):
            s = FS[f]
            sp.wait_ge(ln_done, 4 * (1 + 2 * f) + 4)
            sp.wait_ge(s["comb"], f + 1)
            sp.dma_start(xn_dram[f].rearrange("(p t) d -> p t d", p=P), XW[:, :, :]).then_inc(s["xn_stored"], 16)
            for i in range(2):
                sp.wait_ge(s[f"scat{i}"], 16 * ((N_SLOT_TILES + 1 - i) // 2))
            for g in range(B):
                for choice, Y in enumerate((Y0, Y1)):
                    y = y_dram[f][T * P * choice:T * P * (choice + 1), :].rearrange("(p t) d -> p t d", p=P)
                    sp.dma_start(Y[:, BT * g:BT * g + BT, :], y[:, BT * g:BT * g + BT, :]).then_inc(s[f"y_loaded{g}"], 16)

        def sum_outputs(dve, f, g):
            s = FS[f]
            gs = slice(BT * g, BT * g + BT)
            if g == 0:
                dve.wait_ge(s["y_loaded0"], 32)
                nc.vector.tensor_tensor(Y0[:, gs, :], Y0[:, gs, :], Y1[:, gs, :], ALU.add).then_inc(s["out_sum"], 1)
                dve.wait_ge(s["out_sum"], 1)
            else:
                dve.wait_ge(s["pair_sum"], g)
            nc.vector.tensor_tensor(X[:, gs, :], X[:, gs, :], Y0[:, gs, :], ALU.add).then_inc(s["out_sum"], 1)
            dve.wait_ge(s["out_sum"], g + 2)

        def pair_sums(pool, f):
            for g in range(1, B):
                pool.wait_ge(FS[f][f"y_loaded{g}"], 32)
                gs = slice(BT * g, BT * g + BT)
                nc.gpsimd.tensor_tensor(Y0[:, gs, :], Y0[:, gs, :], Y1[:, gs, :], ALU.add).then_inc(FS[f]["pair_sum"], 1)

        out_stored, cchain, rden_ready, ld_pos = (
            sem("out_stored"), sem("cchain"), sem("rden_ready"), sem("ld_pos"))
        block = ctx.enter_context(nc.Block())

        RN = SCR[:, 8192:10240].bitcast(f32).rearrange("p (a n) -> p a n", a=2)
        FE = SCR[:, 10240:12288].bitcast(f32).rearrange("p (a n) -> p a n", a=2)
        FQK = SCR[:, 12288:14336].bitcast(f32).rearrange("p (a n) -> p a n", a=2)
        AT = SCR[:, 14336:14336 + 2 * PCOLS].bitcast(f32)
        NT = SCR[:, 16896:16896 + 2 * S].bitcast(f32)
        V1 = sb("V1", [P, 2, BT, P])
        la = {n: sem("la_" + n) for n in ("proj", "vproj", "relu", "exp", "feat", "v", "a", "diag", "rest", "num", "nt",
                                          "fin", "den", "x")}

        def la_tensor(pe):
            def project(b):
                pe.wait_ge(xnt_ready, 8 + b + 1)
                xb = XNT[:, S * b:S * b + S]
                nc.tensor.matmul(PS[:, 2, :], WQ2[:, :, :].rearrange("p i k -> p (i k)"), xb, start=True, stop=True)
                nc.tensor.matmul(PS[:, 3, :], WK2[:, :, :].rearrange("p i k -> p (i k)"), xb, start=True,
                                 stop=True).then_inc(la["proj"], 1)

            def project_values(b):
                if b:
                    pe.wait_ge(la["v"], b)
                for t in range(BT):
                    last = nc.tensor.matmul(PS[:, 0, K2 * t:K2 * t + K2], XNT[:, S * b + P * t:S * b + P * t + P],
                                            WV2[:, :], start=True, stop=True)
                last.then_inc(la["vproj"], 1)

            def scores(b):
                pe.wait_ge(la["feat"], b + 1)
                for kb in range(BT):
                    if b or kb >= 2:
                        pe.wait_ge(la["diag"], BT * b + kb - 1)
                        if kb != 1:
                            pe.wait_ge(la["rest"], 3 * b + max(kb - 1, 0))
                    n = S - P * kb
                    nc.tensor.matmul(PS[:, 4 + kb % 2, 0:n], FQK[:, 1, P * kb:P * kb + P], FQK[:, 0, P * kb:S],
                                     start=True, stop=True).then_inc(la["a"], 1)

            def numerator(b):
                pe.wait_ge(la["v"], b + 1)
                if b:
                    pe.wait_ge(la["nt"], b)
                for kb in range(BT):
                    pe.wait_ge(la["diag"], BT * b + kb + 1)
                    pe.wait_ge(la["rest"], 3 * b + min(kb + 1, 3))
                    last = nc.tensor.matmul(PS[:, 1, P * kb:S], V1[:, b % 2, kb, :], AT[:, SEG[kb]:SEG[kb] + S - P * kb],
                                            start=(kb == 0), stop=(kb == BT - 1), skip_group_check=True)
                last.then_inc(la["num"], 1)

            def output(b):
                pe.wait_ge(la["nt"], b + 1)
                if b:
                    pe.wait_ge(la["x"], b)
                for qb in range(BT):
                    last = nc.tensor.matmul(PS[:, 6 + qb // 2, (D + 1) * (qb % 2):(D + 1) * (qb % 2 + 1)],
                                            NT[:, P * qb:P * qb + P], WO2[:, :], start=True, stop=True)
                last.then_inc(la["fin"], 1)

            ln_tensor(pe, 2, 0)
            project(0)
            ln_tensor(pe, 2, 1)
            ln_tensor(pe, 2, 2)
            ln_tensor(pe, 2, 3)
            pe.wait_ge(xnt_ready, 12)
            project_values(0)
            for b in range(B):
                scores(b)
                if b + 1 < B:
                    project(b + 1)
                if b:
                    output(b - 1)
                if b + 1 < B:
                    project_values(b + 1)
                numerator(b)
            output(B - 1)

        def la_scalar(act):
            def exponential(b):
                act.wait_ge(la["proj"], b + 1)
                nc.scalar.activation(RN, PS[:, 2:4, :], ACT.Relu, scale=-1.0).then_inc(la["relu"], 1)
                act.wait_ge(la["relu"], b + 1)
                nc.scalar.activation(FE, RN, ACT.Exp, scale=-1.0).then_inc(la["exp"], 1)

            def values(b):
                act.wait_ge(la["vproj"], b + 1)
                if b >= 2:
                    act.wait_ge(la["num"], b - 1)
                nc.scalar.activation(V1[:, b % 2, :, 0:K2], PS[:, 0, 0:BT * K2].rearrange("p (t m) -> p t m", m=K2),
                                     ACT.Copy).then_inc(la["v"], 1)

            def scores(b):
                for kb in range(BT - 1):
                    act.wait_ge(la["diag"], BT * b + kb + 1)
                    n = S - P * kb
                    nc.scalar.activation(AT[:, SEG[kb] + P:SEG[kb] + n], PS[:, 4 + kb % 2, P:n],
                                         ACT.Copy).then_inc(la["rest"], 1)

            load_table(ACT.Exp)
            exponential(0)
            ln_scalar_copy(act, 2, B - 2)
            ln_scalar_copy(act, 2, B - 1)
            values(0)
            for b in range(B):
                scores(b)
                if b + 1 < B:
                    exponential(b + 1)
                    values(b + 1)
                else:
                    ln_scalar_std(act, 3, 0)
                    ln_scalar_std(act, 3, 1)
                act.wait_ge(la["num"], b + 1)
                if b:
                    act.wait_ge(la["fin"], b)
                nc.scalar.activation(NT, PS[:, 1, :], ACT.Copy).then_inc(la["nt"], 1)

        def la_vector(dve, link):
            def features(b):
                dve.wait_ge(la["exp"], b + 1)
                nc.vector.scalar_tensor_tensor(FQK.rearrange("p a n -> p (a n)"),
                                               PS[:, 2:4, :].rearrange("p a n -> p (a n)"), 0.0,
                                               FE.rearrange("p a n -> p (a n)"), ALU.max,
                                               ALU.add).then_inc(la["feat"], 1)

            def output(b):
                dve.wait_ge(la["fin"], b + 1)
                o = PS[:, 6:8, 0:2 * (D + 1)].rearrange("p k (i n) -> p k i n", i=2)
                den = stat[:, 2, 0:BT].rearrange("p (k i) -> p k i", k=2)
                nc.vector.tensor_scalar(den, o[:, :, :, D], 2e-6, None, ALU.add).then_inc(la["den"], 1)
                dve.wait_ge(la["den"], 2 * b + 1)
                nc.vector.reciprocal(den, den).then_inc(la["den"], 1)
                dve.wait_ge(la["den"], 2 * b + 2)
                for qb in range(BT):
                    x_rows = X[:, BT * b + qb, :]
                    last = nc.vector.scalar_tensor_tensor(x_rows, o[:, qb // 2, qb % 2, 0:D], stat[:, 2, qb:qb + 1],
                                                          x_rows, ALU.mult, ALU.add)
                last.then_inc(la["x"], 1)

            def stats(b):
                dve.wait_ge(la["x"], b + 1)
                ln_stats(dve, link, 3, b)

            features(0)
            for b in range(B):
                if b:
                    dve.wait_ge(la["num"], b)
                for kb in range(BT):
                    dve.wait_ge(la["a"], BT * b + kb + 1)
                    nc.vector.tensor_tensor(AT[:, SEG[kb]:SEG[kb] + P], PS[:, 4 + kb % 2, 0:P], causal1,
                                            ALU.mult).then_inc(la["diag"], 1)
                if b >= 2:
                    stats(b - 2)
                if b:
                    output(b - 1)
                if b + 1 < B:
                    features(b + 1)
            stats(B - 2)
            for g in range(2):
                dve.wait_ge(ln_std, 12 + g + 1)
                gs = slice(BT * g, BT * g + BT)
                nc.vector.reciprocal(rstd[:, gs], std[:, gs]).then_inc(ln_inverse, 1)
            output(B - 1)
            stats(B - 1)
            dve.wait_ge(ln_done, 12 + 2)
            ln_scale(dve, link, 3, 2)
            ln_scale(dve, link, 3, 3)

        @block.sync
        def _(sp):
            for g in range(B):
                sp.dma_start(X[:, BT * g:BT * g + BT, :],
                             x[g].rearrange("(t p) d -> p t d", p=P)).then_inc(ld_x[g], 16)
                if g == 0:
                    sp.dma_start(WQK[:, :], wqk).then_inc(ld_wqkv, 16)
                    sp.dma_start(WV[:, :], wv).then_inc(ld_wqkv, 16)
                    sp.dma_start(CON[:, :], consts[:, :]).then_inc(ld_const, 16)
            sp.wait_ge(slopes_spread, NPART)
            sp.wait_ge(bias_built, 5)
            for side in range(2):
                view = bias_dram[side].rearrange("r h t -> h r t")
                for k in range(2):
                    m_row, p_row = NPART * (k + 2 * side), NPART * (k + 2 - 2 * side)
                    m0 = 2 + NPART * side
                    sp.dma_start(view[:, m_row:m_row + NPART, :], BIAS[:, m0:m0 + NPART, :]).then_inc(bias_stored, 16)
                    sp.dma_start(view[:, p_row:p_row + NPART, :],
                                 BIAS[:, k:k + 1, :].to_broadcast([H, NPART, S])).then_inc(bias_stored, 16)
                sp.dma_start(view[:, 4 * NPART:PROD0, :],
                             BIAS[:, 8:9, :].to_broadcast([H, PROD0 - 4 * NPART, S])).then_inc(bias_stored, 16)
            sp.wait_ge(bias_stored, 16 * 10)
            def load_operands(b, hg):
                cols = slice(UC * hg, UC * hg + UC)
                b1 = ds(b, 1)
                for i in range(NPART):
                    r0 = PROD0 + NPART * HD * i
                    sp.dma_start(QA[hg][r0:r0 + NPART * HD, :],
                                 rows_dram[b1, 0, i, :, cols].to_broadcast([NPART, HD, UC])).then_inc(qk_loaded[hg], 16)
                sp.dma_start(KA[hg][PROD0:KROWS, :],
                             rows_dram[b1, 1, :, :, cols].rearrange("o i d n -> o (i d) n")
                             .to_broadcast([NPART, NPART * HD, UC])).then_inc(qk_loaded[hg], 16)

            for g in range(B):
                if g < 2:
                    sp.wait_ge(part3, g + 1)
                else:
                    sp.wait_ge(part3_pool, g - 1)
                for a in range(2):
                    sp.dma_start(parts_dram[g, a].rearrange("i p t -> p i t"),
                                 QKP[g][:, :, a, :]).then_inc(parts_stored[g], 16)
                if g == 0:
                    for hg in range(HG):
                        for side, A in enumerate((QA, KA)):
                            loaded = crows_loaded[hg] if side == 0 and hg < 2 else bias_loaded
                            sp.dma_start(A[hg][0:PROD0, :].rearrange("r (h t) -> r h t", h=GH),
                                         bias_dram[side, :, GH * hg:GH * hg + GH, :]).then_inc(loaded, 16)
                    sp.wait_ge(parts_stored[0], 32)
                    for hg in range(3):
                        load_operands(0, hg)
            for g in range(1, B):
                sp.wait_ge(parts_stored[g], 32)
            for w, d in ((WQ2, wq2), (WK2, wk2)):
                sp.dma_start(w[:, :, :], d.unsqueeze(1).to_broadcast([P, 2, K2])).then_inc(ld_small, 16)
            for w, d in ((WV2, wv2), (WR, wr)):
                sp.dma_start(w[:, :], d).then_inc(ld_small, 16)
            sp.wait_ge(vu_cleared, 1)
            sp.dma_start(WO2[0:K2, 0:D], wo2).then_inc(ld_small, 16)
            def load_max(u, hg):
                sp.wait_ge(cparts_ready, u + 1)
                for i in range(NPART):
                    sp.dma_start(QA[hg][KROWS + i:KROWS + i + 1, :].rearrange("o (k t) -> o k t", t=P),
                                 cparts[hg % 2][:, i, :]).then_inc(crows_loaded[hg % 2], 16)

            def load_expert_part(b, j):
                e = b * 2 + j // 2
                if j % 2 == 0:
                    for i, w in enumerate((wg, wu)):
                        sp.dma_start(WGU[:, ds(e * (2 * HID) + HID * i, HID)],
                                     w[ds(e, 1)].rearrange("o p c -> (o p) c")).then_inc(ld_experts, 16)
                else:
                    sp.dma_start(WD[:, ds(e * HID, HID)].rearrange("p (j c) -> p j c", j=NJ),
                                 wd[ds(e, 1)].rearrange("o (j p) c -> p (o j) c", p=P)).then_inc(ld_experts, 16)

            load_max(0, 0)
            with sp.Fori(0, B - 1) as b:
                for j in range(HG):
                    u = b * HG + j
                    sp.wait_ge(exp_done, NX * u + 2)
                    load_operands(b + (j + 3) // HG, (j + 3) % HG)
                    load_max(u + 1, (j + 1) % HG)
                    load_expert_part(b, j)
            b = B - 1
            for j in range(HG):
                u = b * HG + j
                if j == 0:
                    sp.wait_ge(exp_done, NX * u + 2)
                    load_operands(b, 3)
                if j < 3:
                    load_max(u + 1, j + 1)
                load_expert_part(b, j)
            ffn_sync(sp, 0)
            ffn_sync(sp, 1)
            for g in range(B):
                sp.wait_ge(FS[1]["out_sum"], g + 2)
                sp.dma_start(out[g].rearrange("(t p) d -> p t d", p=P), X[:, BT * g:BT * g + BT, :]).then_inc(out_stored, 16)
            sp.wait_ge(out_stored, 16 * B)

        @block.gpsimd
        def _(pool):
            count = [0]

            def link(ins):
                count[0] += 1
                ins.then_inc(pool_chain, 1)
                pool.wait_ge(pool_chain, count[0])
            pool.dma_start(POS, pos_in).then_inc(ld_pos, 16)
            pool.dma_start(slope[:, :], slopes).then_inc(ld_pos, 16)
            pool.wait_ge(ld_wqkv, 32)
            nc.gpsimd.tensor_scalar(WQK[:, 0:D], WQK[:, 0:D], float(D) ** -0.5, None, ALU.mult).then_inc(wq_scaled, 1)
            pool.wait_ge(ld_pos, 32)
            link(nc.gpsimd.tensor_copy(slope_pb[:, 0:1], slope[:, :]))
            link(nc.gpsimd.tensor_tensor(slope_r[:, 0:1], slope[:, :], slope_pb[:, 0:1], ALU.subtract))
            link(nc.gpsimd.tensor_copy(slope_pb[:, 1:2], slope_r[:, 0:1]))
            link(nc.gpsimd.tensor_tensor(slope_r[:, 1:2], slope_r[:, 0:1], slope_pb[:, 1:2], ALU.subtract))
            link(nc.gpsimd.tensor_copy(slope_pb[:, 2:3], slope_r[:, 1:2]))
            nc.gpsimd.tensor_copy(slope_p[:, :], slope_pb[:, :]).then_inc(slope_split, 1)
            pos = POS.rearrange("h (k t) -> h k t", k=2)
            nc.gpsimd.tensor_copy(BIAS[:, 0:2, :], pos).then_inc(bias_built, 1)
            nc.gpsimd.memset(BIAS[:, 8, :].bitcast(f32), 0.0).then_inc(bias_built, 1)
            link(nc.gpsimd.memset(zeros16[:, :], 0.0))
            for hg in range(HG):
                nc.gpsimd.memset(KA[hg][KROWS:MROWS, :], 1.0).then_inc(k_ones, 1)
            pool.wait_ge(k_ones, HG)
            for i in range(2):
                link(nc.gpsimd.memset(VU[i][:, :, :, :], 0.0))
                link(nc.gpsimd.memset(VU[i][:, :, :, HD:HD + 1], 1.0))
            link(nc.gpsimd.memset(WO2[:, :], 0.0))
            link(nc.gpsimd.memset(WO2[K2:K2 + 1, D:D + 1], 1.0))
            link(nc.gpsimd.memset(V1[:, :, :, :], 0.0))
            link(nc.gpsimd.memset(V1[:, :, :, K2:K2 + 1], 1.0))
            nc.gpsimd.memset(tok[:, :, :], 0.0).then_inc(vu_cleared, 1)

            for g in range(2, B):
                pool.wait_ge(part2, g + 1)
                nc.gpsimd.tensor_tensor(QKP[g][:, 2], QKR[g % 2], QKP[g][:, 1], ALU.subtract).then_inc(part3_pool, 1)

            def split_max(u, par):
                pool.wait_ge(negc_ready, u + 1)
                if not isinstance(u, int) or u >= 2:
                    pool.wait_ge(crows_loaded[par], 24 * (u - par) + 16)
                nc.gpsimd.tensor_tensor(cparts[par][:, 0, :], negc[par][:, :], zeros16[:, :],
                                        ALU.subtract).then_inc(cchain, 1)
                pool.wait_ge(cchain, 3 * u + 1)
                nc.gpsimd.tensor_tensor(negr[:, 0, :], negc[par][:, :], cparts[par][:, 0, :],
                                        ALU.subtract).then_inc(cchain, 1)
                pool.wait_ge(cchain, 3 * u + 2)
                nc.gpsimd.tensor_tensor(cparts[par][:, 1, :], negr[:, 0, :], zeros16[:, :],
                                        ALU.subtract).then_inc(cchain, 1)
                pool.wait_ge(cchain, 3 * u + 3)
                nc.gpsimd.tensor_tensor(cparts[par][:, 2, :], negr[:, 0, :], cparts[par][:, 1, :],
                                        ALU.subtract).then_inc(cparts_ready, 1)

            def unit_values(u, par, b, hg):
                pool.wait_ge(pv_done, u + 1)
                nc.gpsimd.tensor_copy(VU[par][:, :, :, 0:HD],
                                      V[:, ds(b * BT, BT), 32 * hg:32 * hg + 32]
                                      .rearrange("p t (a d) -> p t a d", a=GH)).then_inc(vu_ready, 1)

            def add_unit(u, par, b, hg):
                pool.wait_ge(normed, u + 2)
                xs = X[:, ds(b * BT, BT), 32 * hg:32 * hg + 32].rearrange("p t (a d) -> p t a d", a=GH)
                nc.gpsimd.tensor_tensor(xs, xs, NRM[par][:, :, :, :], ALU.add).then_inc(x_added, 1)

            def step(u, batch, hg, previous_batch, last=False):
                if not last:
                    split_max(u + 1, (hg + 1) % 2)
                unit_values(u, hg % 2, batch, hg)
                if previous_batch is not None:
                    add_unit(u - 1, (hg + 1) % 2, previous_batch, (hg + 3) % HG)

            nc.gpsimd.memset(carrier[:, :], 0.0).then_inc(x_added, 2)
            pool.wait_ge(v_copied, B)
            split_max(0, 0)
            step(0, 0, 0, None)
            with pool.Fori(0, B - 1) as b:
                for j in range(1, HG + 1):
                    step(b * HG + j, b + j // HG, j % HG, b)
            for u in range(U - 3, U):
                step(u, B - 1, u % HG, B - 1, last=(u == U - 1))
            add_unit(U - 1, 1, B - 1, HG - 1)
            for f in range(2):
                route_pool(pool, link, f)
                ffn_pool(pool, f)
                pair_sums(pool, f)
                if f == 0:
                    la_pool(pool)

        @block.scalar
        def _(act):
            def first_part(g):
                act.wait_ge(qk_proj, g + 1)
                nc.scalar.activation(QKP[g][:, 0], PS[:, 2 + 2 * (g % 2):4 + 2 * (g % 2), :], ACT.Copy).then_inc(part1, 1)

            def second_part(g):
                act.wait_ge(rest1, g + 1)
                nc.scalar.activation(QKP[g][:, 1], QKR[g % 2], ACT.Copy).then_inc(part2, 1)

            def values(g):
                act.wait_ge(v_proj, g + 1)
                nc.scalar.activation(V[:, BT * g:BT * g + BT, :], PS[:, 6 + g % 2, :].rearrange("p (t n) -> p t n", t=BT),
                                     ACT.Copy).then_inc(v_copied, 1)

            act.wait_ge(eps_ready, 1)
            ln_scalar_std(act, 0, 0)
            act.wait_ge(slope_split, 1)
            for i in range(NPART):
                nc.scalar.activation(BIAS[:, 2 + i, :], POS[:, 0:S], ACT.Identity, bias=slope_p[:, i:i + 1],
                                     scale=0.0).then_inc(slopes_spread, 1)
            ln_scalar_std(act, 0, 1)
            ln_scalar_copy(act, 0, 0)
            act.wait_ge(slopes_spread, NPART)
            for i in range(NPART):
                nc.scalar.activation(BIAS[:, 5 + i, :], BIAS[:, 2 + i, :], ACT.Copy,
                                     scale=-1.0).then_inc(bias_built, 1)
            ln_scalar_std(act, 0, 2)
            ln_scalar_copy(act, 0, 1)
            first_part(0)
            ln_scalar_std(act, 0, 3)
            second_part(0)
            first_part(1)
            ln_scalar_copy(act, 0, 2)
            values(0)
            second_part(1)
            first_part(2)
            ln_scalar_copy(act, 0, 3)
            values(1)
            second_part(2)
            first_part(3)
            values(2)
            second_part(3)
            values(3)

            def step(u, par, first=False):
                act.wait_ge(pv_done, u + 1)
                for k, (a0, na, per, kb) in enumerate(XGROUPS):
                    n = S - P * kb
                    act.wait_ge(st_ready, NX * u + k + 1)
                    bank = 2 + 2 * (k % 2)
                    nb = na // per
                    src = (PS[:, bank, 0:na * n].rearrange("p (a n) -> p a n", a=na) if nb == 1 else
                           PS[:, bank:bank + nb, 0:per * n] if per == 1 else
                           PS[:, bank:bank + nb, :].rearrange("p k (a n) -> p (k a) n", a=per))
                    nc.scalar.activation(PT[par][:, a0:a0 + na, SEG[kb]:SEG[kb] + n], src,
                                         ACT.Exp).then_inc(exp_done, 1)
                    if k == 3 and not first:
                        evacuate(u - 1)

            def evacuate(u):
                act.wait_ge(pv_done, u + 3)
                act.wait_ge(to_ready, u + 1)
                nc.scalar.activation(OT[:, :], PS[:, 6, :], ACT.Copy).then_inc(ot_ready, 1)

            step(0, 0, first=True)
            with act.Fori(0, B - 1) as b:
                for j in range(1, HG + 1):
                    step(b * HG + j, j % 2)
            for u in range(U - 3, U):
                step(u, u % 2)
            for g in range(B - 1):
                ln_scalar_std(act, 1, g)
            evacuate(U - 1)
            for g in range(B - 1):
                ln_scalar_copy(act, 1, g)
            ln_scalar_std(act, 1, B - 1)
            ln_scalar_copy(act, 1, B - 1)
            ffn_scalar_route(act, 0)
            ffn_scalar(act, 0)
            ln_scalar_std(act, 2, 0)
            ln_scalar_std(act, 2, 1)
            ln_scalar_copy(act, 2, 0)
            ln_scalar_std(act, 2, 2)
            ln_scalar_copy(act, 2, 1)
            ln_scalar_std(act, 2, 3)
            la_scalar(act)
            ln_scalar_std(act, 3, 2)
            ln_scalar_copy(act, 3, 0)
            ln_scalar_copy(act, 3, 1)
            ln_scalar_std(act, 3, 3)
            ln_scalar_copy(act, 3, 2)
            ln_scalar_copy(act, 3, 3)
            ffn_scalar_route(act, 1)
            ffn_scalar(act, 1)

        @block.tensor
        def _(pe):
            pe.wait_ge(ld_const, 16)
            def project(g):
                pe.wait_ge(xnt_ready, g + 1)
                if g >= 2:
                    pe.wait_ge(rest1, g - 1)
                xg = XNT[:, S * g:S * g + S]
                nc.tensor.matmul(PS[:, 2 + 2 * (g % 2), :], WQK[:, 0:D], xg, start=True, stop=True)
                nc.tensor.matmul(PS[:, 3 + 2 * (g % 2), :], WQK[:, D:2 * D], xg, start=True, stop=True).then_inc(qk_proj, 1)
                if g >= 2:
                    pe.wait_ge(v_copied, g - 1)
                for t in range(BT):
                    last = nc.tensor.matmul(PS[:, 6 + g % 2, P * t:P * t + P], XNT[:, S * g + P * t:S * g + P * t + P],
                                            WV[:, :], start=True, stop=True)
                last.then_inc(v_proj, 1)

            ln_tensor(pe, 0, 0)
            pe.wait_ge(wq_scaled, 1)
            for g in range(B):
                if g + 1 < B:
                    ln_tensor(pe, 0, g + 1)
                project(g)
            pe.wait_ge(consts_cast, 1)

            def max_bank(u, hg, k, index, first):
                a0, na, i = MBANKS[k]
                n = P * (i + 1)
                bank = (NM * hg + k) % 2
                if not (first and index < 2):
                    pe.wait_ge(max_used, index - 1)
                for a in range(a0, a0 + na):
                    seg = PS[:, bank, (a - a0) * n:(a - a0) * n + n]
                    nc.tensor.matmul(seg, QA[hg][0:KROWS, S * a + P * i:S * a + P * i + P],
                                     KA[hg][0:KROWS, S * a:S * a + n], start=(a == a0), stop=False,
                                     skip_group_check=True)
                diag = PS[:, bank, 0:na * n].rearrange("p (a n) -> p a n", a=na)[:, :, n - P:n]
                nc.tensor.matmul(diag, ident_b[:, :], mask_qk4[:, 0:na, :], start=False, stop=True,
                                 skip_group_check=True).then_inc(max_ready, 1)

            def transpose_max(u, par):
                pe.wait_ge(max_used, NM * (u + 1))
                if not isinstance(u, int) or u:
                    pe.wait_ge(negc_ready, u)
                if not isinstance(u, int) or u >= 2:
                    pe.wait_ge(normed, u - 1)
                nc.tensor.transpose(PS[0:GH * BT, 7, 0:P], cmax[par][:, :, :].rearrange("p a i -> p (a i)"),
                                    ident).then_inc(cmax_transposed, 1)

            def scores_t(u, hg, k):
                a0, na, per, kb = XGROUPS[k]
                n = S - P * kb
                pe.wait_ge(exp_done, NX * u + k + 1)
                for a in range(a0, a0 + na):
                    bank = 2 + 2 * (k % 2) + (a - a0) // per
                    c = (a - a0) % per * n
                    nc.tensor.matmul(PS[:, bank, c:c + n], KA[hg][0:MROWS, S * a + P * kb:S * a + P * kb + P],
                                     QA[hg][0:MROWS, S * a + P * kb:S * a + S], start=(c == 0), stop=False,
                                     skip_group_check=True)
                for bk in range(na // per):
                    bank = 2 + 2 * (k % 2) + bk
                    diag = PS[:, bank, 0:per * n].rearrange("p (a n) -> p a n", a=per)[:, :, 0:P]
                    last = nc.tensor.matmul(diag, ident_b[:, :], mask_kq[:, 0:per, :], start=False, stop=True,
                                            skip_group_check=True)
                last.then_inc(st_ready, 1)

            def values(u, par, kb):
                pe.wait_ge(exp_done, NX * u + GROUPS_OF_KB[kb] + 2)
                if kb == 0:
                    pe.wait_ge(vu_ready, u + 1)
                    pe.wait_ge(ot_ready, u + 1)
                for a in range(GH):
                    last = nc.tensor.matmul(PS[32 * a:32 * a + 32, 6, P * kb:S], VU[par][:, kb, a, :],
                                            PT[par][:, a, SEG[kb]:SEG[kb] + S - P * kb],
                                            start=(kb == 0), stop=(kb == BT - 1), skip_group_check=True)
                if kb == BT - 1:
                    last.then_inc(pv_done, 1)

            def transpose_out(u):
                pe.wait_ge(ot_ready, u + 2)
                for t in range(BT):
                    last = nc.tensor.transpose(PS[:, 7, P * t:P * t + P], OT[:, P * t:P * t + P], ident)
                last.then_inc(to_ready, 1)

            def step(u, batch, hg, lookahead=2, first=False):
                def maximum(*ks):
                    if lookahead == 2:
                        for k in ks:
                            max_bank(u + 2, (hg + 2) % HG, k, NM * (u + 2) + k, False)

                def previous(kb):
                    if not first:
                        values(u - 1, (hg + 1) % 2, kb)
                if lookahead == 2:
                    pe.wait_ge(qk_loaded[(hg + 2) % HG], 64 * (batch + (hg + 2) // HG + 1))
                maximum(0, 1)
                if lookahead >= 1:
                    transpose_max(u + 1, (hg + 1) % 2)
                pe.wait_ge(crows_loaded[hg % 2], 24 * (u - hg % 2) + 64)
                scores_t(u, hg, 0)
                maximum(2)
                scores_t(u, hg, 1)
                maximum(3)
                previous(0)
                maximum(4)
                scores_t(u, hg, 2)
                maximum(5)
                previous(1)
                maximum(6)
                scores_t(u, hg, 3)
                maximum(7)
                previous(2)
                previous(3)
                maximum(8)
                scores_t(u, hg, 4)
                maximum(9)
                scores_t(u, hg, 5)
                maximum(10)
                if not first:
                    if lookahead >= 1:
                        pe.wait_ge(negc_ready, u + 2)
                    else:
                        pe.wait_ge(normed, u)
                    transpose_out(u - 1)

            pe.wait_ge(bias_loaded, 6 * 16)
            pe.wait_ge(k_ones, HG)
            for i in range(2):
                pe.wait_ge(crows_loaded[i], 16)
            pe.wait_ge(exp_done, 2)
            for u in range(2):
                pe.wait_ge(qk_loaded[u], 64)
                for k in range(NM):
                    max_bank(u, u, k, NM * u + k, True)
                if u == 0:
                    pe.wait_ge(v_copied, B)
                    transpose_max(0, 0)
            step(0, 0, 0, first=True)
            with pe.Fori(0, B - 1) as b:
                for j in range(1, HG + 1):
                    step(b * HG + j, b + j // HG, j % HG)
            for u in range(U - 3, U):
                step(u, B - 1, u % HG, lookahead=min(2, U - 1 - u))
            for kb in range(BT):
                values(U - 1, 1, kb)
            pe.wait_ge(normed, U)
            transpose_out(U - 1)
            for f in range(2):
                ffn_tensor(pe, f)
                if f == 0:
                    la_tensor(pe)

        @block.vector
        def _(dve):
            count = [0]

            def link(ins):
                count[0] += 1
                ins.then_inc(dve_chain, 1)
                dve.wait_ge(dve_chain, count[0])
            nc.vector.memset(table_in[:, :], 0.0)
            nc.vector.memset(eps[:, :], EPS).then_inc(eps_ready, 1)
            def stats(g):
                dve.wait_ge(ld_x[g], 16)
                ln_stats(dve, link, 0, g)

            stats(0)
            stats(1)
            ln_scale(dve, link, 0, 0)
            stats(2)
            ln_scale(dve, link, 0, 1)
            stats(3)
            dve.wait_ge(ld_const, 16)
            nc.vector.memset(ones_b[:, :], 1.0).then_inc(exp_done, 2)
            nc.vector.tensor_copy(upper_b[:, :], upper1)
            nc.vector.tensor_copy(ident_b[:, :], ident).then_inc(pv_done, 2)
            for a in range(GH):
                nc.vector.tensor_scalar(mask_kq[:, a, :], causal1, -NEG, NEG, ALU.mult, ALU.add)
            for a in range(GH):
                nc.vector.tensor_scalar(mask_qk4[:, a, :], upper1, NEG, None,
                                        ALU.mult).then_inc((normed, ot_ready, to_ready, consts_cast)[a], 1)
            def rest(g):
                dve.wait_ge(part1, g + 1)
                nc.vector.tensor_tensor(QKR[g % 2], PS[:, 2 + 2 * (g % 2):4 + 2 * (g % 2), :], QKP[g][:, 0],
                                        ALU.subtract).then_inc(rest1, 1)

            def third_part(g):
                dve.wait_ge(part2, g + 1)
                nc.vector.tensor_tensor(QKP[g][:, 2], QKR[g % 2], QKP[g][:, 1], ALU.subtract).then_inc(part3, 1)

            rest(0)
            ln_scale(dve, link, 0, 2)
            third_part(0)
            ln_scale(dve, link, 0, 3)
            rest(1)
            third_part(1)
            rest(2)
            rest(3)

            def reduce(u, hg, k, index):
                a0, na, i = MBANKS[k]
                n = P * (i + 1)
                dve.wait_ge(max_ready, index + 1)
                nc.vector.reduce_max(cmax[hg % 2][:, a0:a0 + na, i],
                                     PS[:, (NM * hg + k) % 2, 0:na * n].rearrange("p (a n) -> p a n", a=na),
                                     AX.X).then_inc(max_used, 1)

            def negate(u, par):
                dve.wait_ge(cmax_transposed, u + 1)
                if not isinstance(u, int) or u:
                    dve.wait_ge(cparts_ready, u)
                nc.vector.tensor_scalar(negc[par][:, :], PS[0:GH * BT, 7, 0:P], -1.0, None,
                                        ALU.mult).then_inc(negc_ready, 1)

            def normalise(u, par):
                dve.wait_ge(to_ready, u + 2)
                o = PS[:, 7, :].rearrange("p (t a m) -> p t a m", t=BT, a=GH)
                nc.vector.reciprocal(rden[:, :, :], o[:, :, :, HD]).then_inc(rden_ready, 1)
                dve.wait_ge(rden_ready, u + 1)
                dve.wait_ge(x_added, u + 1)
                nc.vector.tensor_tensor(NRM[par][:, :, :, :].rearrange("p t a d -> p (t a) d"),
                                        PS[:, 7, :].rearrange("p (g m) -> p g m", m=32)[:, :, 0:HD],
                                        rden[:, :, :].rearrange("p t a -> p (t a)").unsqueeze(2)
                                        .to_broadcast([P, BT * GH, HD]), ALU.mult).then_inc(normed, 1)

            def step(u, hg, lookahead=2, first=False):
                for k in range(NM):
                    if lookahead == 2:
                        reduce(u + 2, (hg + 2) % HG, k, NM * (u + 2) + k)
                    if k == 1 and lookahead >= 1:
                        negate(u + 1, (hg + 1) % 2)
                if not first:
                    normalise(u - 1, (hg + 1) % 2)

            for u in range(2):
                for k in range(NM):
                    reduce(u, u, k, NM * u + k)
                if u == 0:
                    negate(0, 0)
            step(0, 0, first=True)
            with dve.Fori(0, B - 1) as b:
                for j in range(1, HG + 1):
                    step(b * HG + j, j % HG)
            step(U - 3, 1)
            step(U - 2, 2, lookahead=1)
            for g in range(B - 1):
                dve.wait_ge(x_added, 2 + HG * (g + 1))
                ln_stats(dve, link, 1, g)
            step(U - 1, 3, lookahead=0)
            ln_scale(dve, link, 1, 0)
            ln_scale(dve, link, 1, 1)
            normalise(U - 1, 1)
            ln_scale(dve, link, 1, 2)
            dve.wait_ge(x_added, 2 + U)
            ln_stats(dve, link, 1, B - 1)
            ln_scale(dve, link, 1, B - 1)
            route_vector(dve, link, 0)
            ffn_vector(dve, 0)
            for g in range(B):
                sum_outputs(dve, 0, g)
                ln_stats(dve, link, 2, g)
                if g:
                    ln_scale(dve, link, 2, g - 1)
            ln_scale(dve, link, 2, B - 1)
            la_vector(dve, link)
            route_vector(dve, link, 1)
            ffn_vector(dve, 1)
            for g in range(B):
                sum_outputs(dve, 1, g)


def kernel(**inputs):
    import numpy as np
    import concourse.bacc as bacc
    from concourse.bass_utils import run_bass_kernel_spmd

    f = {n: np.asarray(a) for n, a in inputs.items()}
    w = f["L0_attn_a_W_kqv"]
    by_place = [np.ascontiguousarray(w[:, i * D:(i + 1) * D].reshape(D, H, HD).transpose(0, 2, 1).reshape(D, D))
                for i in (1, 0)]
    p, c = np.arange(P)[:, None], np.arange(P)[None, :]
    row = lambda v: np.broadcast_to(np.asarray(v, np.float32), (P, len(v)))
    consts = np.concatenate([
        (p == c), (c > p), (c >= p), row(128 * np.arange(T)), row(E - np.arange(E)), row(np.arange(E)),
        row(np.arange(40)), p, 2 * T * P + p, row(np.tile(np.arange(T), 2)), row(np.arange(P)),
        row(P * np.tri(E, k=-1).ravel()), row(np.tri(E).ravel()), P + p,
        2 * T * P + p + P * (np.arange(N_SLOT_TILES)[None, :] % 2)],
        axis=1).astype(np.float32)
    t = np.arange(S)
    pos = np.broadcast_to(np.concatenate([t % 256, t - t % 256]).astype(np.float32), (H, 2 * S))
    arrays = {
        "x": f["L0_attn_a_x"], "wqk": np.concatenate(by_place, axis=1), "wv": w[:, 2 * D:],
        "slopes": f["L0_attn_a_m"].reshape(H, 1), "wq2": f["L0_attn_b_Wq"].T, "wk2": f["L0_attn_b_Wk"].T,
        "wv2": f["L0_attn_b_Wv"].T, "wo2": f["L0_attn_b_Wo"].T, "wr": f["L0_ffn_Wr"], "wg": f["L0_ffn_Wg"],
        "wu": f["L0_ffn_Wu"], "wd": f["L0_ffn_Wd"], "consts": consts, "pos_in": pos}
    arrays = {n: np.ascontiguousarray(a) for n, a in arrays.items()}
    nc = bacc.Bacc("TRN2", target_bir_lowering=False, num_devices=1)
    args = {n: nc.dram_tensor(n, a.shape, mybir.dt.from_np(a.dtype), kind="ExternalInput").ap()
            for n, a in arrays.items()}
    args["out"] = nc.dram_tensor("out", (B, S, D), mybir.dt.float32, kind="ExternalOutput").ap()
    build(nc, **args)
    r = run_bass_kernel_spmd(nc, [arrays], core_ids=[0])
    return r.results[0]["out"]
```
